# Optimizing a Trainium2 kernel written in Bass

```python
import numpy as np
import jax
import jax.numpy as jnp

def _softmax(x, axis=-1):
    return jax.nn.softmax(x, axis=axis)
def _gelu(x):
    return jax.nn.gelu(x, approximate=True)
def _silu(x):
    return jax.nn.silu(x)
def _sigmoid(x):
    return jax.nn.sigmoid(x)
def _layernorm(x, axis=-1, eps=1e-5):
    m = jnp.mean(x, axis=axis, keepdims=True)
    v = jnp.var(x, axis=axis, keepdims=True)
    return (x - m) / jnp.sqrt(v + eps)
def _scatter_add(tgt, idx, src, axis=0):
    return tgt.at[idx].add(src)
def _segment_sum(src, seg, n):
    return jax.ops.segment_sum(src, seg, n)

kernel_name = 'mk_conv_preact_d2_conv_nchw32_bfca55'

def setup_inputs(seed: int = 0):
    np.random.seed(seed)
    _w = jnp.asarray
    def _rec_inputs():
        import jax
        import jax.numpy as jnp
        _gk = jax.random.key(seed)
        x = -9.806e-05 + 1 * jax.random.normal(jax.random.fold_in(_gk, 1), (4, 32, 64, 64), jnp.float32)
        return x
    x = _rec_inputs()
    def _L0_conv_setup():
        import jax, jax.numpy as jnp
        import numpy as np
        B, C, H, W = (4, 32, 64, 64)
        K = 3
        HEADS = 8
        SF = 4
        D = C * K * K
        E = D // 2
        DH = E // HEADS
        SCALE = DH ** (-0.5)
        N = H * W

        def unfold(x):
            xp = jnp.pad(x, ((0, 0), (0, 0), (1, 1), (1, 1)))
            patches = jnp.stack([xp[:, :, i:i + H, j:j + W] for i in range(K) for j in range(K)], axis=2)
            return patches.reshape(x.shape[0], C * K * K, H * W)

        def fold(cols):
            b = cols.shape[0]
            y = cols.reshape(b, C, K, K, H, W)
            out = jnp.zeros((b, C, H + 2, W + 2), cols.dtype)
            for i in range(K):
                for j in range(K):
                    out = out.at[:, :, i:i + H, j:j + W].add(y[:, :, i, j])
            return out[:, :, 1:-1, 1:-1]

        def layernorm_cols(cols, g, b):
            xt = cols.transpose(0, 2, 1)
            mu = xt.mean(-1, keepdims=True)
            var = xt.var(-1, keepdims=True)
            y = (xt - mu) / jnp.sqrt(var + 1e-05) * g + b
            return y.transpose(0, 2, 1)

        def emha(x, wr, br, wqkv, we, be):
            b, _, n_tok = x.shape
            xr = jnp.einsum('bdn,ed->ben', x, wr) + br[None, :, None]
            t = xr.transpose(0, 2, 1)
            qkv = t @ wqkv.T
            q, k, v = jnp.split(qkv, 3, axis=-1)
            n = n_tok // SF

            def rs(a):
                return a.reshape(b, n_tok, HEADS, DH).transpose(0, 2, 1, 3).reshape(b, HEADS, SF, n, DH)
            q, k, v = (rs(q), rs(k), rs(v))
            attn = jax.nn.softmax(jnp.einsum('bhsnd,bhsmd->bhsnm', q, k) * SCALE, axis=-1)
            o = jnp.einsum('bhsnm,bhsmd->bhsnd', attn, v)
            o = o.reshape(b, HEADS, n_tok, DH).transpose(0, 2, 1, 3).reshape(b, n_tok, E).transpose(0, 2, 1)
            return jnp.einsum('ben,fe->bfn', o, we) + be[None, :, None]

        def conv3x3(x, w, b):
            y = jax.lax.conv_general_dilated(x, w, (1, 1), ((1, 1), (1, 1)), dimension_numbers=('NCHW', 'OIHW', 'NCHW'))
            return y + b[None, :, None, None]
        key = jax.random.key(seed)
        ks = jax.random.split(key, 20)
        s = 0.02
        inp = {'x': jax.random.normal(ks[0], (B, C, H, W), jnp.float32), 'ln_g': jnp.ones((D,), jnp.float32), 'ln_b': jnp.zeros((D,), jnp.float32), 'conv_w': jax.random.normal(ks[1], (C, C, 3, 3), jnp.float32) * s, 'conv_b': jnp.zeros((C,), jnp.float32)}
        for i in range(3):
            k0, k1, k2 = jax.random.split(ks[2 + i], 3)
            inp[f'wr{i + 1}'] = jax.random.normal(k0, (E, D), jnp.float32) * s
            inp[f'br{i + 1}'] = jnp.zeros((E,), jnp.float32)
            inp[f'wqkv{i + 1}'] = jax.random.normal(k1, (3 * E, E), jnp.float32) * s
            inp[f'we{i + 1}'] = jax.random.normal(k2, (D, E), jnp.float32) * s
            inp[f'be{i + 1}'] = jnp.zeros((D,), jnp.float32)
        return inp
    _L0_conv_all = _L0_conv_setup()
    _L0_conv_in = {k: v for k, v in _L0_conv_all.items() if k in ('ln_g', 'ln_b', 'conv_w', 'conv_b', 'wr1', 'br1', 'wqkv1', 'we1', 'be1', 'wr2', 'br2', 'wqkv2', 'we2', 'be2', 'wr3', 'br3', 'wqkv3', 'we3', 'be3', )}
    del _L0_conv_all

    def _L1_conv_setup():
        import jax, jax.numpy as jnp
        import numpy as np
        K = 3
        PAD = 1
        C_IN = 32
        C_OUT = 32
        CKK = C_IN * K * K
        HID = C_OUT

        def _unfold(x):
            B, C, H, W = x.shape
            xp = jnp.pad(x, ((0, 0), (0, 0), (PAD, PAD), (PAD, PAD)))
            patches = jnp.stack([xp[:, :, i:i + H, j:j + W] for i in range(K) for j in range(K)], axis=2)
            return patches.reshape(B, C * K * K, H * W)
        key = jax.random.key(seed)
        ks = jax.random.split(key, 6)
        B, H, W = (2, 64, 64)
        x = jax.random.normal(ks[0], (B, C_IN, H, W), dtype=jnp.float32)
        s1 = 1.0 / np.sqrt(CKK)
        s2 = 1.0 / np.sqrt(HID)
        W1 = jax.random.uniform(ks[1], (HID, CKK), jnp.float32, -s1, s1)
        b1 = jax.random.uniform(ks[2], (HID,), jnp.float32, -s1, s1)
        W2 = jax.random.uniform(ks[3], (C_OUT * CKK, HID), jnp.float32, -s2, s2)
        b2 = jax.random.uniform(ks[4], (C_OUT * CKK,), jnp.float32, -s2, s2)
        bias = jax.random.uniform(ks[5], (C_OUT,), jnp.float32, -s1, s1)
        return {'x': x, 'W1': W1, 'b1': b1, 'W2': W2, 'b2': b2, 'bias': bias}
    _L1_conv_all = _L1_conv_setup()
    _L1_conv_in = {k: v for k, v in _L1_conv_all.items() if k in ('W1', 'b1', 'W2', 'b2', 'bias', )}
    del _L1_conv_all

    return {
        "x": x,
        "L0_conv_ln_g": _L0_conv_in["ln_g"],
        "L0_conv_ln_b": _L0_conv_in["ln_b"],
        "L0_conv_conv_w": _L0_conv_in["conv_w"],
        "L0_conv_conv_b": _L0_conv_in["conv_b"],
        "L0_conv_wr1": _L0_conv_in["wr1"],
        "L0_conv_br1": _L0_conv_in["br1"],
        "L0_conv_wqkv1": _L0_conv_in["wqkv1"],
        "L0_conv_we1": _L0_conv_in["we1"],
        "L0_conv_be1": _L0_conv_in["be1"],
        "L0_conv_wr2": _L0_conv_in["wr2"],
        "L0_conv_br2": _L0_conv_in["br2"],
        "L0_conv_wqkv2": _L0_conv_in["wqkv2"],
        "L0_conv_we2": _L0_conv_in["we2"],
        "L0_conv_be2": _L0_conv_in["be2"],
        "L0_conv_wr3": _L0_conv_in["wr3"],
        "L0_conv_br3": _L0_conv_in["br3"],
        "L0_conv_wqkv3": _L0_conv_in["wqkv3"],
        "L0_conv_we3": _L0_conv_in["we3"],
        "L0_conv_be3": _L0_conv_in["be3"],
        "L1_conv_W1": _L1_conv_in["W1"],
        "L1_conv_b1": _L1_conv_in["b1"],
        "L1_conv_W2": _L1_conv_in["W2"],
        "L1_conv_b2": _L1_conv_in["b2"],
        "L1_conv_bias": _L1_conv_in["bias"],
    }

def reference(x, L0_conv_ln_g, L0_conv_ln_b, L0_conv_conv_w, L0_conv_conv_b, L0_conv_wr1, L0_conv_br1, L0_conv_wqkv1, L0_conv_we1, L0_conv_be1, L0_conv_wr2, L0_conv_br2, L0_conv_wqkv2, L0_conv_we2, L0_conv_be2, L0_conv_wr3, L0_conv_br3, L0_conv_wqkv3, L0_conv_we3, L0_conv_be3, L1_conv_W1, L1_conv_b1, L1_conv_W2, L1_conv_b2, L1_conv_bias):
    import jax
    import jax.numpy as jnp
    def _L0_conv_ref(x, ln_g, ln_b, conv_w, conv_b, wr1, br1, wqkv1, we1, be1, wr2, br2, wqkv2, we2, be2, wr3, br3, wqkv3, we3, be3):
        import jax, jax.numpy as jnp
        import numpy as np
        B, C, H, W = (4, 32, 64, 64)
        K = 3
        HEADS = 8
        SF = 4
        D = C * K * K
        E = D // 2
        DH = E // HEADS
        SCALE = DH ** (-0.5)
        N = H * W

        def unfold(x):
            xp = jnp.pad(x, ((0, 0), (0, 0), (1, 1), (1, 1)))
            patches = jnp.stack([xp[:, :, i:i + H, j:j + W] for i in range(K) for j in range(K)], axis=2)
            return patches.reshape(x.shape[0], C * K * K, H * W)

        def fold(cols):
            b = cols.shape[0]
            y = cols.reshape(b, C, K, K, H, W)
            out = jnp.zeros((b, C, H + 2, W + 2), cols.dtype)
            for i in range(K):
                for j in range(K):
                    out = out.at[:, :, i:i + H, j:j + W].add(y[:, :, i, j])
            return out[:, :, 1:-1, 1:-1]

        def layernorm_cols(cols, g, b):
            xt = cols.transpose(0, 2, 1)
            mu = xt.mean(-1, keepdims=True)
            var = xt.var(-1, keepdims=True)
            y = (xt - mu) / jnp.sqrt(var + 1e-05) * g + b
            return y.transpose(0, 2, 1)

        def emha(x, wr, br, wqkv, we, be):
            b, _, n_tok = x.shape
            xr = jnp.einsum('bdn,ed->ben', x, wr) + br[None, :, None]
            t = xr.transpose(0, 2, 1)
            qkv = t @ wqkv.T
            q, k, v = jnp.split(qkv, 3, axis=-1)
            n = n_tok // SF

            def rs(a):
                return a.reshape(b, n_tok, HEADS, DH).transpose(0, 2, 1, 3).reshape(b, HEADS, SF, n, DH)
            q, k, v = (rs(q), rs(k), rs(v))
            attn = jax.nn.softmax(jnp.einsum('bhsnd,bhsmd->bhsnm', q, k) * SCALE, axis=-1)
            o = jnp.einsum('bhsnm,bhsmd->bhsnd', attn, v)
            o = o.reshape(b, HEADS, n_tok, DH).transpose(0, 2, 1, 3).reshape(b, n_tok, E).transpose(0, 2, 1)
            return jnp.einsum('ben,fe->bfn', o, we) + be[None, :, None]

        def conv3x3(x, w, b):
            y = jax.lax.conv_general_dilated(x, w, (1, 1), ((1, 1), (1, 1)), dimension_numbers=('NCHW', 'OIHW', 'NCHW'))
            return y + b[None, :, None, None]
        t = x
        for wr, br, wqkv, we, be in ((wr1, br1, wqkv1, we1, be1), (wr2, br2, wqkv2, we2, be2), (wr3, br3, wqkv3, we3, be3)):
            cols = unfold(t)
            cols_n = layernorm_cols(cols, ln_g, ln_b)
            cols = emha(cols_n, wr, br, wqkv, we, be) + cols
            t = fold(cols)
        return x + jax.nn.elu(conv3x3(t, conv_w, conv_b))

    def _L1_conv_ref(x, W1, b1, W2, b2, bias):
        import jax, jax.numpy as jnp
        import numpy as np
        K = 3
        PAD = 1
        C_IN = 32
        C_OUT = 32
        CKK = C_IN * K * K
        HID = C_OUT

        def _unfold(x):
            B, C, H, W = x.shape
            xp = jnp.pad(x, ((0, 0), (0, 0), (PAD, PAD), (PAD, PAD)))
            patches = jnp.stack([xp[:, :, i:i + H, j:j + W] for i in range(K) for j in range(K)], axis=2)
            return patches.reshape(B, C * K * K, H * W)
        B, C, H, W = x.shape
        L = H * W
        u = _unfold(x)
        ut = u.transpose(0, 2, 1)
        h = jnp.tanh(jnp.einsum('blj,hj->blh', ut, W1) + b1)
        kern = jnp.einsum('blh,oh->blo', h, W2) + b2
        kern = kern.reshape(B, L, C_OUT, CKK)
        out = jnp.einsum('bloj,blj->bol', kern, ut)
        out = out.reshape(B, C_OUT, H, W) + bias[None, :, None, None]
        return out

    def _gn(v, G=16, eps=1e-5):
        B_, C_, H_, W_ = v.shape
        g = v.reshape(B_, G, C_ // G, H_, W_)
        m = jnp.mean(g, axis=(2, 3, 4), keepdims=True)
        s = jnp.var(g, axis=(2, 3, 4), keepdims=True)
        return ((g - m) / jnp.sqrt(s + eps)).reshape(v.shape)

    def _ln_c(v, eps=1e-6):
        m = jnp.mean(v, axis=1, keepdims=True)
        s = jnp.var(v, axis=1, keepdims=True)
        return (v - m) / jnp.sqrt(s + eps)

    def _ln_t(v, eps=1e-5):
        m = jnp.mean(v, axis=-1, keepdims=True)
        s = jnp.var(v, axis=-1, keepdims=True)
        return (v - m) / jnp.sqrt(s + eps)

    def _to_tokens(v):
        B_, C_, H_, W_ = v.shape
        return v.reshape(B_, C_, H_ * W_).transpose(0, 2, 1)
    def _from_tokens(t, like):
        B_, C_, H_, W_ = like.shape
        return t.transpose(0, 2, 1).reshape(B_, C_, H_, W_)

    x = x + _L0_conv_ref(_gn(x), L0_conv_ln_g, L0_conv_ln_b, L0_conv_conv_w, L0_conv_conv_b, L0_conv_wr1, L0_conv_br1, L0_conv_wqkv1, L0_conv_we1, L0_conv_be1, L0_conv_wr2, L0_conv_br2, L0_conv_wqkv2, L0_conv_we2, L0_conv_be2, L0_conv_wr3, L0_conv_br3, L0_conv_wqkv3, L0_conv_we3, L0_conv_be3)
    x = x + _L1_conv_ref(_gn(x), L1_conv_W1, L1_conv_b1, L1_conv_W2, L1_conv_b2, L1_conv_bias)
    return x


_drawn_inputs = setup_inputs


def setup_inputs(seed=0):
    import zlib

    import numpy as np

    out = dict(_drawn_inputs(seed))
    spreads = {'L0_conv_ln_g': (1.0, 0.6),
     'L0_conv_ln_b': (0.0, 0.8),
     'L0_conv_conv_b': (0.0, 2.0),
     'L0_conv_br1': (0.0, 0.8),
     'L0_conv_be1': (0.0, 1.401),
     'L0_conv_br2': (0.0, 0.8),
     'L0_conv_be2': (0.0, 2.0),
     'L0_conv_br3': (0.0, 2.0),
     'L0_conv_be3': (0.0, 2.0)}
    factors = {'L0_conv_wr1': 8.0,
     'L0_conv_wqkv1': 8.0,
     'L0_conv_we1': 8.0,
     'L0_conv_wr2': 8.0,
     'L0_conv_wqkv2': 8.0,
     'L0_conv_we2': 8.0,
     'L0_conv_wr3': 38.239,
     'L0_conv_wqkv3': 35.09,
     'L0_conv_we3': 35.716,
     'L1_conv_b1': 64.0,
     'L1_conv_b2': 32.439,
     'L1_conv_bias': 64.0,
     'L1_conv_W1': 8.0,
     'L1_conv_W2': 8.0}
    for name, (base, spread) in spreads.items():
        noise = np.random.default_rng([zlib.crc32(name.encode()), seed]).standard_normal(out[name].shape)
        drawn = base * np.exp(spread * noise) if base else spread * noise
        out[name] = jnp.asarray(drawn.astype(out[name].dtype))
    for name, factor in factors.items():
        out[name] = (out[name] * factor).astype(out[name].dtype)
    return out
```

```python
from contextlib import ExitStack

import numpy as np

import concourse.bass as bass
from concourse import mybir

ALU = mybir.AluOpType
ACT = mybir.ActivationFunctionType
F32 = mybir.dt.float32
BF16 = mybir.dt.bfloat16
AX_X = mybir.AxisListType.X

C = 32
IMG = 64
PAD = IMG + 2
N = IMG * IMG
TAPS = 3
D = C * TAPS * TAPS
E = D // 2
HEADS = 8
DH = E // HEADS
SPLIT = 4
SPAN = N // SPLIT
SCALE = DH ** -0.5
P = 128
BANK = 512
ROWS = BANK // IMG
CHUNKS = N // BANK
KT = SPAN // P
TQ = 3 * C
MT = 3 * E // 4
VA = 2 * DH
PROD = 6 * DH
PROW = PROD + 3
QB = SPAN // 4
EK = E // 2
LN_EPS = 1e-5
GN_EPS = 1e-5
NEG = -1.0


def constants():
    p = np.arange(P)
    group = (p % C) // 2
    gn_mean = (group[:, None] == group[None, :]).astype(np.float32) / (2 * N)
    den_pick = (p[:, None] == (p[None, :] // 32) * 32 + DH).astype(np.float32)
    quad_sum = (p[:, None] % 32 == np.arange(32)[None, :]).astype(np.float32)
    hid_sum = np.zeros((P, 8, 32), np.float32)
    for m in range(8):
        hid_sum[p, m, 4 * m + p // 32] = 1.0
    ident = np.eye(P, dtype=np.float32)
    y = np.full(IMG, 3.0, np.float32)
    y[0] = y[-1] = 2.0
    cover = (y[:, None] * y[None, :]).reshape(2, 4, 1, BANK)
    cover = np.broadcast_to(cover, (2, 4, 32, BANK)).transpose(1, 2, 0, 3).reshape(P, 2 * BANK)
    inside = np.zeros((1, 2, PAD, PAD), np.float32)
    inside[:, :, 1:-1, 1:-1] = 1.0
    return {
        "gn_mean": gn_mean, "den_pick": den_pick, "quad_sum": quad_sum,
        "hid_sum": hid_sum.reshape(P, 256), "ident": ident,
        "cover": np.ascontiguousarray(cover), "inside": inside.reshape(1, 2 * PAD * PAD),
    }


class Chain:

    def __init__(self, eng, sem, base):
        self.eng, self.sem, self.base, self.n = eng, sem, base, 0

    def link(self, ins):
        self.n += 1
        ins.then_inc(self.sem, 1)
        self.eng.wait_ge(self.sem, self.base + self.n)


def preact_block(nc, LAYERS, B, x, ln_g, ln_b, wr, br, wqkv, we, conv_w, conv_b,
                 w1, b1, w2, b2, bias, k, out):
    UNITS = LAYERS * B
    with ExitStack() as ctx:
        def sb(name, shape, dt=F32):
            return ctx.enter_context(nc.sbuf_tensor(name, shape, dt))

        def sem(name):
            return ctx.enter_context(nc.semaphore(name))

        t_img = nc.dram_tensor("t_img", (LAYERS + 1, B, C, N), F32, kind="Internal").ap()
        wc_all = nc.dram_tensor("wc_all", (LAYERS, TQ, 3 * 3 * E), F32, kind="Internal").ap()
        cq_all = nc.dram_tensor("cq_all", (LAYERS, MT, 4), F32, kind="Internal").ap()
        qkp = nc.dram_tensor("qkp", (3, 2 * E, N), BF16, kind="Internal").ap()
        o_pad = nc.dram_tensor("o_pad", (EK + 1, 2, PAD, PAD), F32, kind="Internal").ap()
        u_img = nc.dram_tensor("u_img", (B, C, N), F32, kind="Internal").ap()
        x1_img = nc.dram_tensor("x1_img", (B, C, N), F32, kind="Internal").ap()

        gn_mean = sb("gn_mean_s", [P, P])
        den_pick = sb("den_pick_s", [P, P])
        quad_sum = sb("quad_sum_s", [P, 32])
        hid_sum = sb("hid_sum_s", [P, 256])
        ident = sb("ident_s", [P, P])
        identb = sb("identb", [P, P], BF16)
        cover = sb("cover_s", [P, 2 * BANK])
        mean_w = sb("mean_w", [TQ, P])
        cw = sb("cw", [TQ, 3 * 32])
        cb = sb("cb", [P, 1])
        w1s = sb("w1s", [TQ, 3 * P])
        b1s = sb("b1s", [P, 1])
        w2s = sb("w2s", [TQ, 3 * 1024])
        b2s = sb("b2s", [TQ, 3 * 32])
        bias_s = sb("bias_s", [32, 1])
        wc = sb("wc", [TQ, 9 * E])
        cq = sb("cq", [MT, 4])
        wes = sb("wes", [EK + 1, 2 * 9 * 32])

        T3 = sb("T3", [TQ, PAD, IMG])
        shared = sb("shared", [P, PAD * IMG])
        SQ = shared[0:TQ, :].rearrange("p (y x) -> p y x", x=IMG)
        OP = sb("OP", [EK + 1, 2, PAD, PAD])
        imgA = sb("imgA", [P, 2 * BANK])
        imgB = sb("imgB", [P, 2 * BANK])
        imgC = sb("imgC", [P, 2 * BANK])
        col = sb("col", [P, 8])

        mu = sb("mu", [P, BANK])
        vpe = sb("vpe", [P, BANK])
        lnv = mu
        r0 = sb("r0", [P, BANK])
        na = sb("na", [P, BANK])
        nb = sb("nb", [P, BANK])
        rstd = sb("rstd", [P, BANK])
        qn = sb("qn", [MT, 4, BANK])
        resid = sb("resid", [MT, 3, BANK])
        parts = sb("parts", [MT, 3, 3, BANK], BF16)
        vrow = sb("vrow", [MT, 2, BANK])
        Vall = sb("Vall", [P, N // P, E])

        Q6 = sb("Q6", [PROW, 2, N], BF16)
        K6 = sb("K6", [PROW, 2, N], BF16)
        Vh = sb("Vh", [P, 2, KT, 32])
        Pt = shared[:, 0:4 * SPAN].rearrange("p (r n) -> p r n", r=4)
        mxs = sb("mxs", [P, 2, 2, 16])
        nm = sb("nm", [P, 16])
        cres = sb("cres", [P, 2, 16])
        cparts = sb("cparts", [P, 2, 8, 16], BF16)
        cT = sb("cT", [48, 2, P], BF16)
        Osb = sb("Osb", [P, 2, QB])
        rec = sb("rec", [P, 2, QB])
        On = sb("On", [P, 2, QB])

        score = ctx.enter_context(nc.psum_tensor("score", [P, 4, BANK], F32))
        two = ctx.enter_context(nc.psum_tensor("two", [P, 2, BANK], F32))
        wsum = ctx.enter_context(nc.psum_tensor("wsum", [P, BANK], F32))
        misc = ctx.enter_context(nc.psum_tensor("misc", [P, BANK], F32))

        consts_in = sem("consts_in")
        setup_dve = sem("setup_dve")
        wload = sem("wload")
        wprep = sem("wprep")
        wprep_pe = sem("wprep_pe")
        wprep_out = sem("wprep_out")
        wprep_st = sem("wprep_st")
        gn_in = sem("gn_in")
        gn_step = sem("gn_step")
        gn_pe = sem("gn_pe")
        gn_act = sem("gn_act")
        gn_rec = sem("gn_rec")
        gn_stored = sem("gn_stored")
        t3_in = sem("t3_in")
        sq_ready = sem("sq_ready")
        stat_ready = sem("stat_ready")
        var_ready = sem("var_ready")
        r0_ready = sem("r0_ready")
        act_pre = sem("act_pre")
        pre_step = sem("pre_step")
        qkv_ready = sem("qkv_ready")
        qn_ready = sem("qn_ready")
        act_split = sem("act_split")
        r_ready = sem("r_ready")
        m_done = sem("m_done")
        l_done = sem("l_done")
        part_stored = [sem(f"part_stored{i}") for i in range(3)]
        vt_ready = sem("vt_ready")
        vt_used = sem("vt_used")
        qk_in = [[sem(f"qk_in{par}_{s}") for s in range(SPLIT)] for par in range(2)]
        p1_ready = sem("p1_ready")
        max_done = sem("max_done")
        c_step = sem("c_step")
        tr_ready = sem("tr_ready")
        ct_ready = sem("ct_ready")
        c_stored = [sem(f"c_stored{i}") for i in range(2)]
        p2_ready = sem("p2_ready")
        exp_done = sem("exp_done")
        pv_done = sem("pv_done")
        vh_ready = sem("vh_ready")
        o_evac = sem("o_evac")
        nrm_ready = sem("nrm_ready")
        rec_done = sem("rec_done")
        on_done = sem("on_done")
        on_stored = [sem(f"on_stored{i}") for i in range(2)]
        op_in = sem("op_in")
        post_in = sem("post_in")
        post_cov = sem("post_cov")
        fold_ready = sem("fold_ready")
        new_ready = sem("new_ready")
        post_stored = sem("post_stored")
        tail_in = sem("tail_in")
        tail_pe = sem("tail_pe")
        tail_step = sem("tail_step")
        tail_act = sem("tail_act")
        tail_u = sem("tail_u")
        h_ready = sem("h_ready")
        h_act = sem("h_act")
        g_ready = sem("g_ready")
        y_done = sem("y_done")
        z_ready = sem("z_ready")
        z_sb = sem("z_sb")
        f_ready = sem("f_ready")
        x1_in = sem("x1_in")
        o_done = sem("o_done")
        out_stored = sem("out_stored")

        QN_FREE, SPLIT_FREE, L_FREE = 4, 5, 3
        MAX_FREE, EXP_FREE, PV_FREE, ON_FREE = 2, 2, 12, 2
        P2_FREE = 2 * SPLIT * KT
        SETUP = 8

        def quad(ap):
            return [ap.rearrange("c (g j n) -> j c g n", g=2, j=4)[j] for j in range(4)]

        def quad_dma(eng, tile, ap, s, load):
            for j, piece in enumerate(quad(ap)):
                side = tile[32 * j:32 * j + 32, :].rearrange("p (g n) -> p g n", g=2)
                if load:
                    eng.dma_start(side, piece).then_inc(s, 16)
                else:
                    eng.dma_start(piece, side).then_inc(s, 16)

        def t3_dma(eng, ap, s):
            v = ap.rearrange("c (y x) -> c y x", y=IMG)
            eng.dma_start(T3[0:C, 1:IMG + 1, 1:IMG], v[:, :, 0:IMG - 1]).then_inc(s, 16)
            eng.dma_start(T3[C:2 * C, 1:IMG + 1, :], v[:, :, :]).then_inc(s, 16)
            eng.dma_start(T3[2 * C:TQ, 1:IMG + 1, 0:IMG - 1], v[:, :, 1:IMG]).then_inc(s, 16)

        def taps(c, i):
            return T3[:, :, :].rearrange("p y x -> p (y x)")[:, bass.ds((c * ROWS + i) * IMG, BANK)]

        def sq_taps(c, i):
            return SQ[:, :, :].rearrange("p y x -> p (y x)")[:, bass.ds((c * ROWS + i) * IMG, BANK)]

        def qy(m):
            return Pt[:, m % 4, 0:BANK]
        zsb = Pt[:, 0, BANK:2 * BANK]
        hrep = Pt[:, 1, BANK:2 * BANK]

        CONST_DMAS = 16

        block = ctx.enter_context(nc.Block())

        @block.sync
        def _(sp):
            for dst, src in ((gn_mean, k["gn_mean"]), (den_pick, k["den_pick"]), (quad_sum, k["quad_sum"]),
                             (hid_sum, k["hid_sum"]), (ident, k["ident"]), (cover, k["cover"]),
                             (cw, conv_w), (cb, conv_b), (w1s, w1), (b1s, b1), (w2s, w2), (b2s, b2),
                             (bias_s, bias)):
                sp.dma_start(dst[:, :], src).then_inc(consts_in, 16)
            sp.dma_start(OP[EK:EK + 1, :, :, :].rearrange("p a y x -> p (a y x)"), k["inside"]).then_inc(consts_in, 16)
            sp.dma_start(imgA[0:EK, 0:D], ln_g.to_broadcast([EK, D])).then_inc(consts_in, 16)
            sp.dma_start(imgA[0:EK, BANK:BANK + D], ln_b.to_broadcast([EK, D])).then_inc(consts_in, 16)
            sp.wait_ge(setup_dve, SETUP)
            sp.nop(nofuse=True)
            sp.dma_start(o_pad, OP[:, :, :, :]).then_inc(op_in, 16)
            sp.wait_ge(op_in, 16)
            sp.nop(nofuse=True)

            for L in range(LAYERS):
                if L:
                    sp.wait_ge(wprep_pe, 4 * L)
                    sp.nop(nofuse=True)
                sp.dma_start(imgB[0:EK, 0:2 * D].rearrange("p (a j) -> p a j", a=2), wr[L]).then_inc(wload, 16)
                sp.dma_start(SQ[0:EK, 0:14, :].rearrange("p y x -> p (y x)")[:, 0:6 * E]
                             .rearrange("p (a m) -> p a m", a=2), wqkv[L]).then_inc(wload, 16)
                sp.dma_start(col[0:EK, 0:2], br[L]).then_inc(wload, 16)
                sp.wait_ge(wprep_out, 4 * (L + 1))
                sp.nop(nofuse=True)
                sp.dma_start(wc_all[L], wc[:, :]).then_inc(wprep_st, 16)
                sp.dma_start(cq_all[L], cq[:, :]).then_inc(wprep_st, 16)
                sp.wait_ge(wprep_st, 32 * (L + 1))
                sp.nop(nofuse=True)

            with sp.Fori(0, B) as b:
                quad_dma(sp, imgA, x[b], gn_in, True)
                sp.wait_ge(gn_step, 6 * b + 6)
                sp.nop(nofuse=True)
                quad_dma(sp, imgC, t_img[0, b], gn_stored, False)
                sp.wait_ge(gn_stored, 64 * b + 64)
                sp.nop(nofuse=True)

            with sp.Fori(0, LAYERS) as L:
                with sp.Fori(0, B) as b:
                    u = L * B + b
                    t3_dma(sp, t_img[L, b], t3_in)
                    sp.dma_start(wc[:, :], wc_all[L]).then_inc(t3_in, 16)
                    sp.dma_start(cq[:, :], cq_all[L]).then_inc(t3_in, 16)
                    sp.dma_start(wes[:, :], we[L]).then_inc(t3_in, 16)
                    with sp.Fori(0, CHUNKS) as c:
                        g = u * CHUNKS + c
                        for t in range(3):
                            lo = VA if t == 2 else 0
                            row = MT * t
                            sp.wait_ge(l_done, 3 * g + t + 1 + L_FREE)
                            sp.nop(nofuse=True)
                            sp.dma_start(
                                qkp[:, row:row + MT - lo, bass.ds(c * BANK, BANK)].rearrange("a r n -> r a n"),
                                parts[lo:MT, t, :, :]).then_inc(part_stored[t], 16)
                    for t in range(3):
                        sp.wait_ge(part_stored[t], 16 * CHUNKS * (u + 1))
                        sp.nop(nofuse=True)

                    def load_qk(n, h, par, s):
                        sp.wait_ge(p2_ready, 32 * n + 8 * s + 8)
                        sp.nop(nofuse=True)
                        tok = slice(s * SPAN, (s + 1) * SPAN)
                        q = qkp[:, bass.ds(h * DH, DH), tok]
                        kk = qkp[:, bass.ds(h * DH + E, DH), tok]
                        for i in range(3):
                            sp.dma_start(Q6[DH * i:DH * i + DH, par, tok], q[0]).then_inc(qk_in[par][s], 16)
                        for i in range(2):
                            sp.dma_start(Q6[DH * (3 + i):DH * (4 + i), par, tok], q[1]).then_inc(qk_in[par][s], 16)
                        sp.dma_start(Q6[5 * DH:6 * DH, par, tok], q[2]).then_inc(qk_in[par][s], 16)
                        sp.dma_start(K6[0:3 * DH, par, tok], kk[0:3]).then_inc(qk_in[par][s], 16)
                        sp.dma_start(K6[3 * DH:5 * DH, par, tok], kk[0:2]).then_inc(qk_in[par][s], 16)
                        sp.dma_start(K6[5 * DH:6 * DH, par, tok], kk[0]).then_inc(qk_in[par][s], 16)

                    def store_c(n, par, sp_):
                        sp.wait_ge(ct_ready, 2 * n + sp_ + 1)
                        sp.nop(nofuse=True)
                        for a in range(3):
                            sp.dma_start(
                                Q6[PROD + a:PROD + a + 1, par, sp_ * 2 * SPAN:(sp_ + 1) * 2 * SPAN]
                                .rearrange("o (k n) -> o k n", k=16),
                                cT[16 * a:16 * a + 16, sp_, :]).then_inc(c_stored[sp_], 16)

                    def store_o(n, h2, par, s):
                        w = 4 * n + s
                        sp.wait_ge(on_done, w + 1 + ON_FREE)
                        sp.nop(nofuse=True)
                        for j in range(4):
                            y = 1 + (s * SPAN + j * QB) // IMG
                            sp.dma_start(
                                o_pad[bass.ds(h2 * DH, DH), par, y:y + QB // IMG, 1:IMG + 1],
                                On[32 * j:32 * j + DH, s % 2, :].rearrange("p (y x) -> p y x", x=IMG)
                            ).then_inc(on_stored[s % 2], 16)

                    n0 = u * HEADS
                    for s in range(SPLIT):
                        load_qk(n0, 0, 0, s)
                    for s in range(SPLIT):
                        load_qk(n0 + 1, 1, 1, s)
                    store_c(n0, 0, 0)
                    store_c(n0, 0, 1)

                    def step(kh, h2, par, nxt, nxt2):
                        n = n0 + kh
                        for s in range(SPLIT):
                            if nxt2:
                                load_qk(n + 2, kh + 2, par, s)
                            if s >= 1:
                                store_o(n, h2, par, s - 1)
                            if nxt and s == 2:
                                store_c(n + 1, 1 - par, 0)
                        if nxt:
                            store_c(n + 1, 1 - par, 1)
                        store_o(n, h2, par, SPLIT - 1)

                    step(0, 0, 0, True, True)
                    with sp.Fori(0, HEADS // 2 - 2) as p:
                        step(2 * p + 1, p, 1, True, True)
                        step(2 * p + 2, p + 1, 0, True, True)
                    step(HEADS - 3, (HEADS - 3) // 2, 1, True, True)
                    step(HEADS - 2, (HEADS - 2) // 2, 0, True, False)
                    step(HEADS - 1, (HEADS - 1) // 2, 1, False, False)
                    for i in range(2):
                        sp.wait_ge(on_stored[i], 64 * 2 * HEADS * (u + 1))
                        sp.nop(nofuse=True)

                    sp.dma_start(OP[:, :, :, :], o_pad).then_inc(op_in, 16)
                    quad_dma(sp, imgA, t_img[L, b], post_in, True)
                    sp.wait_ge(new_ready, u + 1)
                    sp.nop(nofuse=True)
                    quad_dma(sp, imgC, t_img[L + 1, b], post_stored, False)
                    sp.wait_ge(post_stored, 64 * (u + 1))
                    sp.nop(nofuse=True)

            with sp.Fori(0, B) as b:
                t3_dma(sp, t_img[LAYERS, b], tail_in)
                quad_dma(sp, imgA, t_img[0, b], tail_in, True)
                quad_dma(sp, imgB, x[b], tail_in, True)
                sp.wait_ge(tail_step, 12 * b + 6)
                sp.nop(nofuse=True)
                quad_dma(sp, imgB, x1_img[b], tail_u, False)
                sp.wait_ge(tail_step, 12 * b + 12)
                sp.nop(nofuse=True)
                quad_dma(sp, imgC, u_img[b], tail_u, False)
                sp.wait_ge(tail_u, 176 * b + 128)
                sp.nop(nofuse=True)
                t3_dma(sp, u_img[b], tail_u)
                with sp.Fori(0, CHUNKS) as c:
                    g = b * CHUNKS + c
                    tok = bass.ds(c * BANK, BANK)
                    sp.dma_start(imgA[0:32, 0:BANK], x1_img[b][:, tok]).then_inc(x1_in, 16)
                    sp.wait_ge(o_done, g + 1)
                    sp.nop(nofuse=True)
                    sp.dma_start(out[b][:, tok], imgA[0:32, BANK:2 * BANK]).then_inc(out_stored, 16)
                    sp.wait_ge(out_stored, 16 * (g + 1))
                    sp.nop(nofuse=True)

        @block.tensor
        def _(pe):
            mm = pe.matmul
            pe.wait_ge(consts_in, 16 * CONST_DMAS)
            pe.wait_ge(setup_dve, SETUP)
            wq_v = SQ[0:EK, 0:14, :].rearrange("p y x -> p (y x)")[:, 0:6 * E].rearrange("p (a m) -> p a m", a=2)
            wr_v = imgB[0:EK, 0:2 * D].rearrange("p (a j) -> p a j", a=2)
            for L in range(LAYERS):
                pe.wait_ge(wprep, 14 * (L + 1))
                for i in range(3):
                    pe.wait_ge(wprep_out, 4 * L + i // 2)
                    for a in range(2):
                        last = mm(two[0:TQ, i % 2, 0:3 * E], wr_v[:, a, i * TQ:(i + 1) * TQ], wq_v[:, a, :],
                                  start=(a == 0), stop=(a == 1))
                    last.then_inc(wprep_pe, 1)
                for t in range(4):
                    for a in range(2):
                        last = mm(misc[0:MT, t:t + 1], wq_v[:, a, t * MT:(t + 1) * MT], col[0:EK, 4 + a:5 + a],
                                  start=(a == 0), stop=(a == 1), skip_group_check=True)
                last.then_inc(wprep_pe, 1)

            with pe.Fori(0, B) as b:
                for i in range(2):
                    pe.wait_ge(gn_step, 6 * b + (1 if i == 0 else 4))
                    mm(misc[:, i:i + 1], gn_mean[:, :], col[:, i:i + 1], start=True, stop=True).then_inc(gn_pe, 1)

            def p1(n, par, s, q):
                tile = slice(s * SPAN + q * P, s * SPAN + (q + 1) * P)
                for i in range(2):
                    pe.wait_ge(max_done, 64 * n + 2 * (8 * s + q) + i + 1)
                    mm(two[:, i, :], Q6[0:PROD, par, tile],
                       K6[0:PROD, par, s * SPAN + i * BANK:s * SPAN + (i + 1) * BANK],
                       start=True, stop=True).then_inc(p1_ready, 1)

            def p2(n, par, s, kt):
                m2 = 32 * n + 8 * s + kt
                pe.wait_ge(exp_done, m2 + 1)
                tile = slice(s * SPAN + kt * P, s * SPAN + (kt + 1) * P)
                for i in range(2):
                    last = mm(score[:, 2 * (kt % 2) + i, :], K6[:, par, tile],
                              Q6[:, par, s * SPAN + i * BANK:s * SPAN + (i + 1) * BANK], start=True, stop=True)
                last.then_inc(p2_ready, 1)

            def pv(n, s, kts):
                w = 4 * n + s
                for kt in kts:
                    if kt == 0:
                        pe.wait_ge(vh_ready, w + 1)
                        pe.wait_ge(o_evac, w)
                    pe.wait_ge(exp_done, 32 * n + 8 * s + kt + 1 + EXP_FREE)
                    for j in range(4):
                        last = mm(wsum[32 * j:32 * j + 32, 0:QB], Vh[:, s % 2, kt, :],
                                  Pt[:, kt % 4, j * QB:(j + 1) * QB], start=(kt == 0), stop=(kt == KT - 1))
                    last.then_inc(pv_done, 1)

            def norm(n, s, n_ct):
                w = 4 * n + s
                pe.wait_ge(o_evac, w + 1)
                pe.wait_ge(rec_done, w)
                pe.wait_ge(ct_ready, n_ct)
                mm(misc[:, 0:QB], den_pick[:, :], Osb[:, s % 2, :], start=True, stop=True).then_inc(nrm_ready, 1)

            def turn(n, sp_, n_rec):
                pe.wait_ge(c_step, 5 * (2 * n + sp_ + 1))
                pe.wait_ge(ct_ready, 2 * n + sp_)
                pe.wait_ge(rec_done, n_rec)
                pe.transpose(misc[:, 0:P // 2].bitcast(BF16), cparts[:, sp_, :, :].rearrange("p a k -> p (a k)"),
                             identb[:, :]).then_inc(tr_ready, 1)

            def step(kh, par, n0, h2, first=False, nxt=True):
                n = n0 + kh
                for s in range(SPLIT):
                    if s % 2 == 0:
                        pe.wait_ge(c_stored[s // 2], 48 * (n + 1))
                    if nxt:
                        pe.wait_ge(qk_in[1 - par][s], 144 * (h2 + 1))
                    for i in range(KT):
                        if nxt:
                            p1(n + 1, 1 - par, s, i)
                        p2(n, par, s, i)
                        if i == 1 and not (first and s == 0):
                            pv(n - (s == 0), (s - 1) % SPLIT, (KT - 2, KT - 1))
                        if i % 2 and i > 1:
                            pv(n, s, (i - 3, i - 2))
                        if i == 5 and not (first and s == 0):
                            norm(n - (s == 0), (s - 1) % SPLIT, 2 * (n + 1) + (1 if nxt and s >= 2 else 0))
                        if i == 3 and nxt and s == 2:
                            turn(n + 1, 0, 4 * n + 1)
                if nxt:
                    turn(n + 1, 1, 4 * n + 3)

            def flush(n):
                pv(n, SPLIT - 1, (KT - 2, KT - 1))
                norm(n, SPLIT - 1, 2 * (n + 1))

            with pe.Fori(0, LAYERS) as L:
                with pe.Fori(0, B) as b:
                    u = L * B + b
                    pe.wait_ge(t3_in, 96 * (u + 1))
                    pe.nop(nofuse=True)
                    with pe.Fori(0, CHUNKS) as c:
                        g = u * CHUNKS + c
                        pe.wait_ge(var_ready, g)
                        for i in range(3):
                            mm(two[:, 0, :], mean_w[:, :], taps(c, i), start=(i == 0), stop=(i == 2))
                        pe.wait_ge(sq_ready, u + 1)
                        for i in range(3):
                            last = mm(two[:, 1, :], mean_w[:, :], sq_taps(c, i), start=(i == 0), stop=(i == 2))
                        last.then_inc(stat_ready, 1)
                        for t in range(4):
                            pe.wait_ge(qn_ready, 4 * g + t + 1)
                            for i in range(3):
                                last = mm(score[0:MT, t, :], wc[:, i * 3 * E + t * MT:i * 3 * E + (t + 1) * MT],
                                          taps(c, i), start=(i == 0), stop=(i == 2))
                            last.then_inc(qkv_ready, 1)
                        pe.wait_ge(act_split, 5 * g + 5 + SPLIT_FREE)
                        pe.wait_ge(vt_used, g)
                        for a in range(4):
                            bank = wsum if a < 2 else misc
                            o = (a % 2) * E
                            pe.transpose(bank[:, o + VA:o + E], vrow[:, 1, a * P:(a + 1) * P], ident[0:MT, 0:MT])
                            last = pe.transpose(bank[:, o:o + VA], vrow[0:VA, 0, a * P:(a + 1) * P],
                                                ident[0:VA, 0:VA])
                        last.then_inc(vt_ready, 1)

                    pe.wait_ge(vt_used, (u + 1) * CHUNKS)
                    pe.nop(nofuse=True)
                    n0, h0 = u * HEADS, u * (HEADS // 2)
                    for s in range(SPLIT):
                        pe.wait_ge(qk_in[0][s], 144 * (h0 + 1))
                        for i in range(KT):
                            p1(n0, 0, s, i)
                        if s % 2:
                            turn(n0, s // 2, 4 * n0)
                    step(0, 0, n0, h0, first=True)
                    with pe.Fori(0, HEADS // 2 - 1) as p:
                        step(2 * p + 1, 1, n0, h0 + p + 1)
                        step(2 * p + 2, 0, n0, h0 + p + 1)
                    step(HEADS - 1, 1, n0, h0, nxt=False)
                    flush(n0 + HEADS - 1)

                    pe.wait_ge(op_in, 16 * (u + 2))
                    for gh in range(2):
                        for a in range(2):
                            for i in range(TAPS):
                                for jj in range(TAPS):
                                    f = (a * 9 + i * 3 + jj) * 32
                                    for j in range(4):
                                        y = (4 * gh + j) * ROWS + 2 - i
                                        last = mm(two[32 * j:32 * j + 32, gh, :], wes[:, f:f + 32],
                                                  OP[:, a, y:y + ROWS, 2 - jj:2 - jj + IMG],
                                                  start=(a == 0 and i == 0 and jj == 0),
                                                  stop=(a == 1 and i == 2 and jj == 2))
                        last.then_inc(fold_ready, 1)

            with pe.Fori(0, B) as b:
                pe.wait_ge(tail_in, 176 * (b + 1))
                for gh in range(2):
                    for i in range(TAPS):
                        for j in range(4):
                            y = (4 * gh + j) * ROWS + i
                            last = mm(two[32 * j:32 * j + 32, gh, :], cw[:, i * 32:(i + 1) * 32],
                                      T3[:, y:y + ROWS, :], start=(i == 0), stop=(i == 2))
                last.then_inc(tail_pe, 1)
                for i in range(2):
                    pe.wait_ge(tail_step, 12 * b + (7 if i == 0 else 10))
                    mm(misc[:, i:i + 1], gn_mean[:, :], col[:, i:i + 1], start=True, stop=True).then_inc(tail_pe, 1)
                pe.wait_ge(tail_u, 176 * (b + 1))
                pe.nop(nofuse=True)
                with pe.Fori(0, CHUNKS) as c:
                    g = b * CHUNKS + c
                    pe.wait_ge(h_act, g)
                    for i in range(3):
                        last = mm(two[:, 0, :], w1s[:, i * P:(i + 1) * P], taps(c, i), start=(i == 0), stop=(i == 2))
                    last.then_inc(h_ready, 1)

                    def reduce_y(m):
                        pe.wait_ge(y_done, 8 * g + m + 1 + 4)
                        j = m % 4
                        return mm(wsum[32 * j:32 * j + 32, :], hid_sum[:, 32 * m:32 * m + 32], qy(m),
                                  start=(m < 4), stop=(m >= 4))

                    for m in range(8):
                        pe.wait_ge(y_done, 8 * g + m + 1)
                        for i in range(3):
                            last = mm(score[:, m % 4, :], w2s[:, i * 1024 + m * P:i * 1024 + (m + 1) * P],
                                      taps(c, i), start=(i == 0), stop=(i == 2))
                        last.then_inc(g_ready, 1)
                        if m == 0:
                            pe.wait_ge(z_sb, g)
                        if m >= 1:
                            reduce_y(m - 1)
                    pe.wait_ge(o_done, g)
                    reduce_y(7).then_inc(z_ready, 1)
                    for i in range(3):
                        mm(misc[0:32, :], b2s[:, i * 32:(i + 1) * 32], taps(c, i), start=(i == 0), stop=False)
                    pe.wait_ge(z_sb, g + 1)
                    mm(misc[0:32, :], quad_sum[:, :], zsb, start=False, stop=True).then_inc(f_ready, 1)

        @block.scalar
        def _(act):
            with act.Fori(0, B) as b:
                act.wait_ge(gn_step, 6 * b + 5)
                act.activation(col[:, 3:4], col[:, 2:3], ACT.Sqrt).then_inc(gn_act, 1)
            with act.Fori(0, LAYERS) as L:
                with act.Fori(0, B) as b:
                    u = L * B + b
                    act.wait_ge(t3_in, 96 * (u + 1))
                    act.activation(SQ[:, :, :], T3[:, :, :], ACT.Square).then_inc(sq_ready, 1)
                    with act.Fori(0, CHUNKS) as c:
                        g = u * CHUNKS + c
                        act.wait_ge(var_ready, g + 1)
                        act.activation(lnv[:, :], vpe[:, :], ACT.Ln).then_inc(act_pre, 1)
                        act.wait_ge(act_pre, g + 1)
                        act.activation(r0[:, :], lnv[:, :], ACT.Exp, scale=-0.5).then_inc(r0_ready, 1)
                        for t in range(4):
                            act.wait_ge(qn_ready, 4 * g + t + 1 + QN_FREE)
                            if t < 3:
                                act.wait_ge(part_stored[t], 16 * g)
                                act.activation(parts[:, t, 0, :], qn[:, t, :], ACT.Identity,
                                               bias=cq[:, t:t + 1]).then_inc(act_split, 1)
                            if t >= 2:
                                act.wait_ge(vt_ready, g)
                                rows = VA if t == 2 else MT
                                act.activation(vrow[0:rows, t - 2, :], qn[0:rows, t, :], ACT.Identity,
                                               bias=cq[0:rows, t:t + 1]).then_inc(act_split, 1)
                        act.wait_ge(vt_ready, g + 1)
                        for a in range(2):
                            bank = wsum if a == 0 else misc
                            last = act.activation(
                                Vall[:, bass.ds(c * 4 + 2 * a, 2), :].rearrange("p k e -> p (k e)"),
                                bank[:, 0:2 * E], ACT.Copy)
                        last.then_inc(vt_used, 1)

                    def exps(n, s):
                        for kt in range(KT):
                            m2 = 32 * n + 8 * s + kt
                            act.wait_ge(p2_ready, m2 + 1 + P2_FREE)
                            act.wait_ge(pv_done, m2 + 1 + PV_FREE - 4)
                            act.activation(Pt[:, kt % 4, :],
                                           score[:, 2 * (kt % 2):2 * (kt % 2) + 2, :].rearrange("p a n -> p (a n)"),
                                           ACT.Exp, scale=SCALE).then_inc(exp_done, 1)

                    with act.Fori(0, HEADS) as h:
                        for s in range(SPLIT):
                            exps(u * HEADS + h, s)
            with act.Fori(0, B) as b:
                act.wait_ge(tail_step, 12 * b + 2)
                act.activation(imgC[:, :], imgC[:, :], ACT.Exp).then_inc(tail_act, 1)
                act.wait_ge(tail_step, 12 * b + 11)
                act.activation(col[:, 3:4], col[:, 2:3], ACT.Sqrt).then_inc(tail_act, 1)
                with act.Fori(0, CHUNKS) as c:
                    g = b * CHUNKS + c
                    act.wait_ge(h_ready, g + 1)
                    act.wait_ge(y_done, 8 * g + 4)
                    act.activation(hrep, two[:, 0, :], ACT.Tanh, bias=b1s[:, 0:1]).then_inc(h_act, 1)

        @block.vector
        def _(dve):
            dve.memset(K6[96:PROW, :, :], 1.0).then_inc(setup_dve, 1)
            dve.memset(T3[:, :, :], 0.0).then_inc(setup_dve, 1)
            dve.memset(mean_w[:, :], 1.0 / D).then_inc(setup_dve, 1)
            dve.memset(OP[0:EK, :, :, :], 0.0).then_inc(setup_dve, 1)
            dve.memset(Vh[:, :, :, :], 0.0).then_inc(setup_dve, 1)
            dve.memset(cparts[:, :, :, :], 0.0).then_inc(setup_dve, 1)
            dve.wait_ge(setup_dve, 6)
            dve.memset(Vh[:, :, :, DH:DH + 1], 1.0).then_inc(setup_dve, 1)
            dve.wait_ge(consts_in, 16 * CONST_DMAS)
            dve.tensor_copy(identb[:, :], ident[:, :]).then_inc(setup_dve, 1)
            for s, v in ((qn_ready, QN_FREE), (act_split, SPLIT_FREE), (l_done, L_FREE), (max_done, MAX_FREE),
                         (exp_done, EXP_FREE), (pv_done, PV_FREE), (on_done, ON_FREE), (y_done, 4),
                         (p2_ready, P2_FREE)):
                dve.sem_inc(s, v)
            wr_v = imgB[0:EK, 0:2 * D].rearrange("p (a j) -> p a j", a=2)
            gain, shift = imgA[0:EK, 0:D], imgA[0:EK, BANK:BANK + D]
            for L in range(LAYERS):
                ch = Chain(dve, wprep, 14 * L)
                dve.wait_ge(wload, 48 * (L + 1))
                if L:
                    dve.wait_ge(wprep_pe, 4 * L)
                for a in range(2):
                    ch.link(dve.tensor_tensor(imgC[0:EK, 0:D], wr_v[:, a, :], shift, ALU.mult))
                    ch.link(dve.tensor_reduce(col[0:EK, 2:3], imgC[0:EK, 0:D], AX_X, ALU.add))
                    ch.link(dve.tensor_tensor(col[0:EK, 4 + a:5 + a], col[0:EK, 2:3], col[0:EK, a:a + 1], ALU.add))
                    ch.link(dve.tensor_tensor(wr_v[:, a, :], wr_v[:, a, :], gain, ALU.mult))
                    ch.link(dve.tensor_reduce(col[0:EK, 3:4], wr_v[:, a, :], AX_X, ALU.add))
                    ch.link(dve.tensor_scalar(col[0:EK, 6:7], col[0:EK, 3:4], 1.0 / D, None, ALU.mult))
                    ch.link(dve.tensor_scalar(wr_v[:, a, :], wr_v[:, a, :], col[0:EK, 6:7], None, ALU.subtract))
                if L:
                    dve.wait_ge(wprep_st, 32 * L)
                for i in range(3):
                    dve.wait_ge(wprep_pe, 4 * L + i + 1)
                    dve.tensor_copy(wc[:, i * 3 * E:(i + 1) * 3 * E], two[0:TQ, i % 2, 0:3 * E]).then_inc(wprep_out, 1)
                dve.wait_ge(wprep_pe, 4 * L + 4)
                dve.tensor_copy(cq[:, :], misc[0:MT, 0:4]).then_inc(wprep_out, 1)

            def group_norm(ch, b, src, pe_sem, pe_base, act_sem, act_n):
                ch.link(dve.tensor_reduce(col[:, 0:1], src[:, :], AX_X, ALU.add))
                dve.wait_ge(pe_sem, pe_base + 1)
                ch.link(dve.tensor_scalar(imgC[:, :], src[:, :], misc[:, 0:1], None, ALU.subtract))
                ch.link(dve.tensor_tensor(cover2(), imgC[:, :], imgC[:, :], ALU.mult))
                ch.link(dve.tensor_reduce(col[:, 1:2], cover2(), AX_X, ALU.add))
                dve.wait_ge(pe_sem, pe_base + 2)
                ch.link(dve.tensor_scalar(col[:, 2:3], misc[:, 1:2], GN_EPS, None, ALU.add))
                dve.wait_ge(act_sem, act_n)
                dve.reciprocal(col[:, 5:6], col[:, 3:4]).then_inc(gn_rec, 1)
                dve.wait_ge(gn_rec, b + 1)
                ch.link(dve.tensor_scalar(imgC[:, :], imgC[:, :], col[:, 5:6], None, ALU.mult))

            def cover2():
                return Pt[:, 3, :]

            dve.nop(nofuse=True)
            with dve.Fori(0, B) as b:
                ch = Chain(dve, gn_step, 6 * b)
                dve.wait_ge(gn_in, 64 * (b + 1))
                dve.wait_ge(gn_stored, 64 * b)
                group_norm(ch, b, imgA, gn_pe, 2 * b, gn_act, b + 1)

            def row_max(n, s, q):
                for i in range(2):
                    dve.wait_ge(p1_ready, 64 * n + 2 * (8 * s + q) + i + 1)
                    dve.tensor_reduce(mxs[:, s // 2, i, (s % 2) * 8 + q:(s % 2) * 8 + q + 1], two[:, i, :],
                                      AX_X, ALU.max).then_inc(max_done, 1)

            def split_c(n, sp_):
                ch = Chain(dve, c_step, 5 * (2 * n + sp_))
                dve.wait_ge(max_done, 64 * n + 32 * (sp_ + 1) + MAX_FREE)
                ch.link(dve.tensor_tensor(nm[:, :], mxs[:, sp_, 0, :], mxs[:, sp_, 1, :], ALU.max))
                ch.link(dve.tensor_scalar(cparts[:, sp_, 0, :], nm[:, :], NEG, None, ALU.mult))
                ch.link(dve.scalar_tensor_tensor(out=cres[:, 0, :], in0=nm[:, :], scalar=NEG,
                                                 in1=cparts[:, sp_, 0, :], op0=ALU.mult, op1=ALU.subtract))
                ch.link(dve.tensor_copy(cparts[:, sp_, 1, :], cres[:, 0, :]))
                ch.link(dve.tensor_tensor(cparts[:, sp_, 2, :], cres[:, 0, :], cparts[:, sp_, 1, :], ALU.subtract))

            def take_c(n, sp_):
                dve.wait_ge(tr_ready, 2 * n + sp_ + 1)
                dve.wait_ge(c_stored[sp_], 48 * n)
                dve.tensor_copy(cT[:, sp_, :], misc[0:48, 0:P // 2].bitcast(BF16)).then_inc(ct_ready, 1)

            def take_o(n, s):
                w = 4 * n + s
                dve.wait_ge(pv_done, 8 * (w + 1) + PV_FREE)
                dve.wait_ge(on_done, w + 1)
                dve.tensor_copy(Osb[:, s % 2, :], wsum[:, 0:QB]).then_inc(o_evac, 1)

            def take_den(n, s):
                dve.wait_ge(nrm_ready, 4 * n + s + 1)
                dve.reciprocal(rec[:, s % 2, :], misc[:, 0:QB]).then_inc(rec_done, 1)

            def step(kh, n0, first=False, nxt=True):
                n = n0 + kh
                for s in range(SPLIT):
                    for i in range(KT):
                        if nxt:
                            row_max(n + 1, s, i)
                        if i == 2 and not (first and s == 0):
                            take_o(n - (s == 0), (s - 1) % SPLIT)
                        if i == 1 and nxt and s == 2:
                            split_c(n + 1, 0)
                        if i == 4 and nxt and s == 2:
                            take_c(n + 1, 0)
                        if i == 6 and not (first and s == 0):
                            take_den(n - (s == 0), (s - 1) % SPLIT)
                if nxt:
                    split_c(n + 1, 1)
                    take_c(n + 1, 1)

            dve.nop(nofuse=True)
            with dve.Fori(0, LAYERS) as L:
                dve.nop(nofuse=True)
                with dve.Fori(0, B) as b:
                    u = L * B + b
                    dve.nop(nofuse=True)
                    with dve.Fori(0, CHUNKS) as c:
                        g = u * CHUNKS + c
                        ch = Chain(dve, pre_step, 6 * g)
                        dve.wait_ge(stat_ready, g + 1)
                        dve.wait_ge(r0_ready, g)
                        ch.link(dve.tensor_copy(mu[:, :], two[:, 0, :]))
                        ch.link(dve.tensor_tensor(na[:, :], two[:, 0, :], mu[:, :], ALU.mult))
                        dve.scalar_tensor_tensor(out=vpe[:, :], in0=two[:, 1, :], scalar=LN_EPS, in1=na[:, :],
                                                 op0=ALU.add, op1=ALU.subtract).then_inc(var_ready, 1)
                        dve.wait_ge(r0_ready, g + 1)
                        ch.link(dve.tensor_tensor(na[:, :], r0[:, :], r0[:, :], ALU.mult))
                        ch.link(dve.tensor_tensor(nb[:, :], na[:, :], vpe[:, :], ALU.mult))
                        ch.link(dve.tensor_scalar(na[:, :], nb[:, :], -0.5, 1.5, ALU.mult, ALU.add))
                        ch.link(dve.tensor_tensor(rstd[:, :], na[:, :], r0[:, :], ALU.mult))
                        reads = (1, 2, 4, 5)
                        for t in range(4):
                            dve.wait_ge(qkv_ready, 4 * g + t + 1)
                            dve.wait_ge(act_split, 5 * g + reads[t])
                            dve.tensor_tensor(qn[:, t, :], score[0:MT, t, :], rstd[0:MT, :],
                                              ALU.mult).then_inc(qn_ready, 1)
                        for t in range(3):
                            dve.wait_ge(act_split, 5 * g + t + 1 + SPLIT_FREE)
                            dve.wait_ge(l_done, 3 * g + t + 1)
                            dve.scalar_tensor_tensor(out=resid[:, t, :], in0=qn[:, t, :], scalar=cq[:, t:t + 1],
                                                     in1=parts[:, t, 0, :], op0=ALU.add,
                                                     op1=ALU.subtract).then_inc(r_ready, 1)

                    n0 = u * HEADS
                    for s in range(SPLIT):
                        for i in range(KT):
                            row_max(n0, s, i)
                        if s % 2:
                            split_c(n0, s // 2)
                            take_c(n0, s // 2)
                    step(0, n0, first=True)
                    dve.nop(nofuse=True)
                    with dve.Fori(1, HEADS - 1) as kh:
                        step(kh, n0)
                    step(HEADS - 1, n0, nxt=False)
                    take_o(n0 + HEADS - 1, SPLIT - 1)
                    take_den(n0 + HEADS - 1, SPLIT - 1)

                    dve.wait_ge(post_cov, u + 1)
                    for gh in range(2):
                        dve.wait_ge(fold_ready, 2 * u + gh + 1)
                        half = slice(gh * BANK, (gh + 1) * BANK)
                        last = dve.tensor_tensor(imgC[:, half], two[:, gh, :], imgB[:, half], ALU.add)
                    last.then_inc(new_ready, 1)

            dve.nop(nofuse=True)
            with dve.Fori(0, B) as b:
                ch = Chain(dve, tail_step, 12 * b)
                dve.wait_ge(tail_in, 176 * (b + 1))
                dve.wait_ge(tail_pe, 3 * b + 1)
                both = two[:, :, :].rearrange("p a n -> p (a n)")
                ch.link(dve.tensor_scalar(cover2(), both, cb[:, 0:1], None, ALU.add))
                ch.link(dve.tensor_scalar(imgC[:, :], cover2(), 0.0, None, ALU.min))
                ch.link(dve.tensor_scalar(cover2(), cover2(), 0.0, -1.0, ALU.max, ALU.add))
                ch.link(dve.tensor_tensor(imgA[:, :], imgA[:, :], imgB[:, :], ALU.add))
                dve.wait_ge(tail_act, 2 * b + 1)
                ch.link(dve.tensor_tensor(imgC[:, :], imgC[:, :], cover2(), ALU.add))
                ch.link(dve.tensor_tensor(imgB[:, :], imgA[:, :], imgC[:, :], ALU.add))
                group_norm(ch, b + B, imgB, tail_pe, 3 * b + 1, tail_act, 2 * b + 2)
                dve.nop(nofuse=True)
                with dve.Fori(0, CHUNKS) as c:
                    g = b * CHUNKS + c
                    dve.wait_ge(h_act, g + 1)
                    for m in range(8):
                        dve.wait_ge(g_ready, 8 * g + m + 1)
                        dve.tensor_tensor(qy(m), score[:, m % 4, :], hrep, ALU.mult).then_inc(y_done, 1)
                    dve.wait_ge(z_ready, g + 1)
                    dve.tensor_copy(zsb, wsum[:, :]).then_inc(z_sb, 1)
                    dve.wait_ge(f_ready, g + 1)
                    dve.wait_ge(x1_in, 16 * (g + 1))
                    dve.scalar_tensor_tensor(out=imgA[0:32, BANK:2 * BANK], in0=misc[0:32, :],
                                             scalar=bias_s[:, 0:1], in1=imgA[0:32, 0:BANK],
                                             op0=ALU.add, op1=ALU.add).then_inc(o_done, 1)

        @block.gpsimd
        def _(pool):
            with pool.Fori(0, LAYERS) as L:
                with pool.Fori(0, B) as b:
                    u = L * B + b
                    with pool.Fori(0, CHUNKS) as c:
                        g = u * CHUNKS + c
                        for t in range(3):
                            pool.wait_ge(r_ready, 3 * g + t + 1)
                            pool.nop(nofuse=True)
                            pool.tensor_copy(parts[:, t, 1, :], resid[:, t, :]).then_inc(m_done, 1)
                            pool.wait_ge(m_done, 3 * g + t + 1)
                            pool.tensor_tensor(parts[:, t, 2, :], resid[:, t, :], parts[:, t, 1, :],
                                               ALU.subtract).then_inc(l_done, 1)
                    pool.wait_ge(vt_used, (u + 1) * CHUNKS)

                    def values(n, h, s):
                        pool.wait_ge(pv_done, 32 * n + 8 * s - 8 + PV_FREE)
                        pool.nop(nofuse=True)
                        pool.tensor_copy(Vh[:, s % 2, :, 0:DH],
                                         Vall[:, s * KT:(s + 1) * KT, bass.ds(h * DH, DH)]).then_inc(vh_ready, 1)

                    def normalise(n, s):
                        w = 4 * n + s
                        pool.wait_ge(rec_done, w + 1)
                        pool.wait_ge(on_stored[s % 2], 64 * (2 * n + s // 2))
                        pool.tensor_tensor(On[:, s % 2, :], Osb[:, s % 2, :], rec[:, s % 2, :],
                                           ALU.mult).then_inc(on_done, 1)

                    n0 = u * HEADS
                    values(n0, 0, 0)
                    with pool.Fori(0, HEADS - 1) as h:
                        for s in range(SPLIT):
                            nxt = 1 if s == SPLIT - 1 else 0
                            values(n0 + h + nxt, h + nxt, (s + 1) % SPLIT)
                            normalise(n0 + h, s)
                    for s in range(SPLIT):
                        if s < 3:
                            values(n0 + HEADS - 1, HEADS - 1, s + 1)
                        normalise(n0 + HEADS - 1, s)
                    pool.wait_ge(post_in, 64 * (u + 1))
                    pool.tensor_tensor(imgB[:, :], imgA[:, :], cover[:, :], ALU.mult).then_inc(post_cov, 1)


def host_layouts(a):
    f = {n: np.ascontiguousarray(np.asarray(v)) for n, v in a.items()}

    def taps_last(w):
        return np.moveaxis(w, -3, -1)

    order = np.concatenate([np.arange(0, 2 * MT), np.arange(2 * E, 2 * E + VA),
                            np.arange(2 * MT, 2 * E), np.arange(2 * E + VA, 3 * E)])
    heads = np.arange(E).reshape(HEADS // 2, 2, DH).transpose(1, 0, 2).reshape(2, EK)
    L = {}
    B = f["x"].shape[0]
    L["x"] = f["x"].reshape(B, C, N)
    L["ln_g"] = taps_last(f["L0_conv_ln_g"].reshape(C, 3, 3)).reshape(1, D)
    L["ln_b"] = taps_last(f["L0_conv_ln_b"].reshape(C, 3, 3)).reshape(1, D)
    two_rows = lambda w: w.reshape(2, EK, -1).transpose(1, 0, 2)
    wr, br, wqkv, we = [], [], [], []
    for i in (1, 2, 3):
        wr.append(two_rows(taps_last(f[f"L0_conv_wr{i}"].reshape(E, C, 3, 3)).reshape(E, D)))
        br.append(f[f"L0_conv_br{i}"].reshape(2, EK).T)
        wqkv.append(two_rows(f[f"L0_conv_wqkv{i}"][order].T))
        w = f[f"L0_conv_we{i}"].reshape(C, 3, 3, E).transpose(3, 1, 2, 0).reshape(E, 9 * C)
        last = np.stack([f[f"L0_conv_be{i}"].reshape(C, 3, 3).transpose(1, 2, 0).reshape(9 * C),
                         np.zeros(9 * C, np.float32)])
        we.append(np.concatenate([w[heads], last[:, None]], axis=1).transpose(1, 0, 2).reshape(EK + 1, 2 * 9 * C))
    L["wr"], L["br"], L["wqkv"], L["we"] = (np.stack(v) for v in (wr, br, wqkv, we))
    L["conv_w"] = f["L0_conv_conv_w"].transpose(3, 1, 2, 0).reshape(TQ, 3 * 32)
    L["conv_b"] = np.tile(f["L0_conv_conv_b"], 4).reshape(P, 1)
    w1 = f["L1_conv_W1"].reshape(32, C, 3, 3).transpose(3, 1, 2, 0)
    L["w1"] = np.tile(w1, (1, 1, 1, 4)).reshape(TQ, 3 * P)
    L["b1"] = np.tile(f["L1_conv_b1"], 4).reshape(P, 1)
    L["w2"] = f["L1_conv_W2"].reshape(32, C, 3, 3, 32).transpose(3, 1, 2, 0, 4).reshape(TQ, 3 * 1024)
    L["b2"] = f["L1_conv_b2"].reshape(32, C, 3, 3).transpose(3, 1, 2, 0).reshape(TQ, 3 * 32)
    L["bias"] = f["L1_conv_bias"].reshape(32, 1)
    return {n: np.ascontiguousarray(v) for n, v in L.items()}


def kernel(**inputs):
    import concourse.bacc as bacc
    from concourse.bass_utils import run_bass_kernel_spmd

    nc = bacc.Bacc("TRN2", target_bir_lowering=False, num_devices=1)
    data, tables = host_layouts(inputs), constants()
    B = data["x"].shape[0]

    def arg(name, a):
        return nc.dram_tensor(name, a.shape, F32, kind="ExternalInput").ap()

    args = {n: arg(f"in_{n}", a) for n, a in data.items()}
    k = {n: arg(f"const_{n}", a) for n, a in tables.items()}
    out = nc.dram_tensor("out_0", (B, C, N), F32, kind="ExternalOutput").ap()
    preact_block(nc, 3, B, k=k, out=out, **args)
    arrays = {f"in_{n}": a for n, a in data.items()} | {f"const_{n}": a for n, a in tables.items()}
    r = run_bass_kernel_spmd(nc, [arrays], core_ids=[0])
    return r.results[0]["out_0"].reshape(B, C, IMG, IMG)
```

```python
from contextlib import ExitStack

import numpy as np

import concourse.bass as bass
from concourse import mybir

ALU = mybir.AluOpType
ACT = mybir.ActivationFunctionType
F32 = mybir.dt.float32
BF16 = mybir.dt.bfloat16
I32 = mybir.dt.int32
AX_X = mybir.AxisListType.X

C = 32
IMG = 64
PAD = IMG + 2
N = IMG * IMG
TAPS = 3
DD = C * TAPS * TAPS
E = DD // 2
HEADS = 8
DH = E // HEADS
SPLIT = 4
SPAN = N // SPLIT
SCALE = DH ** -0.5
P = 128
BANK = 512
ROWS = BANK // IMG
CHUNKS = N // BANK
KT = SPAN // P
TQ = 3 * C
MT = 3 * E // 4
VA = 2 * DH
PROD = 6 * DH
PROW = PROD + 3
QB = SPAN // 4
EK = E // 2
LN_EPS = 1e-5
GN_EPS = 1e-5
NEG = -1.0
LEAD = 10
VRING = CHUNKS + LEAD
HALO = ROWS + 2
Q = SPLIT * KT
START = 128
FAR = START + 2 * 64
MAGIC = 1597463007.0


def constants():
    p = np.arange(P)
    group = (p % C) // 2
    gn_mean = (group[:, None] == group[None, :]).astype(np.float32) / (2 * N)
    den_pick = (p[:, None] == 32 * np.arange(4)[None, :] + DH).astype(np.float32)
    quad_sum = (p[:, None] % 32 == np.arange(32)[None, :]).astype(np.float32)
    hid_sum = np.zeros((P, 8, 32), np.float32)
    for m in range(8):
        hid_sum[p, m, 4 * m + p // 32] = 1.0
    ident = np.eye(P, dtype=np.float32)
    y = np.full(IMG, 3.0, np.float32)
    y[0] = y[-1] = 2.0
    cover = (y[:, None] * y[None, :]).reshape(CHUNKS, 4, 1, 2 * IMG)
    cover = np.broadcast_to(cover, (CHUNKS, 4, 32, 2 * IMG)).transpose(1, 2, 0, 3).reshape(P, CHUNKS * 2 * IMG)
    inside = np.zeros((1, 2, PAD, PAD), np.float32)
    inside[:, :, 1:-1, 1:-1] = 1.0
    return {
        "gn_mean": gn_mean, "den_pick": den_pick, "quad_sum": quad_sum,
        "hid_sum": hid_sum.reshape(P, 256), "ident": ident,
        "cover": np.ascontiguousarray(cover), "inside": inside.reshape(1, 2, PAD, PAD),
    }


class Chain:

    def __init__(self, eng, sem, base):
        self.eng, self.sem, self.base, self.n = eng, sem, base, 0

    def link(self, ins):
        self.n += 1
        ins.then_inc(self.sem, 1)
        self.eng.wait_ge(self.sem, self.base + self.n)


def preact_block(nc, LAYERS, B, x, ln_g, ln_b, wr, br, wqkv, we, conv_w, conv_b,
                 w1, b1, w2, b2, bias, k, out):
    UNITS = LAYERS * B
    UN = UNITS * HEADS
    with ExitStack() as ctx:
        def sb(name, shape, dt=F32):
            return ctx.enter_context(nc.sbuf_tensor(name, shape, dt))

        def sem(name):
            return ctx.enter_context(nc.semaphore(name))

        counted = []

        def csem(name):
            counted.append(sem(name))
            return counted[-1]

        t_pad = nc.dram_tensor("t_pad", (UNITS + B, C, PAD, PAD), F32, kind="Internal").ap()
        o_pad = nc.dram_tensor("o_pad", (2, EK + 1, 2, PAD, PAD), F32, kind="Internal").ap()
        wc_all = nc.dram_tensor("wc_all", (LAYERS, TQ, 3 * 3 * E), F32, kind="Internal").ap()
        cq_all = nc.dram_tensor("cq_all", (LAYERS, MT, 4), F32, kind="Internal").ap()
        qkp = nc.dram_tensor("qkp", (2, 3, 2 * E, N), BF16, kind="Internal").ap()
        u_img = nc.dram_tensor("u_img", (B, C, N), F32, kind="Internal").ap()
        x1_img = nc.dram_tensor("x1_img", (B, C, N), F32, kind="Internal").ap()

        gn_mean = sb("gn_mean_s", [P, P])
        den_pick = sb("den_pick_s", [P, 4])
        quad_sum = sb("quad_sum_s", [P, 32])
        hid_sum = sb("hid_sum_s", [P, 256])
        ident = sb("ident_s", [P, P])
        identb = sb("identb", [P, P], BF16)
        cover = sb("cover_s", [P, CHUNKS * 2 * IMG])
        ones = sb("ones", [P, P])
        mean_w = sb("mean_w", [TQ, 1])
        cw = sb("cw", [TQ, 3 * 32])
        cb = sb("cb", [P, 1])
        w1s = sb("w1s", [TQ, 3 * P])
        b1s = sb("b1s", [P, 1])
        w2s = sb("w2s", [TQ, 3 * 1024])
        b2s = sb("b2s", [TQ, 3 * 32])
        bias_s = sb("bias_s", [32, 1])
        wc = sb("wc", [TQ, 9 * E])
        cq = sb("cq", [MT, 4])
        wes = sb("wes", [EK + 1, 2 * 9 * 32])

        imgA = sb("imgA", [P, 2 * BANK])
        imgB = sb("imgB", [P, 2 * BANK])
        imgC = sb("imgC", [P, 2 * BANK])
        col = sb("col", [P, 8])

        T3c = sb("T3c", [TQ, 2, HALO, IMG])
        SQc = sb("SQc", [TQ, HALO, IMG])
        vsum = sb("vsum", [TQ, 2, ROWS, IMG])
        vtmp = sb("vtmp", [TQ, 2, ROWS, IMG])
        st = sb("st", [P, 8])
        var = sb("var", [P, 4])
        guess = sb("guess", [P, 2, 4])
        nw = sb("nw", [P, 2, 4])
        D = sb("D", [P, 4, P])
        rstd = sb("rstd", [P, BANK])
        qn = sb("qn", [MT, 4, BANK])
        resid = sb("resid", [MT, 3, BANK])
        parts = sb("parts", [MT, 3, 3, BANK], BF16)
        vrow = sb("vrow", [MT, 2, BANK])
        Vall = sb("Vall", [P, VRING * 4, E])
        T3 = Vall[0:TQ, :, :].rearrange("p a e -> p (a e)")[:, 0:PAD * IMG].rearrange("p (y x) -> p y x", x=IMG)

        Q6 = sb("Q6", [PROW, 2, N], BF16)
        K6 = sb("K6", [PROW, 2, N], BF16)
        Vh = sb("Vh", [P, 2, KT, 32])
        Pt = sb("Pt", [P, 4, SPAN])
        mxs = sb("mxs", [P, 2, 2, 16])
        nm = sb("nm", [P, 16])
        cres = sb("cres", [P, 16])
        cparts = sb("cparts", [P, 2, 8, 16], BF16)
        cT = sb("cT", [48, 2, P], BF16)
        Osb = sb("Osb", [P, 2, QB])
        rden = sb("rden", [P, 8])
        rrep = sb("rrep", [P, 8, 32])
        On = sb("On", [P, 2, QB // IMG, PAD])

        OPc = sb("OPc", [EK + 1, 2, 2, HALO, PAD])
        tq = sb("tq", [P, 2, 2, PAD])
        tc_ = sb("tcov", [P, 2, IMG])
        tnew = sb("tnew", [P, 2, PAD])

        def bank(name):
            return ctx.enter_context(nc.psum_tensor(name, [P, BANK], F32))
        score = [bank("score0"), bank("score1")]
        two = ctx.enter_context(nc.psum_tensor("two", [P, 2, BANK], F32))
        wsum = bank("wsum")
        misc = bank("misc")
        aux = [bank("aux0"), bank("aux1")]

        consts_in = sem("consts_in")
        setup_dve = sem("setup_dve")
        border_in = sem("border_in")
        wload = sem("wload")
        wprep = sem("wprep")
        wprep_pe = sem("wprep_pe")
        wprep_out = sem("wprep_out")
        wprep_st = sem("wprep_st")
        gn_in, gn_step, gn_pe, gn_act = csem("gn_in"), csem("gn_step"), csem("gn_pe"), csem("gn_act")
        gn_rec, gn_stored = csem("gn_rec"), csem("gn_stored")
        t3_in = [csem("t3_in0"), csem("t3_in1")]
        w_in = csem("w_in")
        sum_step = csem("sum_step")
        stat_ready = csem("stat_ready")
        pre_step = csem("pre_step")
        rb_ready = csem("rb_ready")
        rstd_done = csem("rstd_done")
        qkv_ready = csem("qkv_ready")
        qn_ready = csem("qn_ready")
        act_split = csem("act_split")
        r_ready = csem("r_ready")
        m_done = csem("m_done")
        l_done = csem("l_done")
        part_stored = [csem(f"part_stored{i}") for i in range(3)]
        vt_ready = csem("vt_ready")
        vt_used = csem("vt_used")
        qk_in = [[csem(f"qk_in{par}_{s}") for s in range(SPLIT)] for par in range(2)]
        p1_ready = csem("p1_ready")
        max_done = csem("max_done")
        c_step = csem("c_step")
        tr_ready = csem("tr_ready")
        ct_ready = csem("ct_ready")
        c_stored = [csem(f"c_stored{i}") for i in range(2)]
        p2_ready = csem("p2_ready")
        exp_done = csem("exp_done")
        pv_done = csem("pv_done")
        vh_ready = csem("vh_ready")
        o_evac = csem("o_evac")
        den_ready = csem("den_ready")
        rec_done = csem("rec_done")
        bc_ready = csem("bc_ready")
        on_done = csem("on_done")
        on_stored = [csem(f"on_stored{i}") for i in range(2)]
        post_in = [csem("post_in0"), csem("post_in1")]
        we_in = csem("we_in")
        cov_done = csem("cov_done")
        fold_ready = csem("fold_ready")
        new_ready = csem("new_ready")
        post_stored = csem("post_stored")
        tail_in, tail_pe, tail_step = csem("tail_in"), csem("tail_pe"), csem("tail_step")
        tail_act, tail_u = csem("tail_act"), csem("tail_u")
        h_ready, h_act = csem("h_ready"), csem("h_act")
        g_ready, y_done = csem("g_ready"), csem("y_done")
        z_ready, z_sb, f_ready = csem("z_ready"), csem("z_sb"), csem("f_ready")
        x1_in, o_done, out_stored = csem("x1_in"), csem("o_done"), csem("out_stored")

        SETUP = 10

        def qy(m):
            return Pt[:, m % 4, 0:BANK]
        zsb = Pt[:, 0, BANK:2 * BANK]
        hrep = Pt[:, 1, BANK:2 * BANK]

        CONST_DMAS = 16

        def quad_dma(eng, tile, ap, s, load):
            pieces = ap.rearrange("c (g j n) -> j c g n", g=2, j=4)
            for j in range(4):
                side = tile[32 * j:32 * j + 32, :].rearrange("p (g n) -> p g n", g=2)
                if load:
                    eng.dma_start(side, pieces[j]).then_inc(s, 16)
                else:
                    eng.dma_start(pieces[j], side).then_inc(s, 16)

        def taps(c, i):
            return T3[:, :, :].rearrange("p y x -> p (y x)")[:, bass.ds((c * ROWS + i) * IMG, BANK)]

        def steps(eng, step, between=lambda: None):
            step(0, 0, 0, True, False, first=True)
            step(1, 0, 1, True, False)
            with eng.Fori(1, LEAD // 2) as r:
                step(2 * r, r, 0, True, False)
                step(2 * r + 1, r, 1, True, False)
            between()
            with eng.Fori(LEAD // 2, (UN - LEAD) // 2) as r:
                step(2 * r, r, 0, True, True)
                step(2 * r + 1, r, 1, True, True)
            with eng.Fori((UN - LEAD) // 2, UN // 2 - 1) as r:
                step(2 * r, r, 0, False, True)
                step(2 * r + 1, r, 1, False, True)
            step(UN - 2, UN // 2 - 1, 0, False, True, ahead=False)
            step(UN - 1, UN // 2 - 1, 1, False, True, nxt=False, ahead=False)

        gbank = [score[0][:, :], score[1][:, :], aux[0][:, :], aux[1][:, :]]

        block = ctx.enter_context(nc.Block())

        @block.sync
        def _(sp):
            for dst, src in ((gn_mean, k["gn_mean"]), (den_pick, k["den_pick"]), (quad_sum, k["quad_sum"]),
                             (hid_sum, k["hid_sum"]), (ident, k["ident"]), (cover, k["cover"]),
                             (cw, conv_w), (cb, conv_b), (w1s, w1), (b1s, b1), (w2s, w2), (b2s, b2),
                             (bias_s, bias)):
                sp.dma_start(dst[:, :], src).then_inc(consts_in, 16)
            sp.dma_start(imgA[0:EK, 0:DD], ln_g.to_broadcast([EK, DD])).then_inc(consts_in, 16)
            sp.dma_start(imgA[0:EK, BANK:BANK + DD], ln_b.to_broadcast([EK, DD])).then_inc(consts_in, 16)
            sp.dma_start(o_pad[0, EK:EK + 1], k["inside"]).then_inc(consts_in, 16)
            sp.dma_start(o_pad[1, EK:EK + 1], k["inside"]).then_inc(border_in, 16)
            sp.wait_ge(setup_dve, SETUP)
            zero = Vall[:, :, :].rearrange("p a e -> p (a e)")
            sp.dma_start(t_pad[0:B].rearrange("b c y x -> (b c) (y x)"), zero[0:B * C, 0:PAD * PAD]).then_inc(border_in, 16)
            for y in (0, PAD - 1):
                for u in range(B, UNITS + B, B):
                    sp.dma_start(t_pad[u:u + B, :, y, :].rearrange("b c x -> (b c) x"), zero[0:B * C, 0:PAD]).then_inc(border_in, 16)
                for i in range(2):
                    for a in range(2):
                        sp.dma_start(o_pad[i, 0:EK, a, y, :], zero[0:EK, 0:PAD]).then_inc(border_in, 16)
            sp.wait_ge(border_in, 16 * (2 + 2 * (UNITS // B + 4)))

            for L in range(LAYERS):
                if L:
                    sp.wait_ge(wprep_pe, 4 * L)
                sp.dma_start(imgB[0:EK, 0:2 * DD].rearrange("p (a j) -> p a j", a=2), wr[L]).then_inc(wload, 16)
                sp.dma_start(T3[0:EK, 0:14, :].rearrange("p y x -> p (y x)")[:, 0:6 * E]
                             .rearrange("p (a m) -> p a m", a=2), wqkv[L]).then_inc(wload, 16)
                sp.dma_start(col[0:EK, 0:2], br[L]).then_inc(wload, 16)
                sp.wait_ge(wprep_out, 4 * (L + 1))
                sp.dma_start(wc_all[L], wc[:, :]).then_inc(wprep_st, 16)
                sp.dma_start(cq_all[L], cq[:, :]).then_inc(wprep_st, 16)
                sp.wait_ge(wprep_st, 32 * (L + 1))

            with sp.Fori(0, B) as b:
                quad_dma(sp, imgA, x[b], gn_in, True)
                sp.wait_ge(gn_step, START + 6 * b + 6)
                sp.nop(nofuse=True)
                rows = t_pad[b, :, 1:IMG + 1, 1:IMG + 1]
                for gh in range(2):
                    for j in range(4):
                        y = (4 * gh + j) * ROWS
                        sp.dma_start(rows[:, y:y + ROWS, :],
                                     imgC[32 * j:32 * j + 32, gh * BANK:(gh + 1) * BANK]
                                     .rearrange("p (y x) -> p y x", x=IMG)).then_inc(gn_stored, 16)
                sp.wait_ge(gn_stored, START + 128 * b + 128)
                sp.nop(nofuse=True)

            def load_image(g, par):
                sp.wait_ge(qkv_ready, START + 4 * (g - 1))
                sp.wait_ge(sum_step, START + 5 * (g - 1))
                sp.nop(nofuse=True)
                for dj in range(TAPS):
                    sp.dma_start(T3c[C * dj:C * dj + C, par, :, :],
                                 t_pad[g // CHUNKS, :, bass.ds((g % CHUNKS) * ROWS, HALO), dj:dj + IMG]
                                 ).then_inc(t3_in[par], 16)

            def load_weights(g):
                sp.wait_ge(qkv_ready, START + 4 * g)
                sp.wait_ge(act_split, START + 5 * g)
                sp.wait_ge(r_ready, START + 3 * g)
                sp.nop(nofuse=True)
                L = g // (CHUNKS * B)
                sp.dma_start(wc[:, :], wc_all[L]).then_inc(w_in, 16)
                sp.dma_start(cq[:, :], cq_all[L]).then_inc(w_in, 16)

            def store_part(g, t):
                lo = VA if t == 2 else 0
                row = MT * t
                sp.wait_ge(l_done, START + 3 * g + t + 1)
                sp.nop(nofuse=True)
                sp.dma_start(
                    qkp[(g // CHUNKS) % 2, :, row:row + MT - lo, bass.ds((g % CHUNKS) * BANK, BANK)]
                    .rearrange("a r n -> r a n"),
                    parts[lo:MT, t, :, :]).then_inc(part_stored[t], 16)

            def load_qk(n, par, s):
                sp.wait_ge(p2_ready, START + 64 * n + 16 * s - 112)
                for t in range(3):
                    sp.wait_ge(part_stored[t], START + 16 * (CHUNKS * (n // HEADS) + 2 * s + 2))
                sp.nop(nofuse=True)
                tok = slice(s * SPAN, (s + 1) * SPAN)
                h = (n % HEADS) * DH
                q = qkp[(n // HEADS) % 2, :, bass.ds(h, DH), tok]
                kk = qkp[(n // HEADS) % 2, :, bass.ds(h + E, DH), tok]
                sp.dma_start(Q6[0:3 * DH, par, tok], q[0:1].to_broadcast([3, DH, SPAN])).then_inc(qk_in[par][s], 16)
                sp.dma_start(Q6[3 * DH:5 * DH, par, tok], q[1:2].to_broadcast([2, DH, SPAN])).then_inc(qk_in[par][s], 16)
                sp.dma_start(Q6[5 * DH:6 * DH, par, tok], q[2]).then_inc(qk_in[par][s], 16)
                sp.dma_start(K6[0:3 * DH, par, tok], kk[0:3]).then_inc(qk_in[par][s], 16)
                sp.dma_start(K6[3 * DH:5 * DH, par, tok], kk[0:2]).then_inc(qk_in[par][s], 16)
                sp.dma_start(K6[5 * DH:6 * DH, par, tok], kk[0]).then_inc(qk_in[par][s], 16)

            def store_c(n, par, half):
                sp.wait_ge(ct_ready, START + 2 * n + half + 1)
                for a in range(3):
                    sp.dma_start(
                        Q6[PROD + a:PROD + a + 1, par, half * 2 * SPAN:(half + 1) * 2 * SPAN]
                        .rearrange("o (k n) -> o k n", k=16),
                        cT[16 * a:16 * a + 16, half, :]).then_inc(c_stored[half], 16)

            def store_o(n, par, s):
                sp.wait_ge(on_done, START + 4 * n + s + 1)
                sp.nop(nofuse=True)
                for j in range(4):
                    y = 1 + (s * SPAN + j * QB) // IMG
                    sp.dma_start(
                        o_pad[(n // HEADS) % 2, bass.ds(((n % HEADS) // 2) * DH, DH), par, y:y + QB // IMG, :],
                        On[32 * j:32 * j + DH, s % 2, :, :]).then_inc(on_stored[s % 2], 16)

            def load_fold(m, par):
                sp.wait_ge(fold_ready, START + m - 1)
                sp.wait_ge(cov_done, START + m - 1)
                for i in range(2):
                    sp.wait_ge(on_stored[i], START + 64 * 2 * HEADS * (m // HEADS + 1))
                sp.nop(nofuse=True)
                row = (m % CHUNKS) * ROWS
                sp.dma_start(OPc[:, par, :, :, :],
                             o_pad[(m // HEADS) % 2, :, :, bass.ds(row, HALO), :]).then_inc(post_in[par], 16)
                for j in range(4):
                    sp.dma_start(tq[32 * j:32 * j + 32, par, :, :],
                                 t_pad[m // CHUNKS, :, bass.ds(row + 1 + 2 * j, 2), :]).then_inc(post_in[par], 16)

            def load_we(m):
                sp.wait_ge(fold_ready, START + m)
                sp.nop(nofuse=True)
                sp.dma_start(wes[:, :], we[m // (CHUNKS * B)]).then_inc(we_in, 16)

            def store_new(m):
                sp.wait_ge(post_stored, START + 64 * (m - 1))
                sp.nop(nofuse=True)
                sp.wait_ge(new_ready, START + m + 1)
                sp.nop(nofuse=True)
                for j in range(4):
                    sp.dma_start(t_pad[m // CHUNKS + B, :, bass.ds((m % CHUNKS) * ROWS + 1 + 2 * j, 2), :],
                                 tnew[32 * j:32 * j + 32, :, :]).then_inc(post_stored, 16)

            load_image(0, 0)
            with sp.Fori(0, LEAD // 2) as r:
                for par in range(2):
                    g = 2 * r + par
                    load_weights(g)
                    load_image(g + 1, 1 - par)
                    for t in range(3):
                        store_part(g, t)
            for n in range(2):
                for s in range(SPLIT):
                    load_qk(n, n, s)
            store_c(0, 0, 0)

            def step(n, r, par, pre, post, first=False, nxt=True, ahead=True):
                g, m = n + LEAD, n - LEAD
                if pre:
                    load_weights(g)
                    load_image(g + 1, 1 - par)
                if post:
                    load_we(m)
                    load_fold(m + 1, 1 - par)
                for s in range(SPLIT):
                    if ahead:
                        load_qk(n + 2, par, s)
                    if s == 0:
                        store_c(n, par, 1)
                    if post and s == 1:
                        sp.wait_ge(post_in[1 - par], START + 80 * (r - LEAD // 2 + par + 1))
                        sp.nop(nofuse=True)
                    if s or not first:
                        store_o(n - (0 if s else 1), par if s else 1 - par, (s - 1) % SPLIT)
                    if s == 2 and nxt:
                        store_c(n + 1, 1 - par, 0)
                    if pre and s == 2:
                        for i in range(SPLIT):
                            sp.wait_ge(qk_in[1 - par][i], START + 96 * (r + par + 1))
                        sp.nop(nofuse=True)
                        store_part(g, 0)
                    if pre and s == 3:
                        store_part(g, 1)
                        store_part(g, 2)
                if post:
                    store_new(m)

            steps(sp, step, between=lambda: load_fold(0, 0))
            store_o(UN - 1, 1, SPLIT - 1)
            with sp.Fori((UN - LEAD) // 2, UN // 2 - 1) as r:
                for par in range(2):
                    m = 2 * r + par
                    load_we(m)
                    load_fold(m + 1, 1 - par)
                    store_new(m)
            load_we(UN - 2)
            load_fold(UN - 1, 1)
            store_new(UN - 2)
            load_we(UN - 1)
            store_new(UN - 1)
            sp.wait_ge(post_stored, START + 64 * UN)

            with sp.Fori(0, B) as b:
                for dj in range(TAPS):
                    sp.dma_start(T3[C * dj:C * dj + C, :, :],
                                 t_pad[b + UNITS, :, :, dj:dj + IMG]).then_inc(tail_in, 16)
                for gh in range(2):
                    for j in range(4):
                        y = (4 * gh + j) * ROWS + 1
                        sp.dma_start(imgA[32 * j:32 * j + 32, gh * BANK:(gh + 1) * BANK]
                                     .rearrange("p (y x) -> p y x", x=IMG),
                                     t_pad[b, :, y:y + ROWS, 1:IMG + 1]).then_inc(tail_in, 16)
                quad_dma(sp, imgB, x[b], tail_in, True)
                sp.wait_ge(tail_step, START + 12 * b + 6)
                sp.nop(nofuse=True)
                quad_dma(sp, imgB, x1_img[b], tail_u, False)
                sp.wait_ge(tail_step, START + 12 * b + 12)
                sp.nop(nofuse=True)
                quad_dma(sp, imgC, u_img[b], tail_u, False)
                sp.wait_ge(tail_u, START + 176 * b + 128)
                sp.nop(nofuse=True)
                v = u_img[b].rearrange("c (y x) -> c y x", y=IMG)
                sp.dma_start(T3[0:C, 1:IMG + 1, 1:IMG], v[:, :, 0:IMG - 1]).then_inc(tail_u, 16)
                sp.dma_start(T3[C:2 * C, 1:IMG + 1, :], v[:, :, :]).then_inc(tail_u, 16)
                sp.dma_start(T3[2 * C:TQ, 1:IMG + 1, 0:IMG - 1], v[:, :, 1:IMG]).then_inc(tail_u, 16)
                with sp.Fori(0, CHUNKS) as c:
                    g = b * CHUNKS + c
                    tok = bass.ds(c * BANK, BANK)
                    sp.dma_start(imgA[0:32, 0:BANK], x1_img[b][:, tok]).then_inc(x1_in, 16)
                    sp.wait_ge(o_done, START + g + 1)
                    sp.nop(nofuse=True)
                    sp.dma_start(out[b][:, tok], imgA[0:32, BANK:2 * BANK]).then_inc(out_stored, 16)
                    sp.wait_ge(out_stored, START + 16 * (g + 1))
                    sp.nop(nofuse=True)

        @block.tensor
        def _(pe):
            mm = pe.matmul
            pe.wait_ge(consts_in, 16 * CONST_DMAS)
            pe.wait_ge(setup_dve, SETUP)
            wq_v = T3[0:EK, 0:14, :].rearrange("p y x -> p (y x)")[:, 0:6 * E].rearrange("p (a m) -> p a m", a=2)
            wr_v = imgB[0:EK, 0:2 * DD].rearrange("p (a j) -> p a j", a=2)
            for L in range(LAYERS):
                pe.wait_ge(wprep, 14 * (L + 1))
                for i in range(3):
                    pe.wait_ge(wprep_out, 4 * L + i // 2)
                    for a in range(2):
                        last = mm(two[0:TQ, i % 2, 0:3 * E], wr_v[:, a, i * TQ:(i + 1) * TQ], wq_v[:, a, :],
                                  start=(a == 0), stop=(a == 1))
                    last.then_inc(wprep_pe, 1)
                for t in range(4):
                    for a in range(2):
                        last = mm(misc[0:MT, t:t + 1], wq_v[:, a, t * MT:(t + 1) * MT], col[0:EK, 4 + a:5 + a],
                                  start=(a == 0), stop=(a == 1), skip_group_check=True)
                last.then_inc(wprep_pe, 1)

            with pe.Fori(0, B) as b:
                for i in range(2):
                    pe.wait_ge(gn_step, START + 6 * b + (1 if i == 0 else 4))
                    mm(misc[:, i:i + 1], gn_mean[:, :], col[:, i:i + 1], start=True, stop=True).then_inc(gn_pe, 1)

            def stats(g, folded):
                pe.wait_ge(sum_step, START + 5 * (g + 1))
                pe.wait_ge(vt_used, START + 2 * g)
                pe.wait_ge(new_ready, START + folded)
                for i in range(2):
                    for j in range(4):
                        last = mm(aux[0][:, 4 * i + j:4 * i + j + 1],
                                  vsum[:, i, 2 * j:2 * j + 2, :].rearrange("p y x -> p (y x)"), mean_w[:, :],
                                  start=True, stop=True)
                last.then_inc(stat_ready, 1)

            def spread_rstd(g):
                pe.wait_ge(pre_step, START + 14 * (g + 1))
                mm(aux[1][:, :], ones[:, :], D[:, :, :].rearrange("p j n -> p (j n)"),
                   start=True, stop=True).then_inc(rb_ready, 1)

            def qkv(g, par, t, i):
                if i == 0:
                    if t == 0:
                        pe.wait_ge(w_in, START + 32 * (g + 1))
                    if t == 1:
                        pe.wait_ge(rstd_done, START + g + 1)
                    if t >= 2:
                        pe.wait_ge(qn_ready, START + 4 * g + t - 1)
                last = mm(aux[t % 2][0:MT, :], wc[:, i * 3 * E + t * MT:i * 3 * E + (t + 1) * MT],
                          T3c[:, par, i:i + ROWS, :].rearrange("p y x -> p (y x)"), start=(i == 0), stop=(i == 2))
                if i == 2:
                    last.then_inc(qkv_ready, 1)

            def turn_v(g, a2):
                pe.wait_ge(act_split, START + 5 * g + 5)
                pe.wait_ge(qn_ready, START + 4 * g + 3 + a2)
                for a in range(2 * a2, 2 * a2 + 2):
                    o = (a % 2) * E
                    pe.transpose(aux[a2][:, o + VA:o + E], vrow[:, 1, a * P:(a + 1) * P], ident[0:MT, 0:MT])
                    last = pe.transpose(aux[a2][:, o:o + VA], vrow[0:VA, 0, a * P:(a + 1) * P],
                                        ident[0:VA, 0:VA])
                last.then_inc(vt_ready, 1)

            def fold(m, r, par, part, turned):
                if part == 0:
                    pe.wait_ge(we_in, START + 16 * (m + 1))
                    pe.wait_ge(post_in[par], START + 80 * (r - LEAD // 2 + 1))
                    pe.wait_ge(vt_used, START + turned)
                    pe.wait_ge(new_ready, START + m)
                lo, hi = (18 * part) // 4, (18 * (part + 1)) // 4
                for tap in range(lo, hi):
                    a, i, jj = tap // 9, tap % 9 // 3, tap % 3
                    for j in range(4):
                        y = 2 * j + 2 - i
                        last = mm(aux[0][32 * j:32 * j + 32, 0:2 * IMG], wes[:, tap * 32:(tap + 1) * 32],
                                  OPc[:, par, a, y:y + 2, 2 - jj:2 - jj + IMG], start=(tap == 0), stop=(tap == 17))
                if part == 3:
                    last.then_inc(fold_ready, 1)

            def p1(n, par, s, q):
                tile = slice(s * SPAN + q * P, s * SPAN + (q + 1) * P)
                for i in range(2):
                    pe.wait_ge(max_done, FAR + 64 * n + 2 * (8 * s + q) + i - 1)
                    mm(two[:, i, :], Q6[0:PROD, par, tile],
                       K6[0:PROD, par, s * SPAN + i * BANK:s * SPAN + (i + 1) * BANK],
                       start=True, stop=True).then_inc(p1_ready, 1)

            def p2(n, par, s, kt):
                tile = slice(s * SPAN + kt * P, s * SPAN + (kt + 1) * P)
                for i in range(2):
                    pe.wait_ge(exp_done, START + 64 * n + 2 * (8 * s + kt) + i - 1)
                    mm(score[i][:, :], K6[:, par, tile],
                       Q6[:, par, s * SPAN + i * BANK:s * SPAN + (i + 1) * BANK],
                       start=True, stop=True).then_inc(p2_ready, 1)

            def pv(n, s, kts):
                w = 4 * n + s
                for kt in kts:
                    if kt == 0:
                        pe.wait_ge(vh_ready, START + w + 1)
                        pe.wait_ge(o_evac, START + w)
                    pe.wait_ge(exp_done, START + 64 * n + 16 * s + 2 * kt + 2)
                    for j in range(4):
                        last = mm(wsum[32 * j:32 * j + 32, 0:QB], Vh[:, s % 2, kt, :],
                                  Pt[:, kt % 4, j * QB:(j + 1) * QB], start=(kt == 0), stop=(kt == KT - 1))
                    last.then_inc(pv_done, 1)

            def den(w, s, turned):
                pe.wait_ge(o_evac, START + w + 1)
                pe.wait_ge(on_done, START + w)
                pe.wait_ge(ct_ready, START + turned)
                for i in range(2):
                    last = mm(misc[:, 4 * i:4 * i + 4], Osb[:, s % 2, i * P:(i + 1) * P], den_pick[:, :],
                              start=True, stop=True)
                last.then_inc(den_ready, 1)

            def spread_den(w):
                pe.wait_ge(rec_done, START + 2 * w + 2)
                for i in range(2):
                    last = mm(misc[:, P + i * P:2 * P + i * P],
                              rrep[:, 4 * i:4 * i + 4, :].rearrange("p j k -> p (j k)"),
                              ident[:, :], start=True, stop=True)
                last.then_inc(bc_ready, 1)

            def turn_c(n, half, normed):
                pe.wait_ge(c_step, START + 5 * (2 * n + half + 1))
                pe.wait_ge(ct_ready, START + 2 * n + half)
                pe.wait_ge(on_done, START + normed)
                pe.transpose(misc[:, BANK - P // 2:BANK].bitcast(BF16),
                             cparts[:, half, :, :].rearrange("p a k -> p (a k)"), identb[:, :]).then_inc(tr_ready, 1)

            with pe.Fori(0, LEAD // 2) as r:
                for par in range(2):
                    g = 2 * r + par
                    stats(g, 0)
                    spread_rstd(g)
                    for t in range(4):
                        for i in range(3):
                            qkv(g, par, t, i)
                    turn_v(g, 0)
                    turn_v(g, 1)
            for s in range(SPLIT):
                pe.wait_ge(qk_in[0][s], START + 96)
                for i in range(KT):
                    p1(0, 0, s, i)
                if s == 1:
                    turn_c(0, 0, 0)

            def step(n, r, par, pre, post, first=False, nxt=True, ahead=True):
                g, m = n + LEAD, n - LEAD
                folded = m if post else 0
                for s in range(SPLIT):
                    if s % 2 == 0:
                        pe.wait_ge(c_stored[s // 2], START + 48 * (n + 1))
                    if nxt:
                        pe.wait_ge(qk_in[1 - par][s], START + 96 * (r + 1 + par))
                    for i in range(KT):
                        q = KT * s + i
                        if nxt:
                            p1(n + 1, 1 - par, s, i)
                        p2(n, par, s, i)
                        if i == 1 and (s or not first):
                            pv(n - (0 if s else 1), (s - 1) % SPLIT, (KT - 2, KT - 1))
                        if i % 2 and i > 1:
                            pv(n, s, (i - 3, i - 2))
                        if i == 3 and s == 0:
                            turn_c(n, 1, 4 * n - 1)
                        if i == 3 and s == 2 and nxt:
                            turn_c(n + 1, 0, 4 * n + 1)
                        if i == 4 and (s or not first):
                            den(4 * n + s - 1, (s - 1) % SPLIT, 2 * n + 2 + (1 if s >= 2 and nxt else 0))
                        if i == 6 and (s or not first):
                            spread_den(4 * n + s - 1)
                        if pre:
                            if q == 2:
                                stats(g, folded)
                            if q == 5:
                                spread_rstd(g)
                            if 8 <= q < 20:
                                qkv(g, par, (q - 8) // 3, (q - 8) % 3)
                            if q in (23, 25):
                                turn_v(g, (q - 23) // 2)
                        if post and 27 <= q < 31:
                            fold(m, r, par, q - 27, 2 * (g + 1) if pre else 2 * UN)

            steps(pe, step)
            pv(UN - 1, SPLIT - 1, (KT - 2, KT - 1))
            den(4 * UN - 1, SPLIT - 1, 2 * UN)
            spread_den(4 * UN - 1)
            with pe.Fori((UN - LEAD) // 2, UN // 2) as r:
                for par in range(2):
                    for part in range(4):
                        fold(2 * r + par, r + LEAD // 2, par, part, 2 * UN)

            with pe.Fori(0, B) as b:
                pe.wait_ge(tail_in, START + 240 * (b + 1))
                for gh in range(2):
                    for i in range(TAPS):
                        for j in range(4):
                            y = (4 * gh + j) * ROWS + i
                            last = mm(two[32 * j:32 * j + 32, gh, :], cw[:, i * 32:(i + 1) * 32],
                                      T3[:, y:y + ROWS, :], start=(i == 0), stop=(i == 2))
                last.then_inc(tail_pe, 1)
                for i in range(2):
                    pe.wait_ge(tail_step, START + 12 * b + (7 if i == 0 else 10))
                    mm(misc[:, i:i + 1], gn_mean[:, :], col[:, i:i + 1], start=True, stop=True).then_inc(tail_pe, 1)
                pe.wait_ge(tail_u, START + 176 * (b + 1))
                pe.nop(nofuse=True)
                with pe.Fori(0, CHUNKS) as c:
                    g = b * CHUNKS + c
                    pe.wait_ge(h_act, START + g)
                    for i in range(3):
                        last = mm(two[:, 0, :], w1s[:, i * P:(i + 1) * P], taps(c, i), start=(i == 0), stop=(i == 2))
                    last.then_inc(h_ready, 1)

                    def reduce_y(m):
                        pe.wait_ge(y_done, START + 8 * g + m + 1)
                        j = m % 4
                        return mm(wsum[32 * j:32 * j + 32, :], hid_sum[:, 32 * m:32 * m + 32], qy(m),
                                  start=(m < 4), stop=(m >= 4))

                    for m in range(8):
                        pe.wait_ge(y_done, START + 8 * g + m - 3)
                        for i in range(3):
                            last = mm(gbank[m % 4], w2s[:, i * 1024 + m * P:i * 1024 + (m + 1) * P],
                                      taps(c, i), start=(i == 0), stop=(i == 2))
                        last.then_inc(g_ready, 1)
                        if m == 0:
                            pe.wait_ge(z_sb, START + g)
                        if m >= 1:
                            reduce_y(m - 1)
                    pe.wait_ge(o_done, START + g)
                    reduce_y(7).then_inc(z_ready, 1)
                    for i in range(3):
                        mm(misc[0:32, :], b2s[:, i * 32:(i + 1) * 32], taps(c, i), start=(i == 0), stop=False)
                    pe.wait_ge(z_sb, START + g + 1)
                    mm(misc[0:32, :], quad_sum[:, :], zsb, start=False, stop=True).then_inc(f_ready, 1)

        @block.scalar
        def _(act):
            with act.Fori(0, B) as b:
                act.wait_ge(gn_step, START + 6 * b + 5)
                act.activation(col[:, 3:4], col[:, 2:3], ACT.Sqrt).then_inc(gn_act, 1)

            def take_rstd(g):
                act.wait_ge(rb_ready, START + g + 1)
                act.wait_ge(qn_ready, START + 4 * g)
                act.activation(rstd[:, :], aux[1][:, :], ACT.Copy).then_inc(rstd_done, 1)

            def high_part(g, t):
                act.wait_ge(qn_ready, START + 4 * g + t + 1)
                act.wait_ge(part_stored[t], START + 16 * g)
                act.activation(parts[:, t, 0, :], qn[:, t, :], ACT.Identity, bias=cq[:, t:t + 1]).then_inc(act_split, 1)

            def value_rows(g, t):
                act.wait_ge(qn_ready, START + 4 * g + t + 1)
                act.wait_ge(vt_ready, START + 2 * g)
                rows = VA if t == 2 else MT
                act.activation(vrow[0:rows, t - 2, :], qn[0:rows, t, :], ACT.Identity,
                               bias=cq[0:rows, t:t + 1]).then_inc(act_split, 1)

            def take_v(g, a2):
                act.wait_ge(vt_ready, START + 2 * g + a2 + 1)
                act.activation(Vall[:, bass.ds((g % VRING) * 4 + 2 * a2, 2), :].rearrange("p k e -> p (k e)"),
                               aux[a2][:, 0:2 * E], ACT.Copy).then_inc(vt_used, 1)

            def exps(n, s, kt):
                act.wait_ge(pv_done, START + 32 * n + 8 * s + kt - 3)
                for i in range(2):
                    act.wait_ge(p2_ready, START + 64 * n + 2 * (8 * s + kt) + i + 1)
                    act.activation(Pt[:, kt % 4, i * BANK:(i + 1) * BANK], score[i][:, :],
                                   ACT.Exp, scale=SCALE).then_inc(exp_done, 1)

            def take_o(w, s):
                act.wait_ge(pv_done, START + 8 * (w + 1))
                act.wait_ge(on_done, START + w - 1)
                act.activation(Osb[:, s % 2, :], wsum[:, 0:QB], ACT.Copy).then_inc(o_evac, 1)

            with act.Fori(0, LEAD // 2) as r:
                for par in range(2):
                    g = 2 * r + par
                    act.wait_ge(w_in, START + 32 * (g + 1))
                    take_rstd(g)
                    for t in range(4):
                        if t < 3:
                            high_part(g, t)
                        if t >= 2:
                            value_rows(g, t)
                    take_v(g, 0)
                    take_v(g, 1)

            def step(n, r, par, pre, post, first=False, nxt=True, ahead=True):
                g = n + LEAD
                for s in range(SPLIT):
                    for i in range(KT):
                        q = KT * s + i
                        exps(n, s, i)
                        if i == 2 and (s or not first):
                            take_o(4 * n + s - 1, (s - 1) % SPLIT)
                        if pre:
                            if q == 6:
                                take_rstd(g)
                            if q == 12:
                                high_part(g, 0)
                            if q == 15:
                                high_part(g, 1)
                            if q == 18:
                                high_part(g, 2)
                                value_rows(g, 2)
                            if q == 21:
                                value_rows(g, 3)
                            if q in (24, 26):
                                take_v(g, (q - 24) // 2)

            steps(act, step)
            take_o(4 * UN - 1, SPLIT - 1)

            with act.Fori(0, B) as b:
                act.wait_ge(tail_step, START + 12 * b + 2)
                act.activation(imgC[:, :], imgC[:, :], ACT.Exp).then_inc(tail_act, 1)
                act.wait_ge(tail_step, START + 12 * b + 11)
                act.activation(col[:, 3:4], col[:, 2:3], ACT.Sqrt).then_inc(tail_act, 1)
                with act.Fori(0, CHUNKS) as c:
                    g = b * CHUNKS + c
                    act.wait_ge(h_ready, START + g + 1)
                    act.wait_ge(y_done, START + 8 * g)
                    act.activation(hrep, two[:, 0, :], ACT.Tanh, bias=b1s[:, 0:1]).then_inc(h_act, 1)

        @block.vector
        def _(dve):
            for s in counted:
                dve.sem_inc(s, FAR if s in (p1_ready, max_done) else START)
            dve.memset(Vall[:, 0:31, :], 0.0).then_inc(setup_dve, 1)
            dve.memset(K6[96:PROW, :, :], 1.0).then_inc(setup_dve, 1)
            dve.memset(mean_w[:, :], 1.0 / DD).then_inc(setup_dve, 1)
            dve.memset(ones[:, :], 1.0).then_inc(setup_dve, 1)
            dve.memset(On[:, :, :, :], 0.0).then_inc(setup_dve, 1)
            dve.memset(tnew[:, :, :], 0.0).then_inc(setup_dve, 1)
            dve.memset(Vh[:, :, :, :], 0.0).then_inc(setup_dve, 1)
            dve.memset(cparts[:, :, :, :], 0.0).then_inc(setup_dve, 1)
            dve.wait_ge(setup_dve, 8)
            dve.memset(Vh[:, :, :, DH:DH + 1], 1.0).then_inc(setup_dve, 1)
            dve.wait_ge(consts_in, 16 * CONST_DMAS)
            dve.tensor_copy(identb[:, :], ident[:, :]).then_inc(setup_dve, 1)
            wr_v = imgB[0:EK, 0:2 * DD].rearrange("p (a j) -> p a j", a=2)
            gain, shift = imgA[0:EK, 0:DD], imgA[0:EK, BANK:BANK + DD]
            for L in range(LAYERS):
                ch = Chain(dve, wprep, 14 * L)
                dve.wait_ge(wload, 48 * (L + 1))
                for a in range(2):
                    ch.link(dve.tensor_tensor(imgC[0:EK, 0:DD], wr_v[:, a, :], shift, ALU.mult))
                    ch.link(dve.tensor_reduce(col[0:EK, 2:3], imgC[0:EK, 0:DD], AX_X, ALU.add))
                    ch.link(dve.tensor_tensor(col[0:EK, 4 + a:5 + a], col[0:EK, 2:3], col[0:EK, a:a + 1], ALU.add))
                    ch.link(dve.tensor_tensor(wr_v[:, a, :], wr_v[:, a, :], gain, ALU.mult))
                    ch.link(dve.tensor_reduce(col[0:EK, 3:4], wr_v[:, a, :], AX_X, ALU.add))
                    ch.link(dve.tensor_scalar(col[0:EK, 6:7], col[0:EK, 3:4], 1.0 / DD, None, ALU.mult))
                    ch.link(dve.tensor_scalar(wr_v[:, a, :], wr_v[:, a, :], col[0:EK, 6:7], None, ALU.subtract))
                if L:
                    dve.wait_ge(wprep_st, 32 * L)
                for i in range(3):
                    dve.wait_ge(wprep_pe, 4 * L + i + 1)
                    dve.tensor_copy(wc[:, i * 3 * E:(i + 1) * 3 * E], two[0:TQ, i % 2, 0:3 * E]).then_inc(wprep_out, 1)
                dve.wait_ge(wprep_pe, 4 * L + 4)
                dve.tensor_copy(cq[:, :], misc[0:MT, 0:4]).then_inc(wprep_out, 1)

            square = Pt[:, 3, :]

            def group_norm(ch, b, src, pe_sem, pe_base, act_sem, act_n):
                ch.link(dve.tensor_reduce(col[:, 0:1], src[:, :], AX_X, ALU.add))
                dve.wait_ge(pe_sem, START + pe_base + 1)
                ch.link(dve.tensor_scalar(imgC[:, :], src[:, :], misc[:, 0:1], None, ALU.subtract))
                ch.link(dve.tensor_tensor(square, imgC[:, :], imgC[:, :], ALU.mult))
                ch.link(dve.tensor_reduce(col[:, 1:2], square, AX_X, ALU.add))
                dve.wait_ge(pe_sem, START + pe_base + 2)
                ch.link(dve.tensor_scalar(col[:, 2:3], misc[:, 1:2], GN_EPS, None, ALU.add))
                dve.wait_ge(act_sem, START + act_n)
                dve.reciprocal(col[:, 5:6], col[:, 3:4]).then_inc(gn_rec, 1)
                dve.wait_ge(gn_rec, START + b + 1)
                ch.link(dve.tensor_scalar(imgC[:, :], imgC[:, :], col[:, 5:6], None, ALU.mult))

            with dve.Fori(0, B) as b:
                ch = Chain(dve, gn_step, START + 6 * b)
                dve.wait_ge(gn_in, START + 64 * (b + 1))
                dve.wait_ge(gn_stored, START + 128 * b)
                group_norm(ch, b, imgA, gn_pe, 2 * b, gn_act, b + 1)

            def inverse_std(g):
                ch = Chain(dve, pre_step, START + 14 * g)
                dve.wait_ge(stat_ready, START + g + 1)
                ch.link(dve.tensor_copy(st[:, :], aux[0][:, 0:8]))
                ch.link(dve.tensor_tensor(nw[:, 0, :], st[:, 0:4], st[:, 0:4], ALU.mult))
                ch.link(dve.scalar_tensor_tensor(out=var[:, :], in0=st[:, 4:8], scalar=LN_EPS, in1=nw[:, 0, :],
                                                 op0=ALU.add, op1=ALU.subtract))
                ch.link(dve.tensor_scalar(guess[:, 0, :].bitcast(I32), var[:, :].bitcast(I32), -0.5, MAGIC,
                                          ALU.mult, ALU.add))
                for it in range(3):
                    now, then = guess[:, it % 2, :], guess[:, 1 - it % 2, :]
                    ch.link(dve.tensor_tensor(nw[:, 0, :], now, now, ALU.mult))
                    ch.link(dve.scalar_tensor_tensor(out=nw[:, 1, :], in0=nw[:, 0, :], scalar=-0.5, in1=var[:, :],
                                                     op0=ALU.mult, op1=ALU.mult))
                    ch.link(dve.scalar_tensor_tensor(out=then, in0=nw[:, 1, :], scalar=1.5, in1=now,
                                                     op0=ALU.add, op1=ALU.mult))
                dve.wait_ge(rb_ready, START + g)
                ch.link(dve.tensor_tensor(D[:, :, :], ident[:, :].unsqueeze(1).to_broadcast([P, 4, P]),
                                          guess[:, 1, :].unsqueeze(2).to_broadcast([P, 4, P]), ALU.mult))

            reads = (1, 2, 4, 5)

            def scale(g, t):
                dve.wait_ge(qkv_ready, START + 4 * g + t + 1)
                dve.wait_ge(rstd_done, START + g + 1)
                dve.wait_ge(act_split, START + 5 * (g - 1) + reads[t])
                dve.tensor_tensor(qn[:, t, :], aux[t % 2][0:MT, :], rstd[0:MT, :], ALU.mult).then_inc(qn_ready, 1)

            def residue(g, t):
                dve.wait_ge(act_split, START + 5 * g + t + 1)
                dve.wait_ge(l_done, START + 3 * (g - 1) + t + 1)
                dve.scalar_tensor_tensor(out=resid[:, t, :], in0=qn[:, t, :], scalar=cq[:, t:t + 1],
                                         in1=parts[:, t, 0, :], op0=ALU.add,
                                         op1=ALU.subtract).then_inc(r_ready, 1)

            def row_max(n, s, q):
                for i in range(2):
                    dve.wait_ge(p1_ready, FAR + 64 * n + 2 * (8 * s + q) + i + 1)
                    dve.tensor_reduce(mxs[:, s // 2, i, (s % 2) * 8 + q:(s % 2) * 8 + q + 1], two[:, i, :],
                                      AX_X, ALU.max).then_inc(max_done, 1)

            def split_c(n, half):
                ch = Chain(dve, c_step, START + 5 * (2 * n + half))
                dve.wait_ge(max_done, FAR + 64 * n + 32 * (half + 1))
                ch.link(dve.tensor_tensor(nm[:, :], mxs[:, half, 0, :], mxs[:, half, 1, :], ALU.max))
                ch.link(dve.tensor_scalar(cparts[:, half, 0, :], nm[:, :], NEG, None, ALU.mult))
                ch.link(dve.scalar_tensor_tensor(out=cres[:, :], in0=nm[:, :], scalar=NEG,
                                                 in1=cparts[:, half, 0, :], op0=ALU.mult, op1=ALU.subtract))
                ch.link(dve.tensor_copy(cparts[:, half, 1, :], cres[:, :]))
                ch.link(dve.tensor_tensor(cparts[:, half, 2, :], cres[:, :], cparts[:, half, 1, :], ALU.subtract))

            def take_c(n, half):
                dve.wait_ge(tr_ready, START + 2 * n + half + 1)
                dve.wait_ge(c_stored[half], START + 48 * n)
                dve.tensor_copy(cT[:, half, :], misc[0:48, BANK - P // 2:BANK].bitcast(BF16)).then_inc(ct_ready, 1)

            def take_den(w):
                dve.wait_ge(den_ready, START + w + 1)
                ch = Chain(dve, rec_done, START + 2 * w)
                ch.link(dve.reciprocal(rden[:, :], misc[:, 0:8]))
                ch.link(dve.tensor_copy(rrep[:, :, :], rden[:, :].unsqueeze(2).to_broadcast([P, 8, 32])))

            def normalise(n, s):
                dve.wait_ge(bc_ready, START + 4 * n + s + 1)
                dve.wait_ge(on_stored[s % 2], START + 64 * (2 * n + s // 2))
                dve.tensor_tensor(On[:, s % 2, :, 1:IMG + 1],
                                  misc[:, P:3 * P].rearrange("p (y x) -> p y x", x=IMG),
                                  Osb[:, s % 2, :].rearrange("p (y x) -> p y x", x=IMG), ALU.mult).then_inc(on_done, 1)

            def add_fold(m):
                dve.wait_ge(fold_ready, START + m + 1)
                dve.wait_ge(cov_done, START + m + 1)
                dve.wait_ge(post_stored, START + 64 * m)
                dve.tensor_tensor(tnew[:, :, 1:IMG + 1], aux[0][:, 0:2 * IMG].rearrange("p (y x) -> p y x", x=IMG),
                                  tc_[:, :, :], ALU.add).then_inc(new_ready, 1)

            dve.nop(nofuse=True)
            with dve.Fori(0, LEAD // 2) as r:
                for par in range(2):
                    g = 2 * r + par
                    inverse_std(g)
                    for t in range(4):
                        scale(g, t)
                    for t in range(3):
                        residue(g, t)
            for s in range(SPLIT):
                for i in range(KT):
                    row_max(0, s, i)
                if s == 1:
                    split_c(0, 0)
                    take_c(0, 0)

            def step(n, r, par, pre, post, first=False, nxt=True, ahead=True):
                g, m = n + LEAD, n - LEAD
                for s in range(SPLIT):
                    for i in range(KT):
                        q = KT * s + i
                        if nxt:
                            row_max(n + 1, s, i)
                        if i == 1 and s == 0:
                            split_c(n, 1)
                        if i == 4 and s == 0:
                            take_c(n, 1)
                        if i == 1 and s == 2 and nxt:
                            split_c(n + 1, 0)
                        if i == 4 and s == 2 and nxt:
                            take_c(n + 1, 0)
                        if i == 5 and (s or not first):
                            take_den(4 * n + s - 1)
                        if i == 7 and (s or not first):
                            normalise(n - (0 if s else 1), (s - 1) % SPLIT)
                        if pre:
                            if q == 3:
                                inverse_std(g)
                            if q in (11, 14, 17, 20):
                                scale(g, (q - 11) // 3)
                            if q in (13, 16, 19):
                                residue(g, (q - 13) // 3)
                if post:
                    add_fold(m)

            steps(dve, step)
            take_den(4 * UN - 1)
            normalise(UN - 1, SPLIT - 1)
            dve.nop(nofuse=True)
            with dve.Fori(UN - LEAD, UN) as m:
                add_fold(m)

            dve.nop(nofuse=True)
            with dve.Fori(0, B) as b:
                ch = Chain(dve, tail_step, START + 12 * b)
                dve.wait_ge(tail_in, START + 240 * (b + 1))
                dve.wait_ge(tail_pe, START + 3 * b + 1)
                both = two[:, :, :].rearrange("p a n -> p (a n)")
                ch.link(dve.tensor_scalar(square, both, cb[:, 0:1], None, ALU.add))
                ch.link(dve.tensor_scalar(imgC[:, :], square, 0.0, None, ALU.min))
                ch.link(dve.tensor_scalar(square, square, 0.0, -1.0, ALU.max, ALU.add))
                ch.link(dve.tensor_tensor(imgA[:, :], imgA[:, :], imgB[:, :], ALU.add))
                dve.wait_ge(tail_act, START + 2 * b + 1)
                ch.link(dve.tensor_tensor(imgC[:, :], imgC[:, :], square, ALU.add))
                ch.link(dve.tensor_tensor(imgB[:, :], imgA[:, :], imgC[:, :], ALU.add))
                group_norm(ch, b + B, imgB, tail_pe, 3 * b + 1, tail_act, 2 * b + 2)
                dve.nop(nofuse=True)
                with dve.Fori(0, CHUNKS) as c:
                    g = b * CHUNKS + c
                    dve.wait_ge(h_act, START + g + 1)
                    for m in range(8):
                        dve.wait_ge(g_ready, START + 8 * g + m + 1)
                        dve.tensor_tensor(qy(m), gbank[m % 4], hrep, ALU.mult).then_inc(y_done, 1)
                    dve.wait_ge(z_ready, START + g + 1)
                    dve.tensor_copy(zsb, wsum[:, :]).then_inc(z_sb, 1)
                    dve.wait_ge(f_ready, START + g + 1)
                    dve.wait_ge(x1_in, START + 16 * (g + 1))
                    dve.scalar_tensor_tensor(out=imgA[0:32, BANK:2 * BANK], in0=misc[0:32, :],
                                             scalar=bias_s[:, 0:1], in1=imgA[0:32, 0:BANK],
                                             op0=ALU.add, op1=ALU.add).then_inc(o_done, 1)

        @block.gpsimd
        def _(pool):
            def sums(g, par, half):
                ch = Chain(pool, sum_step, START + 5 * g)
                pool.wait_ge(t3_in[par], START + 48 * (half + 1))
                pool.wait_ge(stat_ready, START + g)
                img = T3c[:, par, :, :]
                ch.link(pool.tensor_tensor(SQc[:, :, :], img, img, ALU.mult))
                for i, t in enumerate((img, SQc[:, :, :])):
                    ch.link(pool.tensor_tensor(vtmp[:, i, :, :], t[:, 0:ROWS, :], t[:, 1:ROWS + 1, :], ALU.add))
                    ch.link(pool.tensor_tensor(vsum[:, i, :, :], vtmp[:, i, :, :], t[:, 2:ROWS + 2, :], ALU.add))

            def low_parts(g, t):
                pool.wait_ge(r_ready, START + 3 * g + t + 1)
                pool.nop(nofuse=True)
                pool.tensor_copy(parts[:, t, 1, :], resid[:, t, :]).then_inc(m_done, 1)
                pool.wait_ge(m_done, START + 3 * g + t + 1)
                pool.tensor_tensor(parts[:, t, 2, :], resid[:, t, :], parts[:, t, 1, :], ALU.subtract).then_inc(l_done, 1)

            def values(n, s):
                pool.wait_ge(pv_done, START + 32 * n + 8 * s - 8)
                pool.wait_ge(vt_used, START + 2 * CHUNKS * (n // HEADS) + 4 * s + 4)
                pool.nop(nofuse=True)
                tile = ((n // HEADS * CHUNKS + 2 * s) % VRING) * 4
                pool.tensor_copy(Vh[:, s % 2, :, 0:DH],
                                 Vall[:, bass.ds(tile, KT), bass.ds((n % HEADS) * DH, DH)]).then_inc(vh_ready, 1)

            def covered(m, par, half):
                pool.wait_ge(post_in[par], START + 80 * (half + 1))
                pool.wait_ge(new_ready, START + m)
                pool.nop(nofuse=True)
                pool.tensor_tensor(tc_[:, :, :], tq[:, par, :, 1:IMG + 1],
                                   cover[:, bass.ds((m % CHUNKS) * 2 * IMG, 2 * IMG)]
                                   .rearrange("p (y x) -> p y x", x=IMG), ALU.mult).then_inc(cov_done, 1)

            pool.wait_ge(setup_dve, SETUP)
            pool.wait_ge(consts_in, 16 * CONST_DMAS)
            sums(0, 0, 0)
            with pool.Fori(0, LEAD // 2) as r:
                for par in range(2):
                    g = 2 * r + par
                    for t in range(3):
                        low_parts(g, t)
                    sums(g + 1, 1 - par, r + par)
            values(0, 0)

            def step(n, r, par, pre, post, first=False, nxt=True, ahead=True):
                g, m = n + LEAD, n - LEAD
                if post:
                    covered(m, par, r - LEAD // 2)
                values(n, 1)
                values(n, 2)
                if pre:
                    low_parts(g, 0)
                    low_parts(g, 1)
                values(n, 3)
                if pre:
                    low_parts(g, 2)
                if nxt:
                    values(n + 1, 0)
                if pre:
                    sums(g + 1, 1 - par, r + LEAD // 2 + par)

            steps(pool, step)
            with pool.Fori((UN - LEAD) // 2, UN // 2) as r:
                for par in range(2):
                    covered(2 * r + par, par, r)


def host_layouts(a):
    f = {n: np.ascontiguousarray(np.asarray(v)) for n, v in a.items()}

    def taps_last(w):
        return np.moveaxis(w, -3, -1)

    order = np.concatenate([np.arange(0, 2 * MT), np.arange(2 * E, 2 * E + VA),
                            np.arange(2 * MT, 2 * E), np.arange(2 * E + VA, 3 * E)])
    heads = np.arange(E).reshape(HEADS // 2, 2, DH).transpose(1, 0, 2).reshape(2, EK)
    L = {}
    B = f["x"].shape[0]
    L["x"] = f["x"].reshape(B, C, N)
    L["ln_g"] = taps_last(f["L0_conv_ln_g"].reshape(C, 3, 3)).reshape(1, DD)
    L["ln_b"] = taps_last(f["L0_conv_ln_b"].reshape(C, 3, 3)).reshape(1, DD)
    two_rows = lambda w: w.reshape(2, EK, -1).transpose(1, 0, 2)
    wr, br, wqkv, we = [], [], [], []
    for i in (1, 2, 3):
        wr.append(two_rows(taps_last(f[f"L0_conv_wr{i}"].reshape(E, C, 3, 3)).reshape(E, DD)))
        br.append(f[f"L0_conv_br{i}"].reshape(2, EK).T)
        wqkv.append(two_rows(f[f"L0_conv_wqkv{i}"][order].T))
        w = f[f"L0_conv_we{i}"].reshape(C, 3, 3, E).transpose(3, 1, 2, 0).reshape(E, 9 * C)
        last = np.stack([f[f"L0_conv_be{i}"].reshape(C, 3, 3).transpose(1, 2, 0).reshape(9 * C),
                         np.zeros(9 * C, np.float32)])
        we.append(np.concatenate([w[heads], last[:, None]], axis=1).transpose(1, 0, 2).reshape(EK + 1, 2 * 9 * C))
    L["wr"], L["br"], L["wqkv"], L["we"] = (np.stack(v) for v in (wr, br, wqkv, we))
    L["conv_w"] = f["L0_conv_conv_w"].transpose(3, 1, 2, 0).reshape(TQ, 3 * 32)
    L["conv_b"] = np.tile(f["L0_conv_conv_b"], 4).reshape(P, 1)
    w1 = f["L1_conv_W1"].reshape(32, C, 3, 3).transpose(3, 1, 2, 0)
    L["w1"] = np.tile(w1, (1, 1, 1, 4)).reshape(TQ, 3 * P)
    L["b1"] = np.tile(f["L1_conv_b1"], 4).reshape(P, 1)
    L["w2"] = f["L1_conv_W2"].reshape(32, C, 3, 3, 32).transpose(3, 1, 2, 0, 4).reshape(TQ, 3 * 1024)
    L["b2"] = f["L1_conv_b2"].reshape(32, C, 3, 3).transpose(3, 1, 2, 0).reshape(TQ, 3 * 32)
    L["bias"] = f["L1_conv_bias"].reshape(32, 1)
    return {n: np.ascontiguousarray(v) for n, v in L.items()}


def kernel(**inputs):
    import concourse.bacc as bacc
    from concourse.bass_utils import run_bass_kernel_spmd

    nc = bacc.Bacc("TRN2", target_bir_lowering=False, num_devices=1)
    data, tables = host_layouts(inputs), constants()
    B = data["x"].shape[0]

    def arg(name, a):
        return nc.dram_tensor(name, a.shape, F32, kind="ExternalInput").ap()

    args = {n: arg(f"in_{n}", a) for n, a in data.items()}
    k = {n: arg(f"const_{n}", a) for n, a in tables.items()}
    out = nc.dram_tensor("out_0", (B, C, N), F32, kind="ExternalOutput").ap()
    preact_block(nc, 3, B, k=k, out=out, **args)
    arrays = {f"in_{n}": a for n, a in data.items()} | {f"const_{n}": a for n, a in tables.items()}
    r = run_bass_kernel_spmd(nc, [arrays], core_ids=[0])
    return r.results[0]["out_0"].reshape(B, C, IMG, IMG)
```

```python
from contextlib import ExitStack

import numpy as np

import concourse.bass as bass
from concourse import mybir

ALU = mybir.AluOpType
ACT = mybir.ActivationFunctionType
F32 = mybir.dt.float32
BF16 = mybir.dt.bfloat16
I32 = mybir.dt.int32
AX_X = mybir.AxisListType.X

C = 32
IMG = 64
PAD = IMG + 2
N = IMG * IMG
TAPS = 3
DD = C * TAPS * TAPS
E = DD // 2
HEADS = 8
DH = E // HEADS
SPLIT = 4
SPAN = N // SPLIT
SCALE = DH ** -0.5
P = 128
BANK = 512
ROWS = BANK // IMG
CHUNKS = N // BANK
PAIRS = CHUNKS // 2
KT = SPAN // P
TQ = 3 * C
MT = 3 * E // 4
VA = 2 * DH
PROD = 6 * DH
PROW = PROD + 3
QB = SPAN // 4
EK = E // 2
LN_EPS = 1e-5
GN_EPS = 1e-5
NEG = -1.0
LEAD = 10
VRING = CHUNKS + LEAD
HALO = ROWS + 2
Q = SPLIT * KT
START = 128
FAR = START + 2 * 64
MAGIC = 1597463007.0


def constants():
    p = np.arange(P)
    group = (p % C) // 2
    gn_mean = (group[:, None] == group[None, :]).astype(np.float32) / (2 * N)
    den_pick = (p[:, None] == 32 * np.arange(4)[None, :] + DH).astype(np.float32)
    quad_sum = (p[:, None] % 32 == np.arange(32)[None, :]).astype(np.float32)
    hid_sum = np.zeros((P, 8, 32), np.float32)
    for m in range(8):
        hid_sum[p, m, 4 * m + p // 32] = 1.0
    ident = np.eye(P, dtype=np.float32)
    y = np.full(IMG, 3.0, np.float32)
    y[0] = y[-1] = 2.0
    cover = (y[:, None] * y[None, :]).reshape(PAIRS, 4, 1, 4 * IMG)
    cover = np.broadcast_to(cover, (PAIRS, 4, 32, 4 * IMG)).transpose(1, 2, 0, 3).reshape(P, PAIRS * 4 * IMG)
    inside = np.zeros((1, 2, PAD, PAD), np.float32)
    inside[:, :, 1:-1, 1:-1] = 1.0
    return {
        "gn_mean": gn_mean, "den_pick": den_pick, "quad_sum": quad_sum,
        "hid_sum": hid_sum.reshape(P, 256), "ident": ident,
        "cover": np.ascontiguousarray(cover), "inside": inside.reshape(1, 2, PAD, PAD),
    }


class Chain:

    def __init__(self, eng, sem, base):
        self.eng, self.sem, self.base, self.n = eng, sem, base, 0

    def link(self, ins):
        self.n += 1
        ins.then_inc(self.sem, 1)
        self.eng.wait_ge(self.sem, self.base + self.n)


def preact_block(nc, LAYERS, B, x, ln_g, ln_b, wr, br, wqkv, we, conv_w, conv_b,
                 w1, b1, w2, b2, bias, k, out):
    UNITS = LAYERS * B
    UN = UNITS * HEADS
    with ExitStack() as ctx:
        def sb(name, shape, dt=F32):
            return ctx.enter_context(nc.sbuf_tensor(name, shape, dt))

        def sem(name):
            return ctx.enter_context(nc.semaphore(name))

        counted = []

        def csem(name):
            counted.append(sem(name))
            return counted[-1]

        t_pad = nc.dram_tensor("t_pad", (UNITS + B, C, PAD, PAD), F32, kind="Internal").ap()
        o_pad = nc.dram_tensor("o_pad", (2, EK + 1, 2, PAD, PAD), F32, kind="Internal").ap()
        wc_all = nc.dram_tensor("wc_all", (LAYERS, TQ, 3 * 3 * E), F32, kind="Internal").ap()
        cq_all = nc.dram_tensor("cq_all", (LAYERS, MT, 4), F32, kind="Internal").ap()
        qkp = nc.dram_tensor("qkp", (2, 3, 2 * E, N), BF16, kind="Internal").ap()
        u_img = nc.dram_tensor("u_img", (B, C, N), F32, kind="Internal").ap()
        x1_img = nc.dram_tensor("x1_img", (B, C, N), F32, kind="Internal").ap()

        gn_mean = sb("gn_mean_s", [P, P])
        den_pick = sb("den_pick_s", [P, 4])
        quad_sum = sb("quad_sum_s", [P, 32])
        hid_sum = sb("hid_sum_s", [P, 256])
        ident = sb("ident_s", [P, P])
        identb = sb("identb", [P, P], BF16)
        cover = sb("cover_s", [P, PAIRS * 4 * IMG])
        ones = sb("ones", [P, P])
        mean_w = sb("mean_w", [TQ, 1])
        cw = sb("cw", [TQ, 3 * 32])
        cb = sb("cb", [P, 1])
        w1s = sb("w1s", [TQ, 3 * P])
        b1s = sb("b1s", [P, 1])
        w2s = sb("w2s", [TQ, 3 * 1024])
        b2s = sb("b2s", [TQ, 3 * 32])
        bias_s = sb("bias_s", [32, 1])
        wc = sb("wc", [TQ, 9 * E])
        cq = sb("cq", [MT, 4])
        wes = sb("wes", [EK + 1, 2 * 9 * 32])

        imgA = sb("imgA", [P, 2 * BANK])
        imgB = sb("imgB", [P, 2 * BANK])
        imgC = sb("imgC", [P, 2 * BANK])
        col = sb("col", [P, 8])

        T3c = sb("T3c", [TQ, 2, HALO, IMG])
        SQc = sb("SQc", [TQ, HALO, IMG])
        vsum = sb("vsum", [TQ, 2, ROWS, IMG])
        vtmp = sb("vtmp", [TQ, 2, ROWS, IMG])
        st = sb("st", [P, 8])
        var = sb("var", [P, 4])
        guess = sb("guess", [P, 2, 4])
        nw = sb("nw", [P, 2, 4])
        D = sb("D", [P, 4, P])
        rstd = sb("rstd", [P, BANK])
        qn = sb("qn", [MT, 4, BANK])
        resid = sb("resid", [MT, 3, BANK])
        parts = sb("parts", [MT, 3, 3, BANK], BF16)
        vrow = sb("vrow", [MT, 2, BANK])
        Vall = sb("Vall", [P, VRING * 4, E])
        Vflat = Vall[:, :, :].rearrange("p a e -> p (a e)")

        Q6 = sb("Q6", [PROW, 2, N], BF16)
        K6 = sb("K6", [PROW, 2, N], BF16)
        Vh = sb("Vh", [P, 2, KT, 32])
        Pt = sb("Pt", [P, 4, SPAN])
        mxs = sb("mxs", [P, 2, 2, 16])
        nm = sb("nm", [P, 16])
        cres = sb("cres", [P, 16])
        cparts = sb("cparts", [P, 2, 8, 16], BF16)
        cT = sb("cT", [48, 2, P], BF16)
        Osb = sb("Osb", [P, 2, QB])
        rden = sb("rden", [P, 8])
        rrep = sb("rrep", [P, 8, 32])
        On = sb("On", [P, 2, QB // IMG, PAD])

        OPc = sb("OPc", [EK + 1, 2, 2 * ROWS + 2, PAD])
        tq = sb("tq", [P, 4, PAD])
        tc_ = sb("tcov", [P, 4, IMG])
        tnew = sb("tnew", [P, 4, PAD])

        HALF = IMG // 2 + 2
        ybuf = Vflat[:, 2 * PAD * IMG:2 * PAD * IMG + 2 * BANK]
        conv_t = [t[0:TQ, :, :].rearrange("p a n -> p (a n)").bitcast(F32)[:, 0:HALF * IMG]
                  .rearrange("p (y x) -> p y x", x=IMG) for t in (K6, Q6)]
        x1_in_t, out_t = qn[0:32, 0, :], qn[0:32, 1, :]

        def bank(name):
            return ctx.enter_context(nc.psum_tensor(name, [P, BANK], F32))
        score = [bank("score0"), bank("score1")]
        two = ctx.enter_context(nc.psum_tensor("two", [P, 2, BANK], F32))
        wsum = bank("wsum")
        misc = bank("misc")
        aux = [bank("aux0"), bank("aux1")]

        consts_in = sem("consts_in")
        setup_dve = sem("setup_dve")
        border_in = sem("border_in")
        wload = sem("wload")
        wprep = sem("wprep")
        wprep_pe = sem("wprep_pe")
        wprep_out = sem("wprep_out")
        wprep_st = sem("wprep_st")
        gn_in, gn_stored = [csem("gn_in0"), csem("gn_in1")], [csem("gn_stored0"), csem("gn_stored1")]
        gn_step, gn_pe, gn_act, gn_rec = csem("gn_step"), csem("gn_pe"), csem("gn_act"), csem("gn_rec")
        t3_in = [csem("t3_in0"), csem("t3_in1")]
        w_in = csem("w_in")
        sum_step = csem("sum_step")
        stat_ready = csem("stat_ready")
        pre_step = csem("pre_step")
        rb_ready = csem("rb_ready")
        rstd_done = csem("rstd_done")
        qkv_ready = csem("qkv_ready")
        qn_ready = csem("qn_ready")
        act_split = csem("act_split")
        r_ready = csem("r_ready")
        m_done = csem("m_done")
        l_done = csem("l_done")
        part_stored = [csem(f"part_stored{i}") for i in range(3)]
        vt_ready = csem("vt_ready")
        vt_used = csem("vt_used")
        qk_in = [[csem(f"qk_in{par}_{s}") for s in range(SPLIT)] for par in range(2)]
        p1_ready = csem("p1_ready")
        max_done = csem("max_done")
        c_step = csem("c_step")
        tr_ready = csem("tr_ready")
        ct_ready = csem("ct_ready")
        c_stored = [csem(f"c_stored{i}") for i in range(2)]
        p2_ready = csem("p2_ready")
        exp_done = csem("exp_done")
        pv_done = csem("pv_done")
        vh_ready = csem("vh_ready")
        o_evac = csem("o_evac")
        den_ready = csem("den_ready")
        rec_done = csem("rec_done")
        bc_ready = csem("bc_ready")
        on_done = csem("on_done")
        on_stored = [csem(f"on_stored{i}") for i in range(2)]
        post_in = csem("post_in")
        we_in = csem("we_in")
        cov_done = csem("cov_done")
        fold_ready = csem("fold_ready")
        new_ready = csem("new_ready")
        post_stored = csem("post_stored")
        conv_in, res_in, conv_done, mean_done = csem("conv_in"), csem("res_in"), csem("conv_done"), csem("mean_done")
        act_front, pool_front, dve_front = csem("act_front"), csem("pool_front"), csem("dve_front")
        tail_u = csem("tail_u")
        u_clear = sem("u_clear")
        h_ready, h_act = csem("h_ready"), csem("h_act")
        g_ready, y_done = csem("g_ready"), csem("y_done")
        z_ready, z_sb, f_ready = csem("z_ready"), csem("z_sb"), csem("f_ready")
        x1_in, o_done, out_stored = csem("x1_in"), csem("o_done"), csem("out_stored")

        SETUP = 10

        def qy(m):
            return Pt[:, m % 4, (m // 4) * BANK:(m // 4 + 1) * BANK]
        zsb = rstd
        hrep = D[:, :, :].rearrange("p j n -> p (j n)")

        CONST_DMAS = 16

        def quad_dma(eng, tile, ap, s, load):
            pieces = ap.rearrange("c (g j n) -> j c g n", g=2, j=4)
            for j in range(4):
                side = tile[32 * j:32 * j + 32, :].rearrange("p (g n) -> p g n", g=2)
                if load:
                    eng.dma_start(side, pieces[j]).then_inc(s, 16)
                else:
                    eng.dma_start(pieces[j], side).then_inc(s, 16)

        def taps(b, c, i):
            return Vflat[0:TQ, bass.ds((b % 2) * PAD * IMG + (c * ROWS + i) * IMG, BANK)]

        def low_parts(eng, g, t):
            eng.wait_ge(r_ready, START + 3 * g + t + 1)
            eng.nop(nofuse=True)
            eng.tensor_copy(parts[:, t, 1, :], resid[:, t, :]).then_inc(m_done, 1)
            eng.wait_ge(m_done, START + 3 * g + t + 1)
            eng.tensor_tensor(parts[:, t, 2, :], resid[:, t, :], parts[:, t, 1, :], ALU.subtract).then_inc(l_done, 1)

        def steps(eng, step, between=lambda: None):
            step(0, 0, 0, True, False, first=True)
            step(1, 0, 1, True, False)
            with eng.Fori(1, LEAD // 2) as r:
                step(2 * r, r, 0, True, False)
                step(2 * r + 1, r, 1, True, False)
            between()
            with eng.Fori(LEAD // 2, (UN - LEAD) // 2) as r:
                step(2 * r, r, 0, True, True)
                step(2 * r + 1, r, 1, True, True)
            with eng.Fori((UN - LEAD) // 2, UN // 2 - 1) as r:
                step(2 * r, r, 0, False, True)
                step(2 * r + 1, r, 1, False, True)
            step(UN - 2, UN // 2 - 1, 0, False, True, ahead=False)
            step(UN - 1, UN // 2 - 1, 1, False, True, nxt=False, ahead=False)

        gn_src, gn_dst = [imgA, imgB], [imgC, Pt[:, 2, :]]

        pro_stat, pro_rstd = misc, wsum[:, :]
        gbank = [score[0][:, :], score[1][:, :]]

        block = ctx.enter_context(nc.Block())

        @block.sync
        def _(sp):
            for dst, src in ((gn_mean, k["gn_mean"]), (den_pick, k["den_pick"]), (quad_sum, k["quad_sum"]),
                             (hid_sum, k["hid_sum"]), (ident, k["ident"]), (cover, k["cover"]),
                             (cw, conv_w), (cb, conv_b), (w1s, w1), (b1s, b1), (w2s, w2), (b2s, b2),
                             (bias_s, bias)):
                sp.dma_start(dst[:, :], src).then_inc(consts_in, 16)
            sp.dma_start(imgA[0:EK, 0:DD], ln_g.to_broadcast([EK, DD])).then_inc(consts_in, 16)
            sp.dma_start(imgA[0:EK, BANK:BANK + DD], ln_b.to_broadcast([EK, DD])).then_inc(consts_in, 16)
            sp.dma_start(o_pad[0, EK:EK + 1], k["inside"]).then_inc(consts_in, 16)
            sp.dma_start(o_pad[1, EK:EK + 1], k["inside"]).then_inc(border_in, 16)
            sp.wait_ge(setup_dve, SETUP)
            sp.dma_start(t_pad[0:B].rearrange("b c y x -> (b c) (y x)"), Vflat[0:B * C, 0:PAD * PAD]).then_inc(border_in, 16)
            for y in (0, PAD - 1):
                for u in range(B, UNITS + B, B):
                    sp.dma_start(t_pad[u:u + B, :, y, :].rearrange("b c x -> (b c) x"), Vflat[0:B * C, 0:PAD]).then_inc(border_in, 16)
                for i in range(2):
                    for a in range(2):
                        sp.dma_start(o_pad[i, 0:EK, a, y, :], Vflat[0:EK, 0:PAD]).then_inc(border_in, 16)
            sp.wait_ge(border_in, 16 * (2 + 2 * (UNITS // B + 4)))

            for L in range(LAYERS):
                if L:
                    sp.wait_ge(wprep_pe, 4 * L)
                sp.dma_start(imgB[0:EK, 0:2 * DD].rearrange("p (a j) -> p a j", a=2), wr[L]).then_inc(wload, 16)
                sp.dma_start(Vflat[0:EK, 0:6 * E]
                             .rearrange("p (a m) -> p a m", a=2), wqkv[L]).then_inc(wload, 16)
                sp.dma_start(col[0:EK, 0:2], br[L]).then_inc(wload, 16)
                sp.wait_ge(wprep_out, 4 * (L + 1))
                sp.dma_start(wc_all[L], wc[:, :]).then_inc(wprep_st, 16)
                sp.dma_start(cq_all[L], cq[:, :]).then_inc(wprep_st, 16)
                sp.wait_ge(wprep_st, 32 * (L + 1))

            def load_x(b):
                quad_dma(sp, gn_src[b % 2], x[b], gn_in[b % 2], True)

            load_x(0)
            for b in range(B):
                if b + 1 < B:
                    load_x(b + 1)
                sp.wait_ge(gn_step, START + 6 * b + 6)
                rows = t_pad[b, :, 1:IMG + 1, 1:IMG + 1]
                for gh in range(2):
                    for j in range(4):
                        y = (4 * gh + j) * ROWS
                        sp.dma_start(rows[:, y:y + ROWS, :],
                                     gn_dst[b % 2][32 * j:32 * j + 32, gh * BANK:(gh + 1) * BANK]
                                     .rearrange("p (y x) -> p y x", x=IMG)).then_inc(gn_stored[b % 2], 16)
            for i in range(2):
                sp.wait_ge(gn_stored[i], START + 128 * ((B + 1 - i) // 2))

            def load_image(g, par):
                sp.wait_ge(qkv_ready, START + 4 * (g - 1))
                sp.wait_ge(sum_step, START + 5 * (g - 1))
                sp.nop(nofuse=True)
                for dj in range(TAPS):
                    sp.dma_start(T3c[C * dj:C * dj + C, par, :, :],
                                 t_pad[g // CHUNKS, :, bass.ds((g % CHUNKS) * ROWS, HALO), dj:dj + IMG]
                                 ).then_inc(t3_in[par], 16)

            def load_weights(g):
                sp.wait_ge(qkv_ready, START + 4 * g)
                sp.wait_ge(act_split, START + 5 * g)
                sp.wait_ge(r_ready, START + 3 * g)
                sp.nop(nofuse=True)
                L = g // (CHUNKS * B)
                sp.dma_start(wc[:, :], wc_all[L]).then_inc(w_in, 16)
                sp.dma_start(cq[:, :], cq_all[L]).then_inc(w_in, 16)

            def store_part(g, t):
                lo = VA if t == 2 else 0
                row = MT * t
                sp.wait_ge(l_done, START + 3 * g + t + 1)
                sp.nop(nofuse=True)
                sp.dma_start(
                    qkp[(g // CHUNKS) % 2, :, row:row + MT - lo, bass.ds((g % CHUNKS) * BANK, BANK)]
                    .rearrange("a r n -> r a n"),
                    parts[lo:MT, t, :, :]).then_inc(part_stored[t], 16)

            def load_qk(n, par, s):
                sp.wait_ge(p2_ready, START + 64 * n + 16 * s - 112)
                for t in range(3):
                    sp.wait_ge(part_stored[t], START + 16 * (CHUNKS * (n // HEADS) + 2 * s + 2))
                sp.nop(nofuse=True)
                tok = slice(s * SPAN, (s + 1) * SPAN)
                h = (n % HEADS) * DH
                q = qkp[(n // HEADS) % 2, :, bass.ds(h, DH), tok]
                kk = qkp[(n // HEADS) % 2, :, bass.ds(h + E, DH), tok]
                sp.dma_start(Q6[0:3 * DH, par, tok], q[0:1].to_broadcast([3, DH, SPAN])).then_inc(qk_in[par][s], 16)
                sp.dma_start(Q6[3 * DH:5 * DH, par, tok], q[1:2].to_broadcast([2, DH, SPAN])).then_inc(qk_in[par][s], 16)
                sp.dma_start(Q6[5 * DH:6 * DH, par, tok], q[2]).then_inc(qk_in[par][s], 16)
                sp.dma_start(K6[0:3 * DH, par, tok], kk[0:3]).then_inc(qk_in[par][s], 16)
                sp.dma_start(K6[3 * DH:5 * DH, par, tok], kk[0:2]).then_inc(qk_in[par][s], 16)
                sp.dma_start(K6[5 * DH:6 * DH, par, tok], kk[0]).then_inc(qk_in[par][s], 16)

            def store_c(n, par, half):
                sp.wait_ge(ct_ready, START + 2 * n + half + 1)
                for a in range(3):
                    sp.dma_start(
                        Q6[PROD + a:PROD + a + 1, par, half * 2 * SPAN:(half + 1) * 2 * SPAN]
                        .rearrange("o (k n) -> o k n", k=16),
                        cT[16 * a:16 * a + 16, half, :]).then_inc(c_stored[half], 16)

            def store_o(n, par, s):
                sp.wait_ge(on_done, START + 4 * n + s + 1)
                sp.nop(nofuse=True)
                for j in range(4):
                    y = 1 + (s * SPAN + j * QB) // IMG
                    sp.dma_start(
                        o_pad[(n // HEADS) % 2, bass.ds(((n % HEADS) // 2) * DH, DH), par, y:y + QB // IMG, :],
                        On[32 * j:32 * j + DH, s % 2, :, :]).then_inc(on_stored[s % 2], 16)

            def load_fold(p):
                sp.wait_ge(fold_ready, START + p)
                sp.wait_ge(cov_done, START + p)
                for i in range(2):
                    sp.wait_ge(on_stored[i], START + 64 * 2 * HEADS * (p // PAIRS + 1))
                sp.nop(nofuse=True)
                row = (p % PAIRS) * 2 * ROWS
                sp.dma_start(OPc[:, :, :, :],
                             o_pad[(p // PAIRS) % 2, :, :, bass.ds(row, 2 * ROWS + 2), :]).then_inc(post_in, 16)
                for j in range(4):
                    sp.dma_start(tq[32 * j:32 * j + 32, :, :],
                                 t_pad[p // PAIRS, :, bass.ds(row + 1 + 4 * j, 4), :]).then_inc(post_in, 16)

            def load_we(p):
                sp.wait_ge(fold_ready, START + p)
                sp.nop(nofuse=True)
                sp.dma_start(wes[:, :], we[p // (PAIRS * B)]).then_inc(we_in, 16)

            def store_new(p):
                sp.wait_ge(post_stored, START + 64 * (p - 1))
                sp.nop(nofuse=True)
                sp.wait_ge(new_ready, START + p + 1)
                sp.nop(nofuse=True)
                for j in range(4):
                    sp.dma_start(t_pad[p // PAIRS + B, :, bass.ds((p % PAIRS) * 2 * ROWS + 1 + 4 * j, 4), :],
                                 tnew[32 * j:32 * j + 32, :, :]).then_inc(post_stored, 16)

            load_image(0, 0)
            load_weights(0)
            with sp.Fori(0, LEAD // 2 - 1) as r:
                for par in range(2):
                    g = 2 * r + par
                    load_image(g + 1, 1 - par)
                    for t in range(3):
                        store_part(g, t)
            for n in range(2):
                load_image(LEAD - 1 + n, 1 - n)
                for s in range(SPLIT):
                    load_qk(n, n, s)
                if n == 1:
                    store_c(0, 0, 0)
                for t in range(3):
                    store_part(LEAD - 2 + n, t)

            def step(n, r, par, pre, post, first=False, nxt=True, ahead=True):
                g, p = n + LEAD, r - LEAD // 2
                if pre:
                    load_weights(g)
                    load_image(g + 1, 1 - par)
                if post and par == 1:
                    load_fold(p + 1)
                    load_we(p + 1)
                for s in range(SPLIT):
                    if ahead:
                        load_qk(n + 2, par, s)
                    if s == 0:
                        store_c(n, par, 1)
                    if post and par == 0 and s == 1:
                        sp.wait_ge(post_in, START + 80 * (p + 1))
                        sp.nop(nofuse=True)
                    if s or not first:
                        store_o(n - (0 if s else 1), par if s else 1 - par, (s - 1) % SPLIT)
                    if post and par == 0 and s == 1:
                        store_new(p)
                    if s == 2 and nxt:
                        store_c(n + 1, 1 - par, 0)
                    if pre and s == 2:
                        for i in range(SPLIT):
                            sp.wait_ge(qk_in[1 - par][i], START + 96 * (r + par + 1))
                        sp.nop(nofuse=True)
                        store_part(g, 0)
                    if pre and s == 3:
                        store_part(g, 1)
                        store_part(g, 2)

            def first_fold():
                load_fold(0)
                load_we(0)

            steps(sp, step, between=first_fold)
            store_o(UN - 1, 1, SPLIT - 1)

            def load_front(b):
                for gh in range(2):
                    for dj in range(TAPS):
                        sp.dma_start(conv_t[gh][C * dj:C * dj + C, :, :],
                                     t_pad[b + UNITS, :, gh * IMG // 2:gh * IMG // 2 + HALF, dj:dj + IMG]
                                     ).then_inc(conv_in, 16)
                for gh in range(2):
                    for j in range(4):
                        y = (4 * gh + j) * ROWS + 1
                        sp.dma_start(imgA[32 * j:32 * j + 32, gh * BANK:(gh + 1) * BANK]
                                     .rearrange("p (y x) -> p y x", x=IMG),
                                     t_pad[b, :, y:y + ROWS, 1:IMG + 1]).then_inc(res_in, 16)
                quad_dma(sp, imgB, x[b], res_in, True)

            sp.wait_ge(p2_ready, START + 64 * UN)
            load_front(0)
            with sp.Fori((UN - LEAD) // 2, UN // 2 - 1) as p:
                load_fold(p + 1)
                store_new(p)
            store_new(UN // 2 - 1)
            sp.wait_ge(post_stored, START + 64 * (UN // 2))

            def turn_front(b):
                sp.wait_ge(pool_front, START + 6 * b + 5)
                sp.nop(nofuse=True)
                quad_dma(sp, imgB, x1_img[b], tail_u, False)
                sp.wait_ge(act_front, START + 6 * b + 6)
                sp.nop(nofuse=True)
                quad_dma(sp, imgC, u_img[b], tail_u, False)
                sp.wait_ge(tail_u, START + 176 * b + 128)
                sp.nop(nofuse=True)
                v = u_img[b].rearrange("c (y x) -> c y x", y=IMG)
                dst = Vflat[:, bass.ds((b % 2) * PAD * IMG, PAD * IMG)].rearrange("p (y x) -> p y x", x=IMG)
                sp.dma_start(dst[0:C, 1:IMG + 1, 1:IMG], v[:, :, 0:IMG - 1]).then_inc(tail_u, 16)
                sp.dma_start(dst[C:2 * C, 1:IMG + 1, :], v[:, :, :]).then_inc(tail_u, 16)
                sp.dma_start(dst[2 * C:TQ, 1:IMG + 1, 0:IMG - 1], v[:, :, 1:IMG]).then_inc(tail_u, 16)

            def chunks(b, lo, hi):
                with sp.Fori(lo, hi) as c:
                    g = b * CHUNKS + c
                    tok = bass.ds(c * BANK, BANK)
                    sp.dma_start(x1_in_t, x1_img[b][:, tok]).then_inc(x1_in, 16)
                    sp.wait_ge(o_done, START + g + 1)
                    sp.nop(nofuse=True)
                    sp.dma_start(out[b][:, tok], out_t).then_inc(out_stored, 16)
                    sp.wait_ge(out_stored, START + 16 * (g + 1))
                    sp.nop(nofuse=True)

            sp.wait_ge(u_clear, 1)
            turn_front(0)
            with sp.Fori(0, B - 1) as b:
                load_front(b + 1)
                chunks(b, 0, 6)
                turn_front(b + 1)
                chunks(b, 6, CHUNKS)
            chunks(B - 1, 0, CHUNKS)

        @block.tensor
        def _(pe):
            mm = pe.matmul
            pe.wait_ge(consts_in, 16 * CONST_DMAS)
            pe.wait_ge(setup_dve, SETUP)
            wq_v = Vflat[0:EK, 0:6 * E].rearrange("p (a m) -> p a m", a=2)
            wr_v = imgB[0:EK, 0:2 * DD].rearrange("p (a j) -> p a j", a=2)
            for L in range(LAYERS):
                pe.wait_ge(wprep, 14 * (L + 1))
                for i in range(3):
                    pe.wait_ge(wprep_out, 4 * L + i // 2)
                    for a in range(2):
                        last = mm(two[0:TQ, i % 2, 0:3 * E], wr_v[:, a, i * TQ:(i + 1) * TQ], wq_v[:, a, :],
                                  start=(a == 0), stop=(a == 1))
                    last.then_inc(wprep_pe, 1)
                for t in range(4):
                    for a in range(2):
                        last = mm(misc[0:MT, t:t + 1], wq_v[:, a, t * MT:(t + 1) * MT], col[0:EK, 4 + a:5 + a],
                                  start=(a == 0), stop=(a == 1), skip_group_check=True)
                last.then_inc(wprep_pe, 1)

            for b in range(B):
                for i in range(2):
                    pe.wait_ge(gn_step, START + 6 * b + (1 if i == 0 else 4))
                    mm(misc[:, i:i + 1], gn_mean[:, :], col[:, i:i + 1], start=True, stop=True).then_inc(gn_pe, 1)

            def stats(g, bank, j):
                if j == 0:
                    pe.wait_ge(sum_step, START + 5 * (g + 1))
                    pe.wait_ge(vt_used, START + 2 * g - (2 if bank is pro_stat else 0))
                for i in range(2):
                    last = mm(bank[:, 4 * i + j:4 * i + j + 1],
                              vsum[:, i, 2 * j:2 * j + 2, :].rearrange("p y x -> p (y x)"), mean_w[:, :],
                              start=True, stop=True)
                if j == 3:
                    last.then_inc(stat_ready, 1)

            def spread_rstd(g, bank):
                pe.wait_ge(pre_step, START + 14 * (g + 1))
                pe.wait_ge(rstd_done, START + g)
                mm(bank, ones[:, :], D[:, :, :].rearrange("p j n -> p (j n)"),
                   start=True, stop=True).then_inc(rb_ready, 1)

            def qkv(g, par, t, i, folded, loads, spread_in_aux=True):
                if i == 0:
                    if t == 0:
                        pe.wait_ge(w_in, START + 32 * loads)
                        pe.wait_ge(t3_in[par], START + 48 * (g // 2 + 1))
                        pe.wait_ge(vt_used, START + 2 * g)
                        pe.wait_ge(new_ready, START + folded)
                    if t == 1 and spread_in_aux:
                        pe.wait_ge(rstd_done, START + g + 1)
                    if t >= 2:
                        pe.wait_ge(qn_ready, START + 4 * g + t - 1)
                last = mm(aux[t % 2][0:MT, :], wc[:, i * 3 * E + t * MT:i * 3 * E + (t + 1) * MT],
                          T3c[:, par, i:i + ROWS, :].rearrange("p y x -> p (y x)"), start=(i == 0), stop=(i == 2))
                if i == 2:
                    last.then_inc(qkv_ready, 1)

            def turn_v(g, a2):
                pe.wait_ge(act_split, START + 5 * g + 5)
                pe.wait_ge(qn_ready, START + 4 * g + 3 + a2)
                for a in range(2 * a2, 2 * a2 + 2):
                    o = (a % 2) * E
                    pe.transpose(aux[a2][:, o + VA:o + E], vrow[:, 1, a * P:(a + 1) * P], ident[0:MT, 0:MT])
                    last = pe.transpose(aux[a2][:, o:o + VA], vrow[0:VA, 0, a * P:(a + 1) * P],
                                        ident[0:VA, 0:VA])
                last.then_inc(vt_ready, 1)

            def fold(p, part, turned, loads):
                if part == 0:
                    pe.wait_ge(we_in, START + 16 * loads)
                    pe.wait_ge(post_in, START + 80 * (p + 1))
                    pe.wait_ge(vt_used, START + turned)
                    pe.wait_ge(new_ready, START + p)
                for tap in range(3 * part, 3 * part + 3):
                    a, i, jj = tap // 9, tap % 9 // 3, tap % 3
                    for j in range(4):
                        y = 4 * j + 2 - i
                        last = mm(aux[0][32 * j:32 * j + 32, 0:4 * IMG], wes[:, tap * 32:(tap + 1) * 32],
                                  OPc[:, a, y:y + 4, 2 - jj:2 - jj + IMG], start=(tap == 0), stop=(tap == 17))
                if part == 5:
                    last.then_inc(fold_ready, 1)

            def p1(n, par, s, q, i):
                tile = slice(s * SPAN + q * P, s * SPAN + (q + 1) * P)
                pe.wait_ge(max_done, FAR + 64 * n + 2 * (8 * s + q) + i - 1)
                mm(two[:, i, :], Q6[0:PROD, par, tile],
                   K6[0:PROD, par, s * SPAN + i * BANK:s * SPAN + (i + 1) * BANK],
                   start=True, stop=True).then_inc(p1_ready, 1)

            def p2(n, par, s, kt, i):
                tile = slice(s * SPAN + kt * P, s * SPAN + (kt + 1) * P)
                pe.wait_ge(exp_done, START + 64 * n + 2 * (8 * s + kt) + i - 1)
                mm(score[i][:, :], K6[:, par, tile],
                   Q6[:, par, s * SPAN + i * BANK:s * SPAN + (i + 1) * BANK],
                   start=True, stop=True).then_inc(p2_ready, 1)

            def pv(n, s, kt):
                if kt == 0:
                    pe.wait_ge(vh_ready, START + 4 * n + s + 1)
                    pe.wait_ge(o_evac, START + 4 * n + s)
                pe.wait_ge(exp_done, START + 64 * n + 16 * s + 2 * kt + 2)
                for j in range(4):
                    last = mm(wsum[32 * j:32 * j + 32, 0:QB], Vh[:, s % 2, kt, :],
                              Pt[:, kt % 4, j * QB:(j + 1) * QB], start=(kt == 0), stop=(kt == KT - 1))
                last.then_inc(pv_done, 1)

            def den(w, s, turned):
                pe.wait_ge(o_evac, START + w + 1)
                pe.wait_ge(on_done, START + w)
                pe.wait_ge(ct_ready, START + turned)
                for i in range(2):
                    last = mm(misc[:, 4 * i:4 * i + 4], Osb[:, s % 2, i * P:(i + 1) * P], den_pick[:, :],
                              start=True, stop=True)
                last.then_inc(den_ready, 1)

            def spread_den(w):
                pe.wait_ge(rec_done, START + 2 * w + 2)
                for i in range(2):
                    last = mm(misc[:, P + i * P:2 * P + i * P],
                              rrep[:, 4 * i:4 * i + 4, :].rearrange("p j k -> p (j k)"),
                              ident[:, :], start=True, stop=True)
                last.then_inc(bc_ready, 1)

            def turn_c(n, half, normed):
                pe.wait_ge(c_step, START + 5 * (2 * n + half + 1))
                pe.wait_ge(ct_ready, START + 2 * n + half)
                pe.wait_ge(on_done, START + normed)
                pe.transpose(misc[:, BANK - P // 2:BANK].bitcast(BF16),
                             cparts[:, half, :, :].rearrange("p a k -> p (a k)"), identb[:, :]).then_inc(tr_ready, 1)

            def project_alone(g, par, first=None):
                for t in range(4):
                    for i in range(3):
                        qkv(g, par, t, i, 0, 1, spread_in_aux=False)
                        if first is not None:
                            first_scores(16 * first + 3 * t + i)
                    if t == 1:
                        spread_rstd(g, pro_rstd)
                        if first == 1:
                            turn_c(0, 0, 0)
                if first != 1:
                    for j in range(4):
                        stats(g + 1, pro_stat, j)
                turn_v(g, 0)
                turn_v(g, 1)
                if first is not None:
                    for k in range(12, 16):
                        first_scores(16 * first + k)

            def first_scores(k):
                if k % KT == 0:
                    pe.wait_ge(qk_in[0][k // KT], START + 96)
                for half in range(2):
                    p1(0, 0, k // KT, k % KT, half)

            for j in range(4):
                stats(0, pro_stat, j)
            with pe.Fori(0, LEAD // 2 - 1) as r:
                for par in range(2):
                    project_alone(2 * r + par, par)
            project_alone(LEAD - 2, 0, first=0)
            project_alone(LEAD - 1, 1, first=1)

            def step(n, r, par, pre, post, first=False, nxt=True, ahead=True):
                g, p = n + LEAD, r - LEAD // 2
                folded = p + 1 if post else 0
                qkv_slots = (8, 9, 10, 14, 15, 16, 17, 18, 20, 21, 22, 24)
                for s in range(SPLIT):
                    if s % 2 == 0:
                        pe.wait_ge(c_stored[s // 2], START + 48 * (n + 1))
                    if nxt:
                        pe.wait_ge(qk_in[1 - par][s], START + 96 * (r + 1 + par))
                    for i in range(KT):
                        q = KT * s + i
                        for half in range(2):
                            if nxt:
                                p1(n + 1, 1 - par, s, i, half)
                            p2(n, par, s, i, half)
                            if half == 0 and i >= 2:
                                pv(n, s, i - 2)
                            if half == 0 and i < 2 and (s or not first):
                                pv(n - (0 if s else 1), (s - 1) % SPLIT, KT - 2 + i)
                        if i == 3 and s == 0:
                            turn_c(n, 1, 4 * n - 1)
                        if i == 3 and s == 2 and nxt:
                            turn_c(n + 1, 0, 4 * n + 1)
                        if i == 4 and (s or not first):
                            den(4 * n + s - 1, (s - 1) % SPLIT, 2 * n + 2 + (1 if s >= 2 and nxt else 0))
                        if i == 6 and (s or not first):
                            spread_den(4 * n + s - 1)
                        if pre:
                            if 1 <= q < 5:
                                stats(g, aux[1], q - 1)
                            if q == 12:
                                spread_rstd(g, aux[1][:, :])
                            if q in qkv_slots:
                                k = qkv_slots.index(q)
                                qkv(g, par, k // 3, k % 3, folded, g - LEAD + 2)
                            if q in (27, 28):
                                turn_v(g, q - 27)
                        if post and par == 0 and q < 6:
                            fold(p, q, 2 * g - 1 if pre else 2 * UN, p + 1)

            steps(pe, step)
            pv(UN - 1, SPLIT - 1, KT - 2)
            pv(UN - 1, SPLIT - 1, KT - 1)
            den(4 * UN - 1, SPLIT - 1, 2 * UN)
            spread_den(4 * UN - 1)

            def convolve(b):
                pe.wait_ge(conv_in, START + 96 * (b + 1))
                pe.wait_ge(act_front, START + 6 * b)
                for gh in range(2):
                    for i in range(TAPS):
                        for j in range(4):
                            y = j * ROWS + i
                            last = mm(aux[gh][32 * j:32 * j + 32, :], cw[:, i * 32:(i + 1) * 32],
                                      conv_t[gh][:, y:y + ROWS, :], start=(i == 0), stop=(i == 2))
                last.then_inc(conv_done, 1)

            def group_mean(b, i):
                pe.wait_ge(dve_front, START + 5 * b + 1 + 2 * i)
                mm(two[:, 1, i:i + 1], gn_mean[:, :], col[:, i:i + 1], start=True, stop=True).then_inc(mean_done, 1)

            convolve(0)
            pe.wait_ge(act_front, START + 2)
            pe.nop(nofuse=True)
            with pe.Fori((UN - LEAD) // 2, UN // 2) as p:
                for part in range(6):
                    fold(p, part, 2 * UN, (UN - LEAD) // 2 + 1)

            def chunks(b, lo, hi):
                pe.wait_ge(tail_u, START + 176 * (b + 1))
                pe.nop(nofuse=True)
                with pe.Fori(lo, hi) as c:
                    g = b * CHUNKS + c
                    pe.wait_ge(h_act, START + g)
                    for i in range(3):
                        last = mm(two[:, 0, :], w1s[:, i * P:(i + 1) * P], taps(b, c, i), start=(i == 0), stop=(i == 2))
                    last.then_inc(h_ready, 1)

                    def reduce_y(hi):
                        for m in range(4 * hi, 4 * hi + 4):
                            pe.wait_ge(y_done, START + 8 * g + m + 1)
                            j = m % 4
                            last = mm(wsum[32 * j:32 * j + 32, :], hid_sum[:, 32 * m:32 * m + 32], qy(m),
                                      start=(m < 4), stop=(m >= 4))
                        return last

                    for m in range(8):
                        pe.wait_ge(y_done, START + 8 * g + m - 1)
                        for i in range(3):
                            last = mm(gbank[m % 2], w2s[:, i * 1024 + m * P:i * 1024 + (m + 1) * P],
                                      taps(b, c, i), start=(i == 0), stop=(i == 2))
                        last.then_inc(g_ready, 1)
                        if m == 4:
                            pe.wait_ge(z_sb, START + g)
                            reduce_y(0)
                    pe.wait_ge(o_done, START + g)
                    pe.nop(nofuse=True)
                    for i in range(3):
                        mm(misc[0:32, :], b2s[:, i * 32:(i + 1) * 32], taps(b, c, i), start=(i == 0), stop=False)
                        if i == 0:
                            reduce_y(1).then_inc(z_ready, 1)
                    pe.wait_ge(z_sb, START + g + 1)
                    mm(misc[0:32, :], quad_sum[:, :], zsb[:, :], start=False, stop=True).then_inc(f_ready, 1)

            for i in range(2):
                group_mean(0, i)
            pe.nop(nofuse=True)
            with pe.Fori(0, B - 1) as b:
                chunks(b, 0, 2)
                convolve(b + 1)
                chunks(b, 2, 4)
                group_mean(b + 1, 0)
                chunks(b, 4, 6)
                group_mean(b + 1, 1)
                chunks(b, 6, CHUNKS)
            chunks(B - 1, 0, CHUNKS)

        @block.scalar
        def _(act):
            for b in range(B):
                act.wait_ge(gn_step, START + 6 * b + 5)
                act.activation(col[:, 3:4], col[:, 2:3], ACT.Sqrt).then_inc(gn_act, 1)

            def take_rstd(g, bank):
                act.wait_ge(rb_ready, START + g + 1)
                act.wait_ge(qn_ready, START + 4 * g)
                act.activation(rstd[:, :], bank, ACT.Copy).then_inc(rstd_done, 1)

            def high_part(g, t):
                act.wait_ge(qn_ready, START + 4 * g + t + 1)
                act.wait_ge(part_stored[t], START + 16 * g)
                act.activation(parts[:, t, 0, :], qn[:, t, :], ACT.Identity, bias=cq[:, t:t + 1]).then_inc(act_split, 1)

            def value_rows(g, t):
                act.wait_ge(qn_ready, START + 4 * g + t + 1)
                act.wait_ge(vt_ready, START + 2 * g)
                rows = VA if t == 2 else MT
                act.activation(vrow[0:rows, t - 2, :], qn[0:rows, t, :], ACT.Identity,
                               bias=cq[0:rows, t:t + 1]).then_inc(act_split, 1)

            def take_v(g, a2):
                act.wait_ge(vt_ready, START + 2 * g + a2 + 1)
                act.activation(Vall[:, bass.ds((g % VRING) * 4 + 2 * a2, 2), :].rearrange("p k e -> p (k e)"),
                               aux[a2][:, 0:2 * E], ACT.Copy).then_inc(vt_used, 1)

            def exps(n, s, kt, i):
                if i == 0:
                    act.wait_ge(pv_done, START + 32 * n + 8 * s + kt - 3)
                act.wait_ge(p2_ready, START + 64 * n + 2 * (8 * s + kt) + i + 1)
                act.activation(Pt[:, kt % 4, i * BANK:(i + 1) * BANK], score[i][:, :],
                               ACT.Exp, scale=SCALE).then_inc(exp_done, 1)

            def take_o(w, s):
                act.wait_ge(pv_done, START + 8 * (w + 1))
                act.wait_ge(on_done, START + w - 1)
                act.activation(Osb[:, s % 2, :], wsum[:, 0:QB], ACT.Copy).then_inc(o_evac, 1)

            act.wait_ge(w_in, START + 32)
            act.nop(nofuse=True)
            with act.Fori(0, LEAD // 2) as r:
                for par in range(2):
                    g = 2 * r + par
                    take_rstd(g, pro_rstd)
                    for t in range(4):
                        if t < 3:
                            high_part(g, t)
                        if t >= 2:
                            value_rows(g, t)
                    take_v(g, 0)
                    take_v(g, 1)

            def step(n, r, par, pre, post, first=False, nxt=True, ahead=True):
                g = n + LEAD
                for s in range(SPLIT):
                    for i in range(KT):
                        q = KT * s + i
                        exps(n, s, i, 0)
                        if i == 1 and (s or not first):
                            take_o(4 * n + s - 1, (s - 1) % SPLIT)
                        exps(n, s, i, 1)
                        if pre:
                            if q == 12:
                                take_rstd(g, aux[1][:, :])
                            if q in (14, 18, 22):
                                high_part(g, (q - 14) // 4)
                            if q in (24, 26):
                                value_rows(g, 2 + (q - 24) // 2)
                            if q in (28, 29):
                                take_v(g, q - 28)

            steps(act, step)
            take_o(4 * UN - 1, SPLIT - 1)

            def front(b, part):
                if part == 0:
                    act.wait_ge(conv_done, START + b + 1)
                    act.wait_ge(tail_u, START + 176 * b)
                    for gh in range(2):
                        act.activation(ybuf[:, gh * BANK:(gh + 1) * BANK], aux[gh][:, :], ACT.Identity,
                                       bias=cb[:, 0:1]).then_inc(act_front, 1)
                elif part == 1:
                    act.wait_ge(pool_front, START + 6 * b + 1)
                    act.activation(imgC[:, :], imgC[:, :], ACT.Exp).then_inc(act_front, 1)
                elif part == 2:
                    act.wait_ge(dve_front, START + 5 * b + 2)
                    act.activation(imgC[:, :], imgB[:, :], ACT.Identity, bias=col[:, 6:7]).then_inc(act_front, 1)
                elif part == 3:
                    act.wait_ge(dve_front, START + 5 * b + 4)
                    act.activation(col[:, 3:4], col[:, 2:3], ACT.Sqrt).then_inc(act_front, 1)
                    act.wait_ge(dve_front, START + 5 * b + 5)
                    act.activation(imgC[:, :], imgC[:, :], ACT.Copy, scale=col[:, 5:6]).then_inc(act_front, 1)

            def chunks(b, lo, hi):
                with act.Fori(lo, hi) as c:
                    g = b * CHUNKS + c
                    act.wait_ge(h_ready, START + g + 1)
                    act.wait_ge(y_done, START + 8 * g)
                    act.activation(hrep, two[:, 0, :], ACT.Tanh, bias=b1s[:, 0:1]).then_inc(h_act, 1)

            for part in range(4):
                front(0, part)
            with act.Fori(0, B - 1) as b:
                chunks(b, 0, 2)
                front(b + 1, 0)
                front(b + 1, 1)
                chunks(b, 2, 4)
                front(b + 1, 2)
                chunks(b, 4, 6)
                front(b + 1, 3)
                chunks(b, 6, CHUNKS)
            chunks(B - 1, 0, CHUNKS)

        @block.vector
        def _(dve):
            for s in counted:
                dve.sem_inc(s, FAR if s in (p1_ready, max_done) else START)
            dve.memset(Vall[:, 0:31, :], 0.0).then_inc(setup_dve, 1)
            dve.memset(K6[96:PROW, :, :], 1.0).then_inc(setup_dve, 1)
            dve.memset(mean_w[:, :], 1.0 / DD).then_inc(setup_dve, 1)
            dve.memset(ones[:, :], 1.0).then_inc(setup_dve, 1)
            dve.memset(On[:, :, :, :], 0.0).then_inc(setup_dve, 1)
            dve.memset(tnew[:, :, :], 0.0).then_inc(setup_dve, 1)
            dve.memset(Vh[:, :, :, :], 0.0).then_inc(setup_dve, 1)
            dve.memset(cparts[:, :, :, :], 0.0).then_inc(setup_dve, 1)
            dve.wait_ge(setup_dve, 8)
            dve.memset(Vh[:, :, :, DH:DH + 1], 1.0).then_inc(setup_dve, 1)
            dve.wait_ge(consts_in, 16 * CONST_DMAS)
            dve.tensor_copy(identb[:, :], ident[:, :]).then_inc(setup_dve, 1)
            wr_v = imgB[0:EK, 0:2 * DD].rearrange("p (a j) -> p a j", a=2)
            gain, shift = imgA[0:EK, 0:DD], imgA[0:EK, BANK:BANK + DD]
            for L in range(LAYERS):
                ch = Chain(dve, wprep, 14 * L)
                dve.wait_ge(wload, 48 * (L + 1))
                for a in range(2):
                    ch.link(dve.tensor_tensor(imgC[0:EK, 0:DD], wr_v[:, a, :], shift, ALU.mult))
                    ch.link(dve.tensor_reduce(col[0:EK, 2:3], imgC[0:EK, 0:DD], AX_X, ALU.add))
                    ch.link(dve.tensor_tensor(col[0:EK, 4 + a:5 + a], col[0:EK, 2:3], col[0:EK, a:a + 1], ALU.add))
                    ch.link(dve.tensor_tensor(wr_v[:, a, :], wr_v[:, a, :], gain, ALU.mult))
                    ch.link(dve.tensor_reduce(col[0:EK, 3:4], wr_v[:, a, :], AX_X, ALU.add))
                    ch.link(dve.tensor_scalar(col[0:EK, 6:7], col[0:EK, 3:4], 1.0 / DD, None, ALU.mult))
                    ch.link(dve.tensor_scalar(wr_v[:, a, :], wr_v[:, a, :], col[0:EK, 6:7], None, ALU.subtract))
                if L:
                    dve.wait_ge(wprep_st, 32 * L)
                for i in range(3):
                    dve.wait_ge(wprep_pe, 4 * L + i + 1)
                    dve.tensor_copy(wc[:, i * 3 * E:(i + 1) * 3 * E], two[0:TQ, i % 2, 0:3 * E]).then_inc(wprep_out, 1)
                dve.wait_ge(wprep_pe, 4 * L + 4)
                dve.tensor_copy(cq[:, :], misc[0:MT, 0:4]).then_inc(wprep_out, 1)

            square = Pt[:, 3, :]
            for b in range(B):
                ch = Chain(dve, gn_step, START + 6 * b)
                src, dst = gn_src[b % 2], gn_dst[b % 2]
                dve.wait_ge(gn_in[b % 2], START + 64 * (b // 2 + 1))
                ch.link(dve.tensor_reduce(col[:, 0:1], src[:, :], AX_X, ALU.add))
                dve.wait_ge(gn_pe, START + 2 * b + 1)
                dve.wait_ge(gn_stored[b % 2], START + 128 * (b // 2))
                ch.link(dve.tensor_scalar(dst[:, :], src[:, :], misc[:, 0:1], None, ALU.subtract))
                ch.link(dve.tensor_tensor(square, dst[:, :], dst[:, :], ALU.mult))
                ch.link(dve.tensor_reduce(col[:, 1:2], square, AX_X, ALU.add))
                dve.wait_ge(gn_pe, START + 2 * b + 2)
                ch.link(dve.tensor_scalar(col[:, 2:3], misc[:, 1:2], GN_EPS, None, ALU.add))
                dve.wait_ge(gn_act, START + b + 1)
                dve.reciprocal(col[:, 5:6], col[:, 3:4]).then_inc(gn_rec, 1)
                dve.wait_ge(gn_rec, START + b + 1)
                ch.link(dve.tensor_scalar(dst[:, :], dst[:, :], col[:, 5:6], None, ALU.mult))

            def inverse_std(g, step, bank):
                now, then = (guess[:, (step - 4) // 3 % 2, :], guess[:, 1 - (step - 4) // 3 % 2, :])
                if step == 0:
                    dve.wait_ge(stat_ready, START + g + 1)
                    op = dve.tensor_copy(st[:, :], bank[:, 0:8])
                else:
                    dve.wait_ge(pre_step, START + 14 * g + step)
                if step == 1:
                    op = dve.tensor_tensor(nw[:, 0, :], st[:, 0:4], st[:, 0:4], ALU.mult)
                elif step == 2:
                    op = dve.scalar_tensor_tensor(out=var[:, :], in0=st[:, 4:8], scalar=LN_EPS, in1=nw[:, 0, :],
                                                  op0=ALU.add, op1=ALU.subtract)
                elif step == 3:
                    op = dve.tensor_scalar(guess[:, 0, :].bitcast(I32), var[:, :].bitcast(I32), -0.5, MAGIC,
                                           ALU.mult, ALU.add)
                elif step in (4, 7, 10):
                    op = dve.tensor_tensor(nw[:, 0, :], now, now, ALU.mult)
                elif step in (5, 8, 11):
                    op = dve.scalar_tensor_tensor(out=nw[:, 1, :], in0=nw[:, 0, :], scalar=-0.5, in1=var[:, :],
                                                  op0=ALU.mult, op1=ALU.mult)
                elif step in (6, 9, 12):
                    op = dve.scalar_tensor_tensor(out=then, in0=nw[:, 1, :], scalar=1.5, in1=now,
                                                  op0=ALU.add, op1=ALU.mult)
                elif step == 13:
                    dve.wait_ge(rb_ready, START + g)
                    op = dve.tensor_tensor(D[:, :, :], ident[:, :].unsqueeze(1).to_broadcast([P, 4, P]),
                                           guess[:, 1, :].unsqueeze(2).to_broadcast([P, 4, P]), ALU.mult)
                op.then_inc(pre_step, 1)

            reads = (1, 2, 4, 5)

            def scale(g, t):
                dve.wait_ge(qkv_ready, START + 4 * g + t + 1)
                dve.wait_ge(rstd_done, START + g + 1)
                dve.wait_ge(act_split, START + 5 * (g - 1) + reads[t])
                dve.tensor_tensor(qn[:, t, :], aux[t % 2][0:MT, :], rstd[0:MT, :], ALU.mult).then_inc(qn_ready, 1)

            def residue(g, t):
                dve.wait_ge(act_split, START + 5 * g + t + 1)
                dve.wait_ge(l_done, START + 3 * (g - 1) + t + 1)
                dve.scalar_tensor_tensor(out=resid[:, t, :], in0=qn[:, t, :], scalar=cq[:, t:t + 1],
                                         in1=parts[:, t, 0, :], op0=ALU.add,
                                         op1=ALU.subtract).then_inc(r_ready, 1)

            def row_max(n, s, q, i):
                dve.wait_ge(p1_ready, FAR + 64 * n + 2 * (8 * s + q) + i + 1)
                dve.tensor_reduce(mxs[:, s // 2, i, (s % 2) * 8 + q:(s % 2) * 8 + q + 1], two[:, i, :],
                                  AX_X, ALU.max).then_inc(max_done, 1)

            def split_c(n, half, step):
                if step == 0:
                    dve.wait_ge(max_done, FAR + 64 * n + 32 * (half + 1))
                    op = dve.tensor_tensor(nm[:, :], mxs[:, half, 0, :], mxs[:, half, 1, :], ALU.max)
                else:
                    dve.wait_ge(c_step, START + 5 * (2 * n + half) + step)
                if step == 1:
                    op = dve.tensor_scalar(cparts[:, half, 0, :], nm[:, :], NEG, None, ALU.mult)
                elif step == 2:
                    op = dve.scalar_tensor_tensor(out=cres[:, :], in0=nm[:, :], scalar=NEG,
                                                  in1=cparts[:, half, 0, :], op0=ALU.mult, op1=ALU.subtract)
                elif step == 3:
                    op = dve.tensor_copy(cparts[:, half, 1, :], cres[:, :])
                elif step == 4:
                    op = dve.tensor_tensor(cparts[:, half, 2, :], cres[:, :], cparts[:, half, 1, :], ALU.subtract)
                op.then_inc(c_step, 1)

            def take_c(n, half):
                dve.wait_ge(tr_ready, START + 2 * n + half + 1)
                dve.wait_ge(c_stored[half], START + 48 * n)
                dve.tensor_copy(cT[:, half, :], misc[0:48, BANK - P // 2:BANK].bitcast(BF16)).then_inc(ct_ready, 1)

            def take_den(w, step):
                if step == 0:
                    dve.wait_ge(den_ready, START + w + 1)
                    dve.reciprocal(rden[:, :], misc[:, 0:8]).then_inc(rec_done, 1)
                else:
                    dve.wait_ge(rec_done, START + 2 * w + 1)
                    dve.tensor_copy(rrep[:, :, :],
                                    rden[:, :].unsqueeze(2).to_broadcast([P, 8, 32])).then_inc(rec_done, 1)

            def normalise(n, s):
                dve.wait_ge(bc_ready, START + 4 * n + s + 1)
                dve.wait_ge(on_stored[s % 2], START + 64 * (2 * n + s // 2))
                dve.tensor_tensor(On[:, s % 2, :, 1:IMG + 1],
                                  misc[:, P:3 * P].rearrange("p (y x) -> p y x", x=IMG),
                                  Osb[:, s % 2, :].rearrange("p (y x) -> p y x", x=IMG), ALU.mult).then_inc(on_done, 1)

            def add_fold(p):
                dve.wait_ge(fold_ready, START + p + 1)
                dve.wait_ge(cov_done, START + p + 1)
                dve.wait_ge(post_stored, START + 64 * p)
                dve.tensor_tensor(tnew[:, :, 1:IMG + 1], aux[0][:, 0:4 * IMG].rearrange("p (y x) -> p y x", x=IMG),
                                  tc_[:, :, :], ALU.add).then_inc(new_ready, 1)

            def project_alone(g, first=None):
                if first == 1:
                    for k in range(5):
                        split_c(0, 0, k)
                for t in range(4):
                    if first is not None:
                        first_maxima(16 * first + 3 * t, 3)
                    if t == 1:
                        scale(g, 0)
                        if first == 1:
                            take_c(0, 0)
                    if t:
                        scale(g, t)
                        residue(g, t - 1)
                        low_parts(dve, g, t - 1)
                if first is not None:
                    first_maxima(16 * first + 12, 4)
                if first != 1:
                    for k in range(14):
                        inverse_std(g + 1, k, pro_stat)

            def first_maxima(k, tiles):
                for tile in range(k, k + tiles):
                    for half in range(2):
                        row_max(0, tile // KT, tile % KT, half)

            for k in range(14):
                inverse_std(0, k, pro_stat)
            with dve.Fori(0, LEAD // 2 - 1) as r:
                for par in range(2):
                    project_alone(2 * r + par)
            project_alone(LEAD - 2, first=0)
            project_alone(LEAD - 1, first=1)

            def step(n, r, par, pre, post, first=False, nxt=True, ahead=True):
                g, p = n + LEAD, r - LEAD // 2
                for s in range(SPLIT):
                    for i in range(KT):
                        q = KT * s + i
                        for half in range(2):
                            h = 2 * i + half
                            if nxt:
                                row_max(n + 1, s, i, half)
                            if h < 5 and s == 0:
                                split_c(n, 1, h)
                            if h < 5 and s == 2 and nxt:
                                split_c(n + 1, 0, h)
                            if h == 7 and s == 0:
                                take_c(n, 1)
                            if h == 7 and s == 2 and nxt:
                                take_c(n + 1, 0)
                            if h in (10, 11) and (s or not first):
                                take_den(4 * n + s - 1, h - 10)
                            if h == 15 and (s or not first):
                                normalise(n - (0 if s else 1), (s - 1) % SPLIT)
                            if pre and 5 <= q < 12:
                                inverse_std(g, 2 * (q - 5) + half, aux[1])
                            if pre and half and q in (13, 17, 21, 25):
                                scale(g, (q - 13) // 4)
                            if pre and half and q in (15, 19, 23):
                                residue(g, (q - 15) // 4)
                            if post and par == 0 and half and q == 6:
                                add_fold(p)

            steps(dve, step)
            take_den(4 * UN - 1, 0)
            take_den(4 * UN - 1, 1)
            normalise(UN - 1, SPLIT - 1)
            dve.nop(nofuse=True)
            with dve.Fori((UN - LEAD) // 2, UN // 2) as p:
                add_fold(p)

            def front(b, part):
                if part == 0:
                    dve.wait_ge(pool_front, START + 6 * b + 5)
                    dve.tensor_reduce(col[:, 0:1], imgB[:, :], AX_X, ALU.add).then_inc(dve_front, 1)
                    dve.wait_ge(mean_done, START + 2 * b + 1)
                    dve.tensor_scalar(col[:, 6:7], two[:, 1, 0:1], NEG, None, ALU.mult).then_inc(dve_front, 1)
                else:
                    dve.wait_ge(pool_front, START + 6 * b + 6)
                    dve.tensor_reduce(col[:, 1:2], ybuf, AX_X, ALU.add).then_inc(dve_front, 1)
                    dve.wait_ge(mean_done, START + 2 * b + 2)
                    dve.tensor_scalar(col[:, 2:3], two[:, 1, 1:2], GN_EPS, None, ALU.add).then_inc(dve_front, 1)
                    dve.wait_ge(act_front, START + 6 * b + 5)
                    dve.reciprocal(col[:, 5:6], col[:, 3:4]).then_inc(dve_front, 1)

            def chunks(b, lo, hi):
                with dve.Fori(lo, hi) as c:
                    g = b * CHUNKS + c
                    dve.wait_ge(h_act, START + g + 1)
                    for m in range(8):
                        dve.wait_ge(g_ready, START + 8 * g + m + 1)
                        dve.tensor_tensor(qy(m), gbank[m % 2], hrep, ALU.mult).then_inc(y_done, 1)
                    dve.wait_ge(z_ready, START + g + 1)
                    dve.tensor_copy(zsb[:, :], wsum[:, :]).then_inc(z_sb, 1)
                    dve.wait_ge(f_ready, START + g + 1)
                    dve.wait_ge(x1_in, START + 16 * (g + 1))
                    dve.scalar_tensor_tensor(out=out_t, in0=misc[0:32, :], scalar=bias_s[:, 0:1], in1=x1_in_t,
                                             op0=ALU.add, op1=ALU.add).then_inc(o_done, 1)

            dve.memset(Vflat[0:TQ, 0:2 * PAD * IMG], 0.0).then_inc(u_clear, 1)
            front(0, 0)
            front(0, 1)
            dve.nop(nofuse=True)
            with dve.Fori(0, B - 1) as b:
                chunks(b, 0, 4)
                front(b + 1, 0)
                chunks(b, 4, 6)
                front(b + 1, 1)
                chunks(b, 6, CHUNKS)
            chunks(B - 1, 0, CHUNKS)

        @block.gpsimd
        def _(pool):
            def sums(g, par, half):
                ch = Chain(pool, sum_step, START + 5 * g)
                pool.wait_ge(t3_in[par], START + 48 * (half + 1))
                pool.wait_ge(stat_ready, START + g)
                img = T3c[:, par, :, :]
                ch.link(pool.tensor_tensor(SQc[:, :, :], img, img, ALU.mult))
                for i, t in enumerate((img, SQc[:, :, :])):
                    ch.link(pool.tensor_tensor(vtmp[:, i, :, :], t[:, 0:ROWS, :], t[:, 1:ROWS + 1, :], ALU.add))
                    ch.link(pool.tensor_tensor(vsum[:, i, :, :], vtmp[:, i, :, :], t[:, 2:ROWS + 2, :], ALU.add))

            def values(n, s):
                pool.wait_ge(pv_done, START + 32 * n + 8 * s - 8)
                pool.wait_ge(vt_used, START + 2 * CHUNKS * (n // HEADS) + 4 * s + 4)
                pool.nop(nofuse=True)
                tile = ((n // HEADS * CHUNKS + 2 * s) % VRING) * 4
                pool.tensor_copy(Vh[:, s % 2, :, 0:DH],
                                 Vall[:, bass.ds(tile, KT), bass.ds((n % HEADS) * DH, DH)]).then_inc(vh_ready, 1)

            def covered(p):
                pool.wait_ge(post_in, START + 80 * (p + 1))
                pool.wait_ge(new_ready, START + p)
                pool.nop(nofuse=True)
                pool.tensor_tensor(tc_[:, :, :], tq[:, :, 1:IMG + 1],
                                   cover[:, bass.ds((p % PAIRS) * 4 * IMG, 4 * IMG)]
                                   .rearrange("p (y x) -> p y x", x=IMG), ALU.mult).then_inc(cov_done, 1)

            pool.wait_ge(setup_dve, SETUP)
            pool.wait_ge(consts_in, 16 * CONST_DMAS)
            sums(0, 0, 0)
            with pool.Fori(0, LEAD // 2) as r:
                for par in range(2):
                    g = 2 * r + par
                    sums(g + 1, 1 - par, r + par)
            values(0, 0)

            def step(n, r, par, pre, post, first=False, nxt=True, ahead=True):
                g, p = n + LEAD, r - LEAD // 2
                if post and par == 0:
                    covered(p)
                values(n, 1)
                values(n, 2)
                if pre:
                    low_parts(pool, g, 0)
                values(n, 3)
                if pre:
                    low_parts(pool, g, 1)
                if nxt:
                    values(n + 1, 0)
                if pre:
                    low_parts(pool, g, 2)
                    sums(g + 1, 1 - par, r + LEAD // 2 + par)

            steps(pool, step)
            def elu_sum(b):
                ch = Chain(pool, pool_front, START + 6 * b)
                pool.wait_ge(act_front, START + 6 * b + 2)
                pool.nop(nofuse=True)
                ch.link(pool.tensor_scalar(imgC[:, :], ybuf, 0.0, None, ALU.min))
                pool.nop(nofuse=True)
                ch.link(pool.tensor_scalar(ybuf, ybuf, 0.0, -1.0, ALU.max, ALU.add))
                pool.wait_ge(res_in, START + 192 * (b + 1))
                ch.link(pool.tensor_tensor(imgA[:, :], imgA[:, :], imgB[:, :], ALU.add))
                pool.wait_ge(act_front, START + 6 * b + 3)
                ch.link(pool.tensor_tensor(imgC[:, :], imgC[:, :], ybuf, ALU.add))
                ch.link(pool.tensor_tensor(imgB[:, :], imgA[:, :], imgC[:, :], ALU.add))

            def squares(b):
                pool.wait_ge(act_front, START + 6 * b + 4)
                pool.tensor_tensor(ybuf, imgC[:, :], imgC[:, :], ALU.mult).then_inc(pool_front, 1)

            elu_sum(0)
            with pool.Fori((UN - LEAD) // 2, UN // 2) as p:
                covered(p)
            squares(0)
            with pool.Fori(0, B - 1) as b:
                elu_sum(b + 1)
                squares(b + 1)


def host_layouts(a):
    f = {n: np.ascontiguousarray(np.asarray(v)) for n, v in a.items()}

    def taps_last(w):
        return np.moveaxis(w, -3, -1)

    order = np.concatenate([np.arange(0, 2 * MT), np.arange(2 * E, 2 * E + VA),
                            np.arange(2 * MT, 2 * E), np.arange(2 * E + VA, 3 * E)])
    heads = np.arange(E).reshape(HEADS // 2, 2, DH).transpose(1, 0, 2).reshape(2, EK)
    L = {}
    B = f["x"].shape[0]
    L["x"] = f["x"].reshape(B, C, N)
    L["ln_g"] = taps_last(f["L0_conv_ln_g"].reshape(C, 3, 3)).reshape(1, DD)
    L["ln_b"] = taps_last(f["L0_conv_ln_b"].reshape(C, 3, 3)).reshape(1, DD)
    two_rows = lambda w: w.reshape(2, EK, -1).transpose(1, 0, 2)
    wr, br, wqkv, we = [], [], [], []
    for i in (1, 2, 3):
        wr.append(two_rows(taps_last(f[f"L0_conv_wr{i}"].reshape(E, C, 3, 3)).reshape(E, DD)))
        br.append(f[f"L0_conv_br{i}"].reshape(2, EK).T)
        wqkv.append(two_rows(f[f"L0_conv_wqkv{i}"][order].T))
        w = f[f"L0_conv_we{i}"].reshape(C, 3, 3, E).transpose(3, 1, 2, 0).reshape(E, 9 * C)
        last = np.stack([f[f"L0_conv_be{i}"].reshape(C, 3, 3).transpose(1, 2, 0).reshape(9 * C),
                         np.zeros(9 * C, np.float32)])
        we.append(np.concatenate([w[heads], last[:, None]], axis=1).transpose(1, 0, 2).reshape(EK + 1, 2 * 9 * C))
    L["wr"], L["br"], L["wqkv"], L["we"] = (np.stack(v) for v in (wr, br, wqkv, we))
    L["conv_w"] = f["L0_conv_conv_w"].transpose(3, 1, 2, 0).reshape(TQ, 3 * 32)
    L["conv_b"] = np.tile(f["L0_conv_conv_b"], 4).reshape(P, 1)
    w1 = f["L1_conv_W1"].reshape(32, C, 3, 3).transpose(3, 1, 2, 0)
    L["w1"] = np.tile(w1, (1, 1, 1, 4)).reshape(TQ, 3 * P)
    L["b1"] = np.tile(f["L1_conv_b1"], 4).reshape(P, 1)
    L["w2"] = f["L1_conv_W2"].reshape(32, C, 3, 3, 32).transpose(3, 1, 2, 0, 4).reshape(TQ, 3 * 1024)
    L["b2"] = f["L1_conv_b2"].reshape(32, C, 3, 3).transpose(3, 1, 2, 0).reshape(TQ, 3 * 32)
    L["bias"] = f["L1_conv_bias"].reshape(32, 1)
    return {n: np.ascontiguousarray(v) for n, v in L.items()}


def kernel(**inputs):
    import concourse.bacc as bacc
    from concourse.bass_utils import run_bass_kernel_spmd

    nc = bacc.Bacc("TRN2", target_bir_lowering=False, num_devices=1)
    data, tables = host_layouts(inputs), constants()
    B = data["x"].shape[0]

    def arg(name, a):
        return nc.dram_tensor(name, a.shape, F32, kind="ExternalInput").ap()

    args = {n: arg(f"in_{n}", a) for n, a in data.items()}
    k = {n: arg(f"const_{n}", a) for n, a in tables.items()}
    out = nc.dram_tensor("out_0", (B, C, N), F32, kind="ExternalOutput").ap()
    preact_block(nc, 3, B, k=k, out=out, **args)
    arrays = {f"in_{n}": a for n, a in data.items()} | {f"const_{n}": a for n, a in tables.items()}
    r = run_bass_kernel_spmd(nc, [arrays], core_ids=[0])
    return r.results[0]["out_0"].reshape(B, C, IMG, IMG)
```
